# Optimizing a Trainium2 kernel written in Bass

```python
import numpy as np
import jax
import jax.numpy as jnp

def _softmax(x, axis=-1):
    return jax.nn.softmax(x, axis=axis)

def _gelu(x):
    return jax.nn.gelu(x, approximate=True)

def _silu(x):
    return jax.nn.silu(x)

def _sigmoid(x):
    return jax.nn.sigmoid(x)

def _layernorm(x, axis=-1, eps=1e-05):
    m = jnp.mean(x, axis=axis, keepdims=True)
    v = jnp.var(x, axis=axis, keepdims=True)
    return (x - m) / jnp.sqrt(v + eps)

def _scatter_add(tgt, idx, src, axis=0):
    return tgt.at[idx].add(src)

def _segment_sum(src, seg, n):
    return jax.ops.segment_sum(src, seg, n)
kernel_name = 'mk_xattn_seq_d4_seqx_r4_f4334e'

def setup_inputs(seed: int=0):
    np.random.seed(seed)
    _w = jnp.asarray

    def _rec_inputs():
        import jax
        import jax.numpy as jnp
        _rk = jax.random.key(seed)
        x = -0.000929 + 1 * jax.random.normal(jax.random.fold_in(_rk, 1), (4, 512, 256), jnp.float32)
        _lenS = 512 - jax.random.randint(jax.random.fold_in(_rk, 7), (4,), 0, max(1, 512 // 4) + 1, jnp.int32)
        _lenS2 = 512 - jax.random.randint(jax.random.fold_in(_rk, 8), (4,), 0, max(1, 512 // 4) + 1, jnp.int32)
        _ctx_1024P = jax.random.normal(jax.random.fold_in(_rk, 11), (4, 16, 256), jnp.float32)
        _ctx_1024c = jax.random.dirichlet(jax.random.fold_in(_rk, 511), 0.3 * jnp.ones((16,), jnp.float32), (4, 512))
        _ctx_1024t = jnp.einsum('bsk,bkd->bsd', _ctx_1024c, _ctx_1024P)
        _ctx_1024t = _ctx_1024t * jax.lax.rsqrt(jnp.mean(jnp.square(_ctx_1024t)) + 1e-12) * 0.953939
        ctx_1024 = -0.000514642 + 1.00011 * (_ctx_1024t + 0.3 * jax.random.normal(jax.random.fold_in(_rk, 611), (4, 512, 256), jnp.float32))
        itok_BxS2_4_31999 = jax.random.randint(jax.random.fold_in(_rk, 13), (4, 512), 4, 8000, jnp.int32)
        _ctxb_2048x64P = jax.random.normal(jax.random.fold_in(_rk, 14), (4, 16, 64), jnp.float32)
        _ctxb_2048x64c = jax.random.dirichlet(jax.random.fold_in(_rk, 514), 0.3 * jnp.ones((16,), jnp.float32), (4, 512))
        _ctxb_2048x64t = jnp.einsum('bsk,bkd->bsd', _ctxb_2048x64c, _ctxb_2048x64P)
        _ctxb_2048x64t = _ctxb_2048x64t * jax.lax.rsqrt(jnp.mean(jnp.square(_ctxb_2048x64t)) + 1e-12) * 0.953939
        ctxb_2048x64 = 0.50053 + 0.288505 * (_ctxb_2048x64t + 0.3 * jax.random.normal(jax.random.fold_in(_rk, 614), (4, 512, 64), jnp.float32))
        _validS = jnp.arange(512)[None, :] < _lenS[:, None]
        _validS2 = jnp.arange(512)[None, :] < _lenS2[:, None]
        _causal = jnp.tril(jnp.ones((512, 512), dtype=bool))
        mask_1xS2_bf0 = jnp.logical_not(jnp.ones((1, 512), dtype=bool))
        return (x, ctx_1024, itok_BxS2_4_31999, ctxb_2048x64, mask_1xS2_bf0)
    x, ctx_1024, itok_BxS2_4_31999, ctxb_2048x64, mask_1xS2_bf0 = _rec_inputs()

    def _L0_xattn_setup():
        import jax, jax.numpy as jnp
        import numpy as np
        D = 256
        D_STATE = 128
        N_HEADS = 8
        D_INNER = 2 * D
        HEADDIM = 64
        H_M = D_INNER // HEADDIM
        D_CONV = 4
        CONV_DIM = D_INNER + 2 * D_STATE
        D_IN_PROJ = 2 * D_INNER + 2 * D_STATE + H_M
        B = 1
        LQ = 256
        LK = 512
        EPS = 1e-05

        def _rms(x, w):
            return x * jax.lax.rsqrt(jnp.mean(x * x, axis=-1, keepdims=True) + EPS) * w

        def _ln(x, w, b):
            mu = jnp.mean(x, axis=-1, keepdims=True)
            v = jnp.mean((x - mu) ** 2, axis=-1, keepdims=True)
            return (x - mu) * jax.lax.rsqrt(v + EPS) * w + b

        def _mamba2_block(x, norm_w, in_proj_w, conv_w, conv_b, dt_bias, A_log, D_skip, gnorm_w, out_proj_w):
            b, L, _ = x.shape
            resid = x
            zxbcdt = _rms(x, norm_w) @ in_proj_w
            z = zxbcdt[..., :D_INNER]
            xBC = zxbcdt[..., D_INNER:D_INNER + CONV_DIM]
            dt = jax.nn.softplus(zxbcdt[..., -H_M:] + dt_bias)
            padded = jnp.pad(xBC, ((0, 0), (D_CONV - 1, 0), (0, 0)))
            conv = conv_b + sum((padded[:, k:k + L, :] * conv_w[:, k] for k in range(D_CONV)))
            xBC = jax.nn.silu(conv)
            xh = xBC[..., :D_INNER].reshape(b, L, H_M, HEADDIM)
            Bm = xBC[..., D_INNER:D_INNER + D_STATE]
            Cm = xBC[..., D_INNER + D_STATE:]
            A = -jnp.exp(A_log)
            decay = jnp.exp(dt * A)
            dbx = dt[..., None] * xh

            def step(h, inp):
                dec, u, bt, ct = inp
                h = h * dec[:, :, None, None] + u[..., None] * bt[:, None, None, :]
                y = jnp.einsum('bhpn,bn->bhp', h, ct)
                return (h, y)
            h0 = jnp.zeros((b, H_M, HEADDIM, D_STATE), x.dtype)
            xs = (decay.transpose(1, 0, 2), dbx.transpose(1, 0, 2, 3), Bm.transpose(1, 0, 2), Cm.transpose(1, 0, 2))
            _, ys = jax.lax.scan(step, h0, xs)
            y = ys.transpose(1, 0, 2, 3) + D_skip[None, None, :, None] * xh
            u = _rms(y.reshape(b, L, D_INNER) * jax.nn.silu(z), gnorm_w)
            return resid + u @ out_proj_w

        def _cross_attention(x, enc, pad_mask, ln_w, ln_b, Wq, Wk, Wv, Wo):
            b, Lq, _ = x.shape
            Lk = enc.shape[1]
            dh = D // N_HEADS
            resid = x
            xn = _ln(x, ln_w, ln_b)
            q = (xn @ Wq).reshape(b, Lq, N_HEADS, dh)
            k = (enc @ Wk).reshape(b, Lk, N_HEADS, dh)
            v = (enc @ Wv).reshape(b, Lk, N_HEADS, dh)
            scores = jnp.einsum('bqhd,bkhd->bhqk', q, k) * np.float32(1.0 / np.sqrt(dh))
            scores = jnp.where(pad_mask[:, None, None, :], jnp.float32(-1000000000.0), scores)
            p = jax.nn.softmax(scores, axis=-1)
            ctx = jnp.einsum('bhqk,bkhd->bqhd', p, v).reshape(b, Lq, D)
            return resid + ctx @ Wo
        key = jax.random.key(seed)
        ks = jax.random.split(key, 10)
        s = 0.02
        return {'x': jax.random.normal(ks[0], (B, LQ, D), jnp.float32), 'encoder_out': jax.random.normal(ks[1], (B, LK, D), jnp.float32), 'encoder_padding_mask': jnp.zeros((B, LK), dtype=bool), 'm_norm_w': jnp.ones((D,), jnp.float32), 'in_proj_w': s * jax.random.normal(ks[2], (D, D_IN_PROJ), jnp.float32), 'conv_w': s * jax.random.normal(ks[3], (CONV_DIM, D_CONV), jnp.float32), 'conv_b': jnp.zeros((CONV_DIM,), jnp.float32), 'dt_bias': jnp.full((H_M,), float(np.log(np.expm1(0.01))), jnp.float32), 'A_log': jnp.log(jnp.linspace(1.0, 16.0, H_M)).astype(jnp.float32), 'D_skip': jnp.ones((H_M,), jnp.float32), 'gnorm_w': jnp.ones((D_INNER,), jnp.float32), 'out_proj_w': s * jax.random.normal(ks[4], (D_INNER, D), jnp.float32), 'ca_ln_w': jnp.ones((D,), jnp.float32), 'ca_ln_b': jnp.zeros((D,), jnp.float32), 'Wq': s * jax.random.normal(ks[5], (D, D), jnp.float32), 'Wk': s * jax.random.normal(ks[6], (D, D), jnp.float32), 'Wv': s * jax.random.normal(ks[7], (D, D), jnp.float32), 'Wo': s * jax.random.normal(ks[8], (D, D), jnp.float32)}
    _L0_xattn_all = _L0_xattn_setup()
    _L0_xattn_in = {k: v for k, v in _L0_xattn_all.items() if k in ('m_norm_w', 'in_proj_w', 'conv_w', 'conv_b', 'dt_bias', 'A_log', 'D_skip', 'gnorm_w', 'out_proj_w', 'ca_ln_w', 'ca_ln_b', 'Wq', 'Wk', 'Wv', 'Wo')}
    del _L0_xattn_all

    def _L1_xattn_setup():
        import jax, jax.numpy as jnp
        import numpy as np
        B, L, D = (32, 128, 256)
        H, DK, DV = (8, 16, 16)

        def _xavier(key, shape):
            fan_in, fan_out = (shape[0], shape[1])
            std = (2.0 / (fan_in + fan_out)) ** 0.5
            return std * jax.random.normal(key, shape, dtype=jnp.float32)
        key = jax.random.key(seed)
        ks = jax.random.split(key, 11)
        return {'Q': jax.random.normal(ks[0], (B, L, D), jnp.float32), 'K': jax.random.normal(ks[1], (B, L, D), jnp.float32), 'V': jax.random.normal(ks[2], (B, L, D), jnp.float32), 'W_q': _xavier(ks[3], (D, H * DK)), 'W_k': _xavier(ks[4], (D, H * DK)), 'W_v': _xavier(ks[5], (D, H * DV)), 'W_o': _xavier(ks[6], (H * DV, D)), 'w1': _xavier(ks[7], (D, D)), 'b1': jnp.zeros((D,), jnp.float32), 'w2': _xavier(ks[8], (D, D)), 'b2': jnp.zeros((D,), jnp.float32)}
    _L1_xattn_all = _L1_xattn_setup()
    _L1_xattn_in = {k: v for k, v in _L1_xattn_all.items() if k in ('W_q', 'W_k', 'W_v', 'W_o', 'w1', 'b1', 'w2', 'b2')}
    del _L1_xattn_all

    def _L2_xattn_setup():
        import jax, jax.numpy as jnp
        import numpy as np
        D_Q = 256
        D_KV = 256
        D_ATTN = 256
        NUM_HEADS = 16
        D_HEAD = D_ATTN // NUM_HEADS

        def layer_norm(x, gamma, beta, eps=1e-05):
            mu = jnp.mean(x, axis=-1, keepdims=True)
            var = jnp.var(x, axis=-1, keepdims=True)
            return (x - mu) * jax.lax.rsqrt(var + eps) * gamma + beta
        key = jax.random.key(seed)
        ks = jax.random.split(key, 10)
        B, N_q, N_kv = (4, 256, 1024)
        s_q = 1.0 / np.sqrt(D_Q)
        s_kv = 1.0 / np.sqrt(D_KV)
        s_a = 1.0 / np.sqrt(D_ATTN)
        return {'q': jax.random.normal(ks[0], (B, N_q, D_Q), jnp.float32), 'kv': jax.random.normal(ks[1], (B, N_kv, D_KV), jnp.float32), 'q_norm_g': jnp.ones((D_Q,), jnp.float32), 'q_norm_b': jnp.zeros((D_Q,), jnp.float32), 'kv_norm_g': jnp.ones((D_KV,), jnp.float32), 'kv_norm_b': jnp.zeros((D_KV,), jnp.float32), 'Wq': jax.random.normal(ks[2], (D_Q, D_ATTN), jnp.float32) * s_q, 'Wk': jax.random.normal(ks[3], (D_KV, D_ATTN), jnp.float32) * s_kv, 'Wv': jax.random.normal(ks[4], (D_KV, D_ATTN), jnp.float32) * s_kv, 'Wo': jax.random.normal(ks[5], (D_ATTN, D_Q), jnp.float32) * s_a, 'bo': jnp.zeros((D_Q,), jnp.float32)}
    _L2_xattn_all = _L2_xattn_setup()
    _L2_xattn_in = {k: v for k, v in _L2_xattn_all.items() if k in ('q_norm_g', 'q_norm_b', 'kv_norm_g', 'kv_norm_b', 'Wq', 'Wk', 'Wv', 'Wo', 'bo')}
    del _L2_xattn_all

    def _L3_xattn_setup():
        import jax, jax.numpy as jnp
        import numpy as np
        BATCH, T, H, S, P, NH = (4, 512, 256, 64, 64, 8)
        HD = H // NH

        def _layernorm(x, g, b):
            mu = jnp.mean(x, axis=-1, keepdims=True)
            var = jnp.mean((x - mu) ** 2, axis=-1, keepdims=True)
            return (x - mu) * jax.lax.rsqrt(var + 1e-05) * g + b

        def _mha(q_in, kv_in, W_qkv, b_qkv, W_o, b_o):
            Wq, Wk, Wv = jnp.split(W_qkv, 3, axis=0)
            bq, bk, bv = jnp.split(b_qkv, 3, axis=0)

            def heads(x, W, b):
                y = x @ W.T + b
                return y.reshape(y.shape[0], y.shape[1], NH, HD).transpose(0, 2, 1, 3)
            q, k, v = (heads(q_in, Wq, bq), heads(kv_in, Wk, bk), heads(kv_in, Wv, bv))
            scores = jnp.einsum('bhqd,bhkd->bhqk', q, k) * (1.0 / np.sqrt(HD))
            attn = jax.nn.softmax(scores, axis=-1)
            out = jnp.einsum('bhqk,bhkd->bhqd', attn, v)
            out = out.transpose(0, 2, 1, 3).reshape(q_in.shape)
            return out @ W_o.T + b_o
        key = jax.random.key(seed)
        ks = jax.random.split(key, 16)
        sH = 1.0 / np.sqrt(H)
        d = {}
        d['builder_state'] = jax.random.normal(ks[0], (BATCH, T, H), jnp.float32)
        d['base_state'] = jax.random.normal(ks[1], (BATCH, T, H), jnp.float32)
        d['input_ids'] = jax.random.randint(ks[2], (BATCH, T), 0, 8000)
        d['program_probs'] = jax.random.uniform(ks[3], (BATCH, T, P), jnp.float32)
        d['A'] = jax.random.normal(ks[4], (S, S), jnp.float32) * (0.5 / np.sqrt(S))
        d['Bmat'] = jax.random.normal(ks[5], (H, S), jnp.float32) * sH
        d['Cmat'] = jax.random.normal(ks[6], (S, H), jnp.float32) * (1.0 / np.sqrt(S))
        d['W_in'] = jax.random.normal(ks[7], (H, H), jnp.float32) * sH
        d['b_in'] = jnp.zeros((H,), jnp.float32)
        d['W_qkv'] = jax.random.normal(ks[8], (3 * H, H), jnp.float32) * sH
        d['b_qkv'] = jnp.zeros((3 * H,), jnp.float32)
        d['W_o'] = jax.random.normal(ks[9], (H, H), jnp.float32) * sH
        d['b_o'] = jnp.zeros((H,), jnp.float32)
        d['W_prog'] = jax.random.normal(ks[10], (H, P), jnp.float32) * (1.0 / np.sqrt(P))
        d['b_prog'] = jnp.zeros((H,), jnp.float32)
        d['g1'] = jnp.ones((H,), jnp.float32)
        d['beta1'] = jnp.zeros((H,), jnp.float32)
        d['g2'] = jnp.ones((H,), jnp.float32)
        d['beta2'] = jnp.zeros((H,), jnp.float32)
        return d
    _L3_xattn_all = _L3_xattn_setup()
    _L3_xattn_in = {k: v for k, v in _L3_xattn_all.items() if k in ('A', 'Bmat', 'Cmat', 'W_in', 'b_in', 'W_qkv', 'b_qkv', 'W_o', 'b_o', 'W_prog', 'b_prog', 'g1', 'beta1', 'g2', 'beta2')}
    del _L3_xattn_all
    return {'x': x, 'ctx_1024': ctx_1024, 'itok_BxS2_4_31999': itok_BxS2_4_31999, 'ctxb_2048x64': ctxb_2048x64, 'mask_1xS2_bf0': mask_1xS2_bf0, 'L0_xattn_m_norm_w': _L0_xattn_in['m_norm_w'], 'L0_xattn_in_proj_w': _L0_xattn_in['in_proj_w'], 'L0_xattn_conv_w': _L0_xattn_in['conv_w'], 'L0_xattn_conv_b': _L0_xattn_in['conv_b'], 'L0_xattn_dt_bias': _L0_xattn_in['dt_bias'], 'L0_xattn_A_log': _L0_xattn_in['A_log'], 'L0_xattn_D_skip': _L0_xattn_in['D_skip'], 'L0_xattn_gnorm_w': _L0_xattn_in['gnorm_w'], 'L0_xattn_out_proj_w': _L0_xattn_in['out_proj_w'], 'L0_xattn_ca_ln_w': _L0_xattn_in['ca_ln_w'], 'L0_xattn_ca_ln_b': _L0_xattn_in['ca_ln_b'], 'L0_xattn_Wq': _L0_xattn_in['Wq'], 'L0_xattn_Wk': _L0_xattn_in['Wk'], 'L0_xattn_Wv': _L0_xattn_in['Wv'], 'L0_xattn_Wo': _L0_xattn_in['Wo'], 'L1_xattn_W_q': _L1_xattn_in['W_q'], 'L1_xattn_W_k': _L1_xattn_in['W_k'], 'L1_xattn_W_v': _L1_xattn_in['W_v'], 'L1_xattn_W_o': _L1_xattn_in['W_o'], 'L1_xattn_w1': _L1_xattn_in['w1'], 'L1_xattn_b1': _L1_xattn_in['b1'], 'L1_xattn_w2': _L1_xattn_in['w2'], 'L1_xattn_b2': _L1_xattn_in['b2'], 'L2_xattn_q_norm_g': _L2_xattn_in['q_norm_g'], 'L2_xattn_q_norm_b': _L2_xattn_in['q_norm_b'], 'L2_xattn_kv_norm_g': _L2_xattn_in['kv_norm_g'], 'L2_xattn_kv_norm_b': _L2_xattn_in['kv_norm_b'], 'L2_xattn_Wq': _L2_xattn_in['Wq'], 'L2_xattn_Wk': _L2_xattn_in['Wk'], 'L2_xattn_Wv': _L2_xattn_in['Wv'], 'L2_xattn_Wo': _L2_xattn_in['Wo'], 'L2_xattn_bo': _L2_xattn_in['bo'], 'L3_xattn_A': _L3_xattn_in['A'], 'L3_xattn_Bmat': _L3_xattn_in['Bmat'], 'L3_xattn_Cmat': _L3_xattn_in['Cmat'], 'L3_xattn_W_in': _L3_xattn_in['W_in'], 'L3_xattn_b_in': _L3_xattn_in['b_in'], 'L3_xattn_W_qkv': _L3_xattn_in['W_qkv'], 'L3_xattn_b_qkv': _L3_xattn_in['b_qkv'], 'L3_xattn_W_o': _L3_xattn_in['W_o'], 'L3_xattn_b_o': _L3_xattn_in['b_o'], 'L3_xattn_W_prog': _L3_xattn_in['W_prog'], 'L3_xattn_b_prog': _L3_xattn_in['b_prog'], 'L3_xattn_g1': _L3_xattn_in['g1'], 'L3_xattn_beta1': _L3_xattn_in['beta1'], 'L3_xattn_g2': _L3_xattn_in['g2'], 'L3_xattn_beta2': _L3_xattn_in['beta2']}

def reference(x, ctx_1024, itok_BxS2_4_31999, ctxb_2048x64, mask_1xS2_bf0, L0_xattn_m_norm_w, L0_xattn_in_proj_w, L0_xattn_conv_w, L0_xattn_conv_b, L0_xattn_dt_bias, L0_xattn_A_log, L0_xattn_D_skip, L0_xattn_gnorm_w, L0_xattn_out_proj_w, L0_xattn_ca_ln_w, L0_xattn_ca_ln_b, L0_xattn_Wq, L0_xattn_Wk, L0_xattn_Wv, L0_xattn_Wo, L1_xattn_W_q, L1_xattn_W_k, L1_xattn_W_v, L1_xattn_W_o, L1_xattn_w1, L1_xattn_b1, L1_xattn_w2, L1_xattn_b2, L2_xattn_q_norm_g, L2_xattn_q_norm_b, L2_xattn_kv_norm_g, L2_xattn_kv_norm_b, L2_xattn_Wq, L2_xattn_Wk, L2_xattn_Wv, L2_xattn_Wo, L2_xattn_bo, L3_xattn_A, L3_xattn_Bmat, L3_xattn_Cmat, L3_xattn_W_in, L3_xattn_b_in, L3_xattn_W_qkv, L3_xattn_b_qkv, L3_xattn_W_o, L3_xattn_b_o, L3_xattn_W_prog, L3_xattn_b_prog, L3_xattn_g1, L3_xattn_beta1, L3_xattn_g2, L3_xattn_beta2):
    import jax
    import jax.numpy as jnp

    def _L0_xattn_ref(x, encoder_out, encoder_padding_mask, m_norm_w, in_proj_w, conv_w, conv_b, dt_bias, A_log, D_skip, gnorm_w, out_proj_w, ca_ln_w, ca_ln_b, Wq, Wk, Wv, Wo):
        import jax, jax.numpy as jnp
        import numpy as np
        D = 256
        D_STATE = 128
        N_HEADS = 8
        D_INNER = 2 * D
        HEADDIM = 64
        H_M = D_INNER // HEADDIM
        D_CONV = 4
        CONV_DIM = D_INNER + 2 * D_STATE
        D_IN_PROJ = 2 * D_INNER + 2 * D_STATE + H_M
        B = 1
        LQ = 256
        LK = 512
        EPS = 1e-05

        def _rms(x, w):
            return x * jax.lax.rsqrt(jnp.mean(x * x, axis=-1, keepdims=True) + EPS) * w

        def _ln(x, w, b):
            mu = jnp.mean(x, axis=-1, keepdims=True)
            v = jnp.mean((x - mu) ** 2, axis=-1, keepdims=True)
            return (x - mu) * jax.lax.rsqrt(v + EPS) * w + b

        def _mamba2_block(x, norm_w, in_proj_w, conv_w, conv_b, dt_bias, A_log, D_skip, gnorm_w, out_proj_w):
            b, L, _ = x.shape
            resid = x
            zxbcdt = _rms(x, norm_w) @ in_proj_w
            z = zxbcdt[..., :D_INNER]
            xBC = zxbcdt[..., D_INNER:D_INNER + CONV_DIM]
            dt = jax.nn.softplus(zxbcdt[..., -H_M:] + dt_bias)
            padded = jnp.pad(xBC, ((0, 0), (D_CONV - 1, 0), (0, 0)))
            conv = conv_b + sum((padded[:, k:k + L, :] * conv_w[:, k] for k in range(D_CONV)))
            xBC = jax.nn.silu(conv)
            xh = xBC[..., :D_INNER].reshape(b, L, H_M, HEADDIM)
            Bm = xBC[..., D_INNER:D_INNER + D_STATE]
            Cm = xBC[..., D_INNER + D_STATE:]
            A = -jnp.exp(A_log)
            decay = jnp.exp(dt * A)
            dbx = dt[..., None] * xh

            def step(h, inp):
                dec, u, bt, ct = inp
                h = h * dec[:, :, None, None] + u[..., None] * bt[:, None, None, :]
                y = jnp.einsum('bhpn,bn->bhp', h, ct)
                return (h, y)
            h0 = jnp.zeros((b, H_M, HEADDIM, D_STATE), x.dtype)
            xs = (decay.transpose(1, 0, 2), dbx.transpose(1, 0, 2, 3), Bm.transpose(1, 0, 2), Cm.transpose(1, 0, 2))
            _, ys = jax.lax.scan(step, h0, xs)
            y = ys.transpose(1, 0, 2, 3) + D_skip[None, None, :, None] * xh
            u = _rms(y.reshape(b, L, D_INNER) * jax.nn.silu(z), gnorm_w)
            return resid + u @ out_proj_w

        def _cross_attention(x, enc, pad_mask, ln_w, ln_b, Wq, Wk, Wv, Wo):
            b, Lq, _ = x.shape
            Lk = enc.shape[1]
            dh = D // N_HEADS
            resid = x
            xn = _ln(x, ln_w, ln_b)
            q = (xn @ Wq).reshape(b, Lq, N_HEADS, dh)
            k = (enc @ Wk).reshape(b, Lk, N_HEADS, dh)
            v = (enc @ Wv).reshape(b, Lk, N_HEADS, dh)
            scores = jnp.einsum('bqhd,bkhd->bhqk', q, k) * np.float32(1.0 / np.sqrt(dh))
            scores = jnp.where(pad_mask[:, None, None, :], jnp.float32(-1000000000.0), scores)
            p = jax.nn.softmax(scores, axis=-1)
            ctx = jnp.einsum('bhqk,bkhd->bqhd', p, v).reshape(b, Lq, D)
            return resid + ctx @ Wo
        h = _mamba2_block(x, m_norm_w, in_proj_w, conv_w, conv_b, dt_bias, A_log, D_skip, gnorm_w, out_proj_w)
        return _cross_attention(h, encoder_out, encoder_padding_mask, ca_ln_w, ca_ln_b, Wq, Wk, Wv, Wo)

    def _L1_xattn_ref(Q, K, V, W_q, W_k, W_v, W_o, w1, b1, w2, b2):
        import jax, jax.numpy as jnp
        import numpy as np
        B, L, D = (32, 128, 256)
        H, DK, DV = (8, 16, 16)

        def _xavier(key, shape):
            fan_in, fan_out = (shape[0], shape[1])
            std = (2.0 / (fan_in + fan_out)) ** 0.5
            return std * jax.random.normal(key, shape, dtype=jnp.float32)
        b, lq, _ = Q.shape
        lk = K.shape[1]
        Qh = (Q @ W_q).reshape(b, lq, H, DK)
        Kh = (K @ W_k).reshape(b, lk, H, DK)
        Vh = (V @ W_v).reshape(b, lk, H, DV)
        scale = 1.0 / jnp.sqrt(jnp.float32(DK))
        scores = jnp.einsum('bqhd,bkhd->bhqk', Qh, Kh) * scale
        attn = jax.nn.softmax(scores, axis=-1)
        ctx = jnp.einsum('bhqk,bkhd->bqhd', attn, Vh).reshape(b, lq, H * DV)
        attn_out = ctx @ W_o
        X = Q + attn_out
        h = jax.nn.relu(X @ w1.T + b1)
        ffn_out = h @ w2.T + b2
        return ffn_out + X

    def _L2_xattn_ref(q, kv, q_norm_g, q_norm_b, kv_norm_g, kv_norm_b, Wq, Wk, Wv, Wo, bo):
        import jax, jax.numpy as jnp
        import numpy as np
        D_Q = 256
        D_KV = 256
        D_ATTN = 256
        NUM_HEADS = 16
        D_HEAD = D_ATTN // NUM_HEADS

        def layer_norm(x, gamma, beta, eps=1e-05):
            mu = jnp.mean(x, axis=-1, keepdims=True)
            var = jnp.var(x, axis=-1, keepdims=True)
            return (x - mu) * jax.lax.rsqrt(var + eps) * gamma + beta
        B, N_q, _ = q.shape
        N_kv = kv.shape[1]
        qn = layer_norm(q, q_norm_g, q_norm_b)
        kvn = layer_norm(kv, kv_norm_g, kv_norm_b)
        Q = (qn @ Wq).reshape(B, N_q, NUM_HEADS, D_HEAD).transpose(0, 2, 1, 3)
        K = (kvn @ Wk).reshape(B, N_kv, NUM_HEADS, D_HEAD).transpose(0, 2, 1, 3)
        V = (kvn @ Wv).reshape(B, N_kv, NUM_HEADS, D_HEAD).transpose(0, 2, 1, 3)
        scores = jnp.einsum('bhqd,bhkd->bhqk', Q, K) / jnp.sqrt(jnp.float32(D_HEAD))
        attn = jax.nn.softmax(scores, axis=-1)
        ctx = jnp.einsum('bhqk,bhkd->bhqd', attn, V)
        ctx = ctx.transpose(0, 2, 1, 3).reshape(B, N_q, D_ATTN)
        out = q + jax.nn.gelu(ctx @ Wo + bo, approximate=False)
        return out

    def _L3_xattn_ref(builder_state, base_state, input_ids, program_probs, A, Bmat, Cmat, W_in, b_in, W_qkv, b_qkv, W_o, b_o, W_prog, b_prog, g1, beta1, g2, beta2):
        import jax, jax.numpy as jnp
        import numpy as np
        BATCH, T, H, S, P, NH = (4, 512, 256, 64, 64, 8)
        HD = H // NH

        def _layernorm(x, g, b):
            mu = jnp.mean(x, axis=-1, keepdims=True)
            var = jnp.mean((x - mu) ** 2, axis=-1, keepdims=True)
            return (x - mu) * jax.lax.rsqrt(var + 1e-05) * g + b

        def _mha(q_in, kv_in, W_qkv, b_qkv, W_o, b_o):
            Wq, Wk, Wv = jnp.split(W_qkv, 3, axis=0)
            bq, bk, bv = jnp.split(b_qkv, 3, axis=0)

            def heads(x, W, b):
                y = x @ W.T + b
                return y.reshape(y.shape[0], y.shape[1], NH, HD).transpose(0, 2, 1, 3)
            q, k, v = (heads(q_in, Wq, bq), heads(kv_in, Wk, bk), heads(kv_in, Wv, bv))
            scores = jnp.einsum('bhqd,bhkd->bhqk', q, k) * (1.0 / np.sqrt(HD))
            attn = jax.nn.softmax(scores, axis=-1)
            out = jnp.einsum('bhqk,bhkd->bhqd', attn, v)
            out = out.transpose(0, 2, 1, 3).reshape(q_in.shape)
            return out @ W_o.T + b_o
        residual = builder_state
        x = _layernorm(builder_state, g1, beta1)
        base_n = _layernorm(base_state, g1, beta1)
        x = residual + _mha(x, base_n, W_qkv, b_qkv, W_o, b_o)
        residual = x
        xn = _layernorm(x, g2, beta2)
        U = (xn @ W_in.T + b_in) @ Bmat

        def step(s, u_t):
            s = jax.nn.silu(s @ A.T) + u_t
            return (s, s)
        _, states = jax.lax.scan(step, jnp.zeros((builder_state.shape[0], S), U.dtype), U.transpose(1, 0, 2))
        ssm_out = jnp.einsum('tbs,sh->bth', states, Cmat)
        x = residual + ssm_out
        mod = program_probs.mean(axis=1) @ W_prog.T + b_prog
        return x + mod[:, None, :]
    x = _L0_xattn_ref(x, ctx_1024, mask_1xS2_bf0, L0_xattn_m_norm_w, L0_xattn_in_proj_w, L0_xattn_conv_w, L0_xattn_conv_b, L0_xattn_dt_bias, L0_xattn_A_log, L0_xattn_D_skip, L0_xattn_gnorm_w, L0_xattn_out_proj_w, L0_xattn_ca_ln_w, L0_xattn_ca_ln_b, L0_xattn_Wq, L0_xattn_Wk, L0_xattn_Wv, L0_xattn_Wo)
    x = _L1_xattn_ref(x, ctx_1024, ctx_1024, L1_xattn_W_q, L1_xattn_W_k, L1_xattn_W_v, L1_xattn_W_o, L1_xattn_w1, L1_xattn_b1, L1_xattn_w2, L1_xattn_b2)
    x = _L2_xattn_ref(x, ctx_1024, L2_xattn_q_norm_g, L2_xattn_q_norm_b, L2_xattn_kv_norm_g, L2_xattn_kv_norm_b, L2_xattn_Wq, L2_xattn_Wk, L2_xattn_Wv, L2_xattn_Wo, L2_xattn_bo)
    x = _L3_xattn_ref(x, ctx_1024, itok_BxS2_4_31999, ctxb_2048x64, L3_xattn_A, L3_xattn_Bmat, L3_xattn_Cmat, L3_xattn_W_in, L3_xattn_b_in, L3_xattn_W_qkv, L3_xattn_b_qkv, L3_xattn_W_o, L3_xattn_b_o, L3_xattn_W_prog, L3_xattn_b_prog, L3_xattn_g1, L3_xattn_beta1, L3_xattn_g2, L3_xattn_beta2)
    return x

_drawn_inputs = setup_inputs


def setup_inputs(seed=0):
    import zlib

    import numpy as np

    out = dict(_drawn_inputs(seed))
    spreads = {'L0_xattn_m_norm_w': (1.0, 0.2),
     'L0_xattn_conv_b': (0.0, 0.1),
     'L0_xattn_dt_bias': (-4.600165843963623, 0.6),
     'L0_xattn_D_skip': (1.0, 0.2),
     'L0_xattn_gnorm_w': (1.0, 0.2),
     'L0_xattn_ca_ln_w': (1.0, 0.6),
     'L0_xattn_ca_ln_b': (0.0, 0.8),
     'L1_xattn_b1': (0.0, 0.1),
     'L1_xattn_b2': (0.0, 0.1),
     'L2_xattn_q_norm_g': (1.0, 0.6),
     'L2_xattn_q_norm_b': (0.0, 0.8),
     'L2_xattn_kv_norm_g': (1.0, 0.2),
     'L2_xattn_kv_norm_b': (0.0, 0.1),
     'L2_xattn_bo': (0.0, 0.1),
     'L3_xattn_b_in': (0.0, 0.1),
     'L3_xattn_b_qkv': (0.0, 0.1),
     'L3_xattn_b_o': (0.0, 0.1),
     'L3_xattn_b_prog': (0.0, 0.1),
     'L3_xattn_g1': (1.0, 0.2),
     'L3_xattn_beta1': (0.0, 0.1),
     'L3_xattn_g2': (1.0, 0.2),
     'L3_xattn_beta2': (0.0, 0.1)}
    factors = {'L0_xattn_A_log': 8.0, 'L0_xattn_Wq': 8.0, 'L0_xattn_Wk': 8.0}
    for name, (base, spread) in spreads.items():
        noise = np.random.default_rng([zlib.crc32(name.encode()), seed]).standard_normal(out[name].shape)
        drawn = base * np.exp(spread * noise) if base else spread * noise
        out[name] = jnp.asarray(drawn.astype(out[name].dtype))
    for name, factor in factors.items():
        out[name] = (out[name] * factor).astype(out[name].dtype)
    return out
```

```python
from contextlib import ExitStack

import numpy as np

import concourse.bass as bass
from concourse import mybir

F32 = mybir.dt.float32
BF16 = mybir.dt.bfloat16
I32 = mybir.dt.int32
ALU = mybir.AluOpType
ACT = mybir.ActivationFunctionType
AX = mybir.AxisListType.X

P = 128
NB = 4
T = 512
D = 256
KD = D // P
NCH = T // P
NT = NB * NCH
EPS = 1e-5

DI = 512
NST = 128
HM = 8
HP = DI // HM
XBC = DI + 2 * NST
XG = XBC // P
CONV = 4

S3 = 64
STEPS = P // NB


class Layer:

    def __init__(self, name, heads, dh, first_unit):
        self.name, self.heads, self.dh = name, heads, dh
        self.width = heads * dh
        self.groups = self.width // P
        self.per_group = P // dh
        self.scale = float(dh) ** -0.5
        self.first = first_unit


L0 = Layer("L0", 8, 32, 0)
L1 = Layer("L1", 8, 16, 8)
L2 = Layer("L2", 16, 16, 16)
L3 = Layer("L3", 8, 32, 32)
LAYERS = (L0, L1, L2, L3)
UNITS = 40


def pack_plan():
    sizes = [
        ("ident", P),
        ("wk0", KD * 256), ("wv0", KD * 256), ("wk1", KD * 128), ("wv1", KD * 128),
        ("wk2", KD * 256), ("wv2", KD * 256), ("wk3", KD * 256), ("wv3", KD * 256),
        ("wprog3", 256), ("bprog3", 256),
        ("kvg2", KD), ("kvb2", KD), ("g31", KD), ("b31", KD), ("bk3", KD), ("bv3", 256),
        ("tri_le", P), ("tri_gt", P), ("ones", P),
        ("inw", KD * 1288), ("mnorm", KD), ("gnorm", 4), ("convw", XG * CONV), ("convb", XG),
        ("dtb", HM), ("alog", HM), ("dskip", HM), ("outw", 4 * 256),
        ("wq0", KD * 256), ("wo0", KD * 256), ("lng0", KD), ("lnb0", KD),
        ("wq1", KD * 128), ("wo1", 256), ("w1", KD * 256), ("w2", KD * 256), ("b1", KD), ("b2", 256),
        ("wq2", KD * 256), ("wo2", KD * 256), ("qg2", KD), ("qb2", KD), ("bo2", 256),
        ("wq3", KD * 256), ("wo3", KD * 256), ("bq3", KD), ("bo3", 256),
        ("win3", KD * 256), ("bin3", KD), ("bmat3", KD * S3), ("g32", KD), ("b32", KD),
        ("at3", S3), ("cmat3", 256),
        ("hm32", 4), ("hm16", 8), ("neghalf", 1), ("inv512", 1), ("pick", P),
    ]
    plan, at = {}, 0
    for name, n in sizes:
        plan[name] = (at, n)
        at += n
    return plan, at


PLAN, NPACK = pack_plan()
CUTS = [0, PLAN["tri_le"][0], PLAN["wq0"][0], NPACK]


class Signal:

    def __init__(self, sem, per):
        self.sem, self.per = sem, per

    def at(self, tile, n):
        return tile * self.per + n


PER = {"cin": 16, "c_tp": 2, "x_in": 16, "res_dma": 16, "m_conv": 4, "p_chain": 20,
       "r_z": STEPS, "r_th": STEPS, "r_r": STEPS, "r_res": 16, "r_out": 16 * NB}
HEAD_STEPS = ("qm", "s", "mx", "exp", "tp", "ev", "pv")
NORM_STEPS = ("bn", "ag", "ve", "rs", "nrm")
NORMS = ("L0", "L2", "L3", "u")


def counted(name):
    who, _, step = name.partition("_")
    if who in ("L0", "L1", "L2", "L3") and step in HEAD_STEPS:
        return f"heads_{step}", UNITS, LAYERS[int(who[1])].first
    if step.removeprefix("n_") in NORM_STEPS and who in NORMS:
        return f"norm_{step.removeprefix('n_')}", len(NORMS), NORMS.index(who)
    if who in ("L0", "L1", "L2", "L3") and step not in ("pre", "gelu"):
        return f"layer_{step}", len(LAYERS), int(who[1])
    if who in ("x1", "x2", "x3", "x4", "x5", "x6", "x7", "x8"):
        return "residual", 8, int(who[1]) - 1
    return name, PER.get(name, 1), 0


class Turn:

    def __init__(self, eng, pers, loop):
        self.eng = eng
        self.regs = {p: eng.alloc_register(name=f"{loop}_turn_x{p}") for p in pers}
        self.sum = eng.alloc_register(name=f"{loop}_sum")
        for r in self.regs.values():
            eng.reg_mov(r, 1)

    def value(self, per, n):
        if n == 1:
            return self.regs[per]
        self.eng.reg_add(self.sum, self.regs[per], n - 1)
        return self.sum

    def end(self):
        for p, r in self.regs.items():
            self.eng.reg_add(r, r, p)


def build(nc, x, ctx_in, probs, maskf, pack, res_dram, out):
    with ExitStack() as stack:
        def sb(name, shape, dt=F32):
            return stack.enter_context(nc.sbuf_tensor(name, shape, dt))

        def psum(name):
            return stack.enter_context(nc.psum_tensor(name, [P, 512], F32))

        sems = {}

        def sem(name):
            name = counted(name)[0]
            if name not in sems:
                sems[name] = stack.enter_context(nc.semaphore(name))
            return sems[name]

        def at(name, tile, n=1, apart=False):
            _, per, before = counted(name)
            value = tile.value(per, before + n)
            if apart:
                tile.eng.wait_ge(sem("par0"), 16)
            return sem(name), value

        W = sb("W", [P, NPACK])

        def w(name, parts=None):
            a, n = PLAN[name]
            v = W[:, a:a + n]
            return v if parts is None else v.rearrange("p (k n) -> p k n", k=parts)

        def col(name, i):
            a, n = PLAN[name]
            return W[:, a + i:a + i + 1]

        def wide(ap, n):
            return ap.unsqueeze(2).to_broadcast([P, ap.shape[1], n])

        KT = [sb(f"KT{i}", [P, l.groups, NB * T]) for i, l in enumerate(LAYERS)]
        V = [sb(f"V{i}", [P, NT, l.width]) for i, l in enumerate(LAYERS)]
        early = V[3][0:1, :, :].rearrange("p a n -> p (a n)")
        m_row = early[:, 0:T]
        m_tmp = early[:, T:4 * T].rearrange("p (i n) -> p i n", i=3)
        m_part = early[:, 4 * T:6 * T].bitcast(BF16)[:, 0:3 * T].rearrange("p (i n) -> p i n", i=3)
        m_rows = sb("m_rows", [3, T], BF16)
        ones_b = sb("ones_b", [3, P], BF16)
        at2 = sb("at2", [S3, P])
        mod = sb("mod", [NB, D])
        pmT = sb("pmT", [S3, NB])
        negA = sb("negA", [P, HM])
        bq3 = sb("bq3", [P, KD])
        hconv = sb("hconv", [P, XG * CONV])
        hconvb = sb("hconvb", [P, XG])
        hist = sb("hist", [P, NB, XG, CONV - 1])
        Hst = sb("Hst", [P, NB, DI])
        UT = sb("UT", [S3, T + 1, NB])
        R2 = sb("R2", [S3, STEPS + 1, NB])
        th3 = sb("th3", [S3, NB])
        SS = sb("SS", [S3, STEPS, NB])

        xrow = sb("xrow", [P, D])
        nrm = sb("nrm", [P, D])
        st = sb("st", [P, 16])
        xT = sb("xT", [P, KD, P])
        qT = sb("qT", [P, KD, P])
        hT = qT
        resr = nrm
        room0 = sb("room0", [P, 2 * T])
        room1 = sb("room1", [P, 2 * T])
        room2 = sb("room2", [P, T])
        cT = [xT, room0[:, 0:D].rearrange("p (k n) -> p k n", k=KD),
              room0[:, D:2 * D].rearrange("p (k n) -> p k n", k=KD)]
        keep = room2
        qm = room2[:, :].rearrange("p (h n) -> p h n", h=4)
        Pr = room0[:, :].rearrange("p (i n) -> p i n", i=2)
        PT = room1[:, :].rearrange("p (i k n) -> p i k n", i=2, k=NCH)
        nmax = sb("nmax", [P, UNITS])
        den = sb("den", [P, UNITS])
        rden = sb("rden", [P, UNITS])
        orows = sb("orows", [P, D])

        first = PLAN["wk0"][0]

        def over(n):
            nonlocal first
            first += n
            assert first <= PLAN["kvg2"][0]
            return W[:, first - n:first]

        xpad = over(XG * (P + CONV - 1)).rearrange("p (g n) -> p g n", g=XG)
        acc = over(XG * P).rearrange("p (g n) -> p g n", g=XG)
        th = over(XG * P).rearrange("p (g n) -> p g n", g=XG)
        dts = sb("dts", [P, 14, HM])
        dAm = room0[:, :].rearrange("p (h n) -> p h n", h=HM)
        seg = room1[:, :].rearrange("p (h n) -> p h n", h=HM)
        dec = sb("dec", [P, 3, HM])
        orow = acc.rearrange("p g n -> p (g n)")[:, 0:D]
        Br, GT = orows[:, 0:P], orows[:, P:2 * P]
        xr = room2
        xw = room0[:, DI:]
        y = over(DI)
        y2 = over(DI)
        xdt = over(DI)
        zt = th.rearrange("p g n -> p (g n)")[:, 0:DI]
        uT = room0[:, 0:DI].rearrange("p (k n) -> p k n", k=4)

        psS = [psum("psS0"), psum("psS1")]
        psT = [psum("psT0"), psum("psT1")]
        psO = psum("psO")
        psA = psum("psA")
        psB = psum("psB")
        psR = psum("psR")
        ident = w("ident")

        block = stack.enter_context(nc.Block())

        def tiles(eng, body, pers, loop="tiles"):
            t = Turn(eng, pers, loop)
            with eng.Fori(0, NCH) as c:
                with eng.Fori(0, NB) as b:
                    body(t, c, b)
                    t.end()
            return t

        def groups(eng, body, pers):
            t = Turn(eng, pers, "groups")
            with eng.Fori(0, T // STEPS) as k:
                body(t, k)
                t.end()

        @block.sync
        def _(sp):
            for i in range(3):
                sp.dma_start(W[:, CUTS[i]:CUTS[i + 1]], pack[:, CUTS[i]:CUTS[i + 1]]).then_inc(sem(f"par{i}"), 16)
            sp.wait_ge(sem("mask_parts"), 6)
            for i in range(3):
                sp.dma_start(m_rows[i:i + 1, :], m_part[0:1, i, :]).then_inc(sem("mask_rows"), 16)

            def ctx_tile(t, b, k):
                sp.wait_ge(*at("c_used", t))
                sp.dma_start(xrow[:, :], ctx_in[b, bass.ts(k, P), :]).then_inc(sem("cin"), 16)

            tiles(sp, ctx_tile, (1, 2, 16), "context")

            def tile(t, c, b):
                sp.wait_ge(*at("tile_done", t))
                sp.dma_start(xrow[:, :], x[b, bass.ts(c, P), :]).then_inc(sem("x_in"), 16)
                sp.wait_ge(*at("res_ready", t))
                sp.dma_start(res_dram[bass.ts(c, P), b, :], orow[:, :]).then_inc(sem("res_dma"), 16)
                sp.wait_ge(*at("res_dma", t, 16, apart=True))

            tiles(sp, tile, (1, 4, 8, 16, 20, UNITS))

            def group(t, k):
                sp.wait_ge(*at("g_done", t))
                sp.dma_start(resr[:, :], res_dram[bass.ts(k, STEPS)].rearrange("t b d -> (t b) d")
                             ).then_inc(sem("r_res"), 16)
                sp.wait_ge(*at("r_orow", t))
                for b in range(NB):
                    sp.dma_start(out[b, bass.ts(k, STEPS), :], orow[b:P:NB, :]).then_inc(sem("r_out"), 16)

            groups(sp, group, (1, 16, STEPS, 16 * NB))
            sp.wait_ge(sem("r_out"), 16 * NB * (T // STEPS))

        @block.gpsimd
        def _(pool):
            pool.dma_start(keep[:, :].bitcast(I32), maskf.partition_broadcast(P)).then_inc(sem("mask_in"), 16)
            pool.dma_start(m_row[:, :].bitcast(I32), maskf.rearrange("(a n) -> a n", a=1)).then_inc(sem("mask_in"), 16)
            pool.dma_start(V[0][:, :, :].rearrange("p a n -> p (a n)")[:, 0:NB * NCH * S3]
                           .rearrange("p (b k s) -> p b k s", b=NB, k=NCH),
                           probs.rearrange("b (k p) s -> p b k s", p=P)).then_inc(sem("probs_in"), 16)
            pool.memset(hist[:, :, :, :], 0.0)
            pool.memset(Hst[:, :, :], 0.0)
            pool.memset(UT[:, 0, :], 0.0)
            pool.memset(R2[:, 0, :], 0.0)
            pool.memset(ones_b[:, :], 1.0).then_inc(sem("zeroed"), 1)

            def root(name, k, t):
                pool.wait_ge(*at(f"{name}_ve", t))
                nc.gpsimd.tensor_tensor(st[:, k + 9:k + 10], st[:, k + 8:k + 9], w("neghalf"),
                                        ALU.pow).then_inc(sem(f"{name}_rs"), 1)

            pool.wait_ge(sem("par2"), 16)

            def ctx_tile(t, b, k):
                root("c", 0, t)

            tiles(pool, ctx_tile, (1, 2, 16), "context")

            def heads(l, t):
                i = LAYERS.index(l)
                pool.wait_ge(*at(f"{l.name}_qT", t, apart=True))
                for h in range(l.heads):
                    if h >= 4:
                        pool.wait_ge(*at(f"{l.name}_s", t, h - 3, apart=True))
                    nc.gpsimd.tensor_scalar(qm[:, h % 4, :], qT[:, h // l.per_group, :],
                                            col(f"hm{l.dh}", h % l.per_group), None,
                                            ALU.mult).then_inc(sem(f"{l.name}_qm"), 1)

            def tile(t, c, b):
                pool.wait_ge(*at("tile_done", t))
                root("m1", 0, t)
                nc.gpsimd.tensor_copy(xpad[:, :, 0:CONV - 1], hist[:, b, :, :]).then_inc(sem("m_hist"), 1)
                pool.wait_ge(*at("m_r", t))
                nc.gpsimd.tensor_tensor(dts[:, 6, :], dts[:, 5, :], dts[:, 5, :], ALU.mult).then_inc(sem("p_chain"), 1)
                n = 1
                pool.wait_ge(*at("p_chain", t, n, apart=True))
                nc.gpsimd.tensor_scalar(dts[:, 7, :], dts[:, 6, :], 1.0 / 19, 1.0 / 17, ALU.mult,
                                        ALU.add).then_inc(sem("p_chain"), 1)
                for q in (15, 13, 11, 9, 7, 5, 3, 1):
                    n += 1
                    pool.wait_ge(*at("p_chain", t, n))
                    nc.gpsimd.tensor_tensor(dts[:, 8, :], dts[:, 7, :], dts[:, 6, :], ALU.mult).then_inc(sem("p_chain"), 1)
                    n += 1
                    pool.wait_ge(*at("p_chain", t, n, apart=True))
                    nc.gpsimd.tensor_scalar(dts[:, 7, :], dts[:, 8, :], 1.0 / q, None, ALU.add).then_inc(sem("p_chain"), 1)
                n += 1
                pool.wait_ge(*at("p_chain", t, n))
                nc.gpsimd.tensor_tensor(dts[:, 8, :], dts[:, 7, :], dts[:, 5, :], ALU.mult).then_inc(sem("p_chain"), 1)
                n += 1
                pool.wait_ge(*at("p_chain", t, n, apart=True))
                nc.gpsimd.tensor_scalar(dts[:, 9, :], dts[:, 8, :], 2.0, None, ALU.mult).then_inc(sem("p_chain"), 1)
                n += 1
                pool.wait_ge(*at("p_chain", t, n))
                nc.gpsimd.tensor_tensor(dts[:, 10, :], dts[:, 9, :], dts[:, 1, :], ALU.add).then_inc(sem("m_dt"), 1)
                pool.wait_ge(*at("m_dt", t))
                nc.gpsimd.tensor_tensor(dts[:, 11, :], dts[:, 10, :], negA[:, :], ALU.mult).then_inc(sem("m_dA"), 1)
                pool.wait_ge(*at("m_dA", t, apart=True))
                for h in range(HM):
                    ins = nc.gpsimd.tensor_scalar(dAm[:, h, :], w("tri_le"), dts[:, 11, h:h + 1], None, ALU.mult)
                ins.then_inc(sem("m_dAm"), 1)
                pool.wait_ge(*at("m_xbc", t, 1, apart=True))
                nc.gpsimd.tensor_copy(hist[:, b, :, :], xpad[:, :, P:P + CONV - 1]).then_inc(sem("m_hist2"), 1)
                pool.wait_ge(*at("m_xr", t))
                nc.gpsimd.tensor_tensor(y2[:, :].rearrange("p (h n) -> p h n", h=HM),
                                        xr[:, :].rearrange("p (h n) -> p h n", h=HM),
                                        wide(w("dskip"), HP), ALU.mult).then_inc(sem("m_xD"), 1)
                pool.wait_ge(*at("m_xdt", t))
                pool.wait_ge(*at("m_dec", t))
                nc.gpsimd.tensor_tensor(xw[:, :].rearrange("p (h n) -> p h n", h=HM),
                                        xdt[:, :].rearrange("p (h n) -> p h n", h=HM),
                                        wide(dec[:, 1, :], HP), ALU.mult).then_inc(sem("m_xw"), 1)
                root("m2", 2, t)
                for i, l in enumerate(LAYERS):
                    if l is not L1:
                        root(f"{l.name}_n", 0, t)
                    heads(l, t)
                root("u", 0, t)

            tiles(pool, tile, (1, 4, 8, 16, 20, UNITS))

        @block.scalar
        def _(act):
            act.wait_ge(sem("par0"), 16)
            act.wait_ge(sem("par1"), 16)
            act.wait_ge(sem("par2"), 16)
            nc.scalar.activation(dts[:, 0, :], w("alog"), ACT.Exp).then_inc(sem("expA"), 1)

            def ctx_tile(t, b, k):
                act.wait_ge(*at("c_tp", t, 2))
                nc.scalar.copy(cT[0][:, :, :].rearrange("p k n -> p (k n)"), psA[:, 0:D])
                for i, (g, bb) in ((1, ("kvg2", "kvb2")), (2, ("g31", "b31"))):
                    for kk in range(KD):
                        ins = nc.scalar.activation(cT[i][:, kk, :], psA[:, D + kk * P:D + (kk + 1) * P], ACT.Identity,
                                                   bias=col(bb, kk), scale=col(g, kk))
                ins.then_inc(sem("c_ev"), 1)
                act.wait_ge(*at("c_k23", t))
                nc.scalar.copy(KT[2][:, :, bass.ts(b * NCH + k, P)], psO[:, 0:D].rearrange("p (g n) -> p g n", g=2))
                for g in range(2):
                    ins = nc.scalar.activation(KT[3][:, g, bass.ts(b * NCH + k, P)], psO[:, D + g * P:D + (g + 1) * P],
                                               ACT.Identity, bias=col("bk3", g))
                act.wait_ge(*at("c_v01", t))
                nc.scalar.copy(V[0][:, bass.ds(b * NCH + k, 1), :], psS[0][:, 0:256].unsqueeze(1))
                nc.scalar.copy(V[1][:, bass.ds(b * NCH + k, 1), :], psS[0][:, 256:384].unsqueeze(1)).then_inc(sem("c_act"), 1)

            act.wait_ge(sem("mod_pm"), 1)
            nc.scalar.copy(pmT[:, :], psB[0:S3, 0:NB]).then_inc(sem("mod_pmT"), 1)
            act.wait_ge(sem("mod_done"), 1)
            tiles(act, ctx_tile, (1, 2, 16), "context")

            def heads(l, t):
                name = l.name
                q0 = l.first
                for h in range(l.heads + 1):
                    if h < l.heads:
                        act.wait_ge(*at(f"{name}_mx", t, h + 1))
                        if h >= 2:
                            act.wait_ge(*at(f"{name}_tp", t, h - 1))
                        nc.scalar.activation(Pr[:, h % 2, :], psS[h % 2][:, :], ACT.Exp,
                                             bias=nmax[:, q0 + h:q0 + h + 1],
                                             accum_out=den[:, q0 + h:q0 + h + 1]).then_inc(sem(f"{name}_exp"), 1)
                    k = h - 1
                    if k >= 0 and k % 2 == 0:
                        act.wait_ge(*at(f"{name}_tp", t, k + 1))
                        if k >= 2:
                            act.wait_ge(*at(f"{name}_pv", t, k - 1))
                            act.wait_ge(*at(f"{name}_ev", t, k))
                        nc.scalar.copy(PT[:, k % 2, :, :].rearrange("p a n -> p (a n)"),
                                       psT[k % 2][:, :]).then_inc(sem(f"{name}_ev"), 1)

            def evac_xT(name, t, g=None, b=None, src=psA, dst=xT, out_name=None):
                act.wait_ge(*at(f"{name}_xtp", t))
                if g is None:
                    nc.scalar.copy(dst[:, :, :].rearrange("p k n -> p (k n)"), src[:, 0:D]).then_inc(sem(f"{name}_xT"), 1)
                else:
                    for kk in range(KD):
                        ins = nc.scalar.activation(dst[:, kk, :], src[:, kk * P:(kk + 1) * P], ACT.Identity,
                                                   bias=col(b, kk) if b else 0.0, scale=col(g, kk))
                    ins.then_inc(sem(f"{name}_xT"), 1)

            def attention(l, t, g=None, b=None):
                evac_xT(l.name, t, g, b)
                act.wait_ge(*at(f"{l.name}_q", t))
                for gi in range(l.groups):
                    ins = nc.scalar.activation(qT[:, gi, :], psB[:, gi * P:(gi + 1) * P], ACT.Identity,
                                               bias=bq3[:, gi:gi + 1] if l is L3 else 0.0, scale=l.scale)
                ins.then_inc(sem(f"{l.name}_qT"), 1)
                heads(l, t)
                act.wait_ge(*at(f"{l.name}_otp", t))
                nc.scalar.copy(hT[:, 0:l.groups, :].rearrange("p k n -> p (k n)"),
                               psA[:, 0:l.width]).then_inc(sem(f"{l.name}_oT"), 1)

            def tile(t, c, b):
                act.wait_ge(*at("tile_done", t))
                evac_xT("m1", t, "mnorm")
                act.wait_ge(*at("m_pa", t))
                nc.scalar.copy(xpad[:, 0:4, CONV - 1:], psB[:, :].rearrange("p (g n) -> p g n", g=4))
                act.wait_ge(*at("m_pb", t))
                nc.scalar.copy(xpad[:, 4:6, CONV - 1:],
                               psO[:, 0:256].rearrange("p (g n) -> p g n", g=2)).then_inc(sem("m_xbc"), 1)
                act.wait_ge(*at("m_v", t))
                nc.scalar.activation(dts[:, 3, :], dts[:, 2, :], ACT.Exp).then_inc(sem("m_e"), 1)
                act.wait_ge(*at("m_conv", t, 4))
                nc.scalar.activation(th[:, :, :].rearrange("p g n -> p (g n)"),
                                     acc[:, :, :].rearrange("p g n -> p (g n)"), ACT.Tanh).then_inc(sem("m_th"), 1)
                act.wait_ge(*at("m_xc", t))
                act.wait_ge(*at("m_z", t))
                nc.scalar.activation(zt, psS[0][:, :], ACT.Tanh, scale=0.5).then_inc(sem("m_zt"), 1)
                act.wait_ge(*at("m_seg", t, 1))
                for i in range(2):
                    nc.scalar.activation(seg[:, 4 * i:4 * i + 4, :].rearrange("p g n -> p (g n)"), psT[i][:, :], ACT.Exp)
                nc.scalar.activation(dec[:, :, :].rearrange("p g n -> p (g n)"), psA[:, 256:256 + 3 * HM],
                                     ACT.Exp).then_inc(sem("m_dec"), 1)
                act.wait_ge(*at("m_rows", t))
                nc.scalar.copy(xr[:, :], psS[1][:, :]).then_inc(sem("m_xr"), 1)
                nc.scalar.copy(Br[:, :], psA[:, 0:NST]).then_inc(sem("m_Br"), 1)
                act.wait_ge(*at("m_utp", t))
                for k in range(4):
                    ins = nc.scalar.activation(uT[:, k, :], psS[1][:, k * P:(k + 1) * P], ACT.Copy,
                                               scale=col("gnorm", k))
                ins.then_inc(sem("m_uT"), 1)
                attention(L0, t, "lng0", "lnb0")
                attention(L1, t)
                evac_xT("f", t)
                act.wait_ge(*at("f_h", t))
                for g in range(KD):
                    ins = nc.scalar.activation(hT[:, g, :], psB[:, g * P:(g + 1) * P], ACT.Relu, bias=col("b1", g))
                ins.then_inc(sem("f_hT"), 1)
                attention(L2, t, "qg2", "qb2")
                act.wait_ge(*at("L2_pre", t))
                nc.scalar.activation(nrm[:, :], orows[:, :], ACT.Gelu).then_inc(sem("L2_gelu"), 1)
                attention(L3, t, "g31", "b31")
                evac_xT("u", t, "g32", "b32")
                act.wait_ge(*at("u_h", t))
                for g in range(KD):
                    ins = nc.scalar.activation(hT[:, g, :], psB[:, g * P:(g + 1) * P], ACT.Identity, bias=col("bin3", g))
                ins.then_inc(sem("u_hT"), 1)
                act.wait_ge(*at("u_u", t))
                nc.scalar.copy(UT[:, bass.ds(c * P + 1, P), bass.ds(b, 1)].squeeze(2) if False else
                               UT[:, bass.ds(c * P + 1, P), bass.ds(b, 1)],
                               psA[0:S3, 0:P].unsqueeze(2)).then_inc(sem("u_out"), 1)

            tiles(act, tile, (1, 4, 8, 16, 20, UNITS))

            def group(t, k):
                for j in range(STEPS):
                    act.wait_ge(*at("r_z", t, j + 1))
                    if j:
                        act.wait_ge(*at("r_r", t, j))
                    nc.scalar.activation(th3[:, :], psR[0:S3, NB * j:NB * (j + 1)], ACT.Tanh,
                                         scale=0.5).then_inc(sem("r_th"), 1)

            groups(act, group, (1, 16, STEPS, 16 * NB))

        @block.vector
        def _(dve):
            for i in range(3):
                dve.wait_ge(sem(f"par{i}"), 16)
            dve.wait_ge(sem("mask_in"), 32)
            dve.wait_ge(sem("expA"), 1)
            nc.vector.tensor_scalar(keep[:, :], keep[:, :].bitcast(I32), -1.0, 1.0, ALU.mult, ALU.add)
            nc.vector.tensor_scalar(negA[:, :], dts[:, 0, :], -1.0, None, ALU.mult)
            nc.vector.tensor_scalar(at2[:, :], W[0:S3, PLAN["at3"][0]:PLAN["at3"][0] + P], 0.5, None, ALU.mult)
            nc.vector.tensor_scalar(bq3[:, :], w("bq3"), L3.scale, None, ALU.mult)
            nc.vector.tensor_scalar(hconv[:, :], w("convw"), 0.5, None, ALU.mult)
            nc.vector.tensor_scalar(hconvb[:, :], w("convb"), 0.5, None, ALU.mult)
            nc.vector.tensor_scalar(m_tmp[:, 0, :], m_row[:, :].bitcast(I32), -1e9, None, ALU.mult).then_inc(sem("mask_parts"), 1)
            dve.wait_ge(sem("mask_parts"), 1)
            nc.vector.tensor_copy(m_part[:, 0, :], m_tmp[:, 0, :]).then_inc(sem("mask_parts"), 1)
            dve.wait_ge(sem("mask_parts"), 2)
            nc.vector.tensor_tensor(m_tmp[:, 1, :], m_tmp[:, 0, :], m_part[:, 0, :], ALU.subtract).then_inc(sem("mask_parts"), 1)
            dve.wait_ge(sem("mask_parts"), 3)
            nc.vector.tensor_copy(m_part[:, 1, :], m_tmp[:, 1, :]).then_inc(sem("mask_parts"), 1)
            dve.wait_ge(sem("mask_parts"), 4)
            nc.vector.tensor_tensor(m_tmp[:, 2, :], m_tmp[:, 1, :], m_part[:, 1, :], ALU.subtract).then_inc(sem("mask_parts"), 1)
            dve.wait_ge(sem("mask_parts"), 5)
            nc.vector.tensor_copy(m_part[:, 2, :], m_tmp[:, 2, :]).then_inc(sem("mask_parts"), 1)
            dve.wait_ge(sem("mod_mm"), 1)
            nc.vector.tensor_tensor(mod[:, :], psS[0][0:NB, 0:D], w("bprog3")[0:NB, :], ALU.add).then_inc(sem("mod_done"), 1)
            nc.vector.memset(st[:, 0:1], 0.0).then_inc(sem("c_used"), 1)

            def norm_rows(name, t, src):
                nc.vector.bn_stats(st[:, 0:6], src).then_inc(sem(f"{name}_bn"), 1)
                dve.wait_ge(*at(f"{name}_bn", t, apart=True))
                nc.vector.bn_aggr(st[:, 6:8], st[:, 0:6]).then_inc(sem(f"{name}_ag"), 1)
                dve.wait_ge(*at(f"{name}_ag", t))
                nc.vector.tensor_scalar(st[:, 8:9], st[:, 7:8], EPS, None, ALU.add).then_inc(sem(f"{name}_ve"), 1)
                dve.wait_ge(*at(f"{name}_rs", t))
                nc.vector.tensor_scalar(nrm[:, :], src, st[:, 6:7], st[:, 9:10], ALU.subtract,
                                        ALU.mult).then_inc(sem(f"{name}_nrm"), 1)

            def ctx_tile(t, b, k):
                dve.wait_ge(*at("c_used", t))
                dve.wait_ge(*at("cin", t, 16))
                norm_rows("c", t, xrow[:, :])
                dve.wait_ge(*at("c_k01", t))
                nc.vector.tensor_tensor(KT[0][:, :, bass.ts(b * NCH + k, P)], psB[:, 0:256].rearrange("p (g n) -> p g n", g=2),
                                        keep[:, bass.ts(k, P)].unsqueeze(1).to_broadcast([P, 2, P]), ALU.mult)
                nc.vector.tensor_copy(KT[1][:, 0, bass.ts(b * NCH + k, P)], psB[:, 256:384])
                dve.wait_ge(*at("c_v23", t))
                nc.vector.tensor_copy(V[2][:, bass.ds(b * NCH + k, 1), :], psS[1][:, 0:256].unsqueeze(1))
                nc.vector.tensor_tensor(V[3][:, bass.ds(b * NCH + k, 1), :], psS[1][:, 256:512].unsqueeze(1),
                                        w("bv3").unsqueeze(1), ALU.add).then_inc(sem("c_dve"), 1)
                dve.wait_ge(*at("c_act", t))
                dve.wait_ge(*at("c_dve", t))
                nc.vector.memset(st[:, 0:1], 0.0).then_inc(sem("c_used"), 1)

            tiles(dve, ctx_tile, (1, 2, 16), "context")
            nc.vector.memset(st[:, 10:11], 0.0).then_inc(sem("tile_done"), 1)

            def heads(l, t):
                name, q0 = l.name, l.first
                for h in range(l.heads + 1):
                    if h < l.heads:
                        dve.wait_ge(*at(f"{name}_s", t, h + 1))
                        nc.vector.tensor_reduce(nmax[:, q0 + h:q0 + h + 1], psS[h % 2][:, :], AX, ALU.max,
                                                negate=True).then_inc(sem(f"{name}_mx"), 1)
                    k = h - 1
                    if k >= 0 and k % 2 == 1:
                        dve.wait_ge(*at(f"{name}_tp", t, k + 1))
                        if k >= 2:
                            dve.wait_ge(*at(f"{name}_pv", t, k - 1))
                        dve.wait_ge(*at(f"{name}_ev", t, k))
                        nc.vector.tensor_copy(PT[:, k % 2, :, :].rearrange("p a n -> p (a n)"),
                                              psT[k % 2][:, :]).then_inc(sem(f"{name}_ev"), 1)
                dve.wait_ge(*at(f"{name}_exp", t, l.heads))
                nc.vector.reciprocal(rden[:, q0:q0 + l.heads], den[:, q0:q0 + l.heads]).then_inc(sem(f"{name}_rd"), 1)
                dve.wait_ge(*at(f"{name}_rd", t))
                dve.wait_ge(*at(f"{name}_pv", t, l.heads))
                nc.vector.tensor_tensor(orows[:, 0:l.width].rearrange("p (h n) -> p h n", h=l.heads),
                                        psO[:, 0:l.width].rearrange("p (h n) -> p h n", h=l.heads),
                                        wide(rden[:, q0:q0 + l.heads], l.dh), ALU.mult).then_inc(sem(f"{name}_on"), 1)

            def add_rows(name, t, src, out_name):
                dve.wait_ge(*at(name, t))
                nc.vector.tensor_tensor(xrow[:, :], xrow[:, :], src, ALU.add).then_inc(sem(out_name), 1)
                dve.wait_ge(*at(out_name, t))

            def tile(t, c, b):
                dve.wait_ge(*at("tile_done", t))
                dve.wait_ge(*at("x_in", t, 16))
                nc.vector.tensor_tensor_reduce(out=y[:, 0:D], in0=xrow[:, :], in1=xrow[:, :], scale=1.0, scalar=0.0,
                                               op0=ALU.mult, op1=ALU.add, accum_out=st[:, 7:8]).then_inc(sem("m1_ss"), 1)
                dve.wait_ge(*at("m1_ss", t))
                nc.vector.tensor_scalar(st[:, 8:9], st[:, 7:8], 1.0 / D, EPS, ALU.mult, ALU.add).then_inc(sem("m1_ve"), 1)
                dve.wait_ge(*at("m1_rs", t))
                nc.vector.tensor_scalar(nrm[:, :], xrow[:, :], st[:, 9:10], None, ALU.mult).then_inc(sem("m1_nrm"), 1)
                dve.wait_ge(*at("m_xbc", t))
                nc.vector.tensor_tensor(dts[:, 0, :], psO[:, 256:256 + HM], w("dtb"), ALU.add).then_inc(sem("m_v0"), 1)
                dve.wait_ge(*at("m_v0", t))
                nc.vector.tensor_scalar(dts[:, 1, :], dts[:, 0, :], 0.0, None, ALU.max).then_inc(sem("m_v1"), 1)
                dve.wait_ge(*at("m_v1", t))
                nc.vector.scalar_tensor_tensor(dts[:, 2, :], dts[:, 1, :], -2.0, dts[:, 0, :], ALU.mult,
                                               ALU.add).then_inc(sem("m_v"), 1)
                dve.wait_ge(*at("m_hist", t))
                for k in range(CONV):
                    if k:
                        dve.wait_ge(*at("m_conv", t, k))
                    for g in range(XG):
                        src = xpad[:, g, k:k + P]
                        wk = hconv[:, g * CONV + k:g * CONV + k + 1]
                        if k == 0:
                            ins = nc.vector.tensor_scalar(acc[:, g, :], src, wk, hconvb[:, g:g + 1], ALU.mult, ALU.add)
                        else:
                            ins = nc.vector.scalar_tensor_tensor(acc[:, g, :], src, wk, acc[:, g, :], ALU.mult, ALU.add)
                    ins.then_inc(sem("m_conv"), 1)
                    if k == 0:
                        dve.wait_ge(*at("m_e", t))
                        nc.vector.tensor_scalar(dts[:, 4, :], dts[:, 3, :], 2.0, None, ALU.add).then_inc(sem("m_e2"), 1)
                    if k == 1:
                        dve.wait_ge(*at("m_e2", t))
                        nc.vector.reciprocal(dts[:, 12, :], dts[:, 4, :]).then_inc(sem("m_rc"), 1)
                    if k == 2:
                        dve.wait_ge(*at("m_rc", t))
                        nc.vector.tensor_tensor(dts[:, 5, :], dts[:, 3, :], dts[:, 12, :], ALU.mult).then_inc(sem("m_r"), 1)
                dve.wait_ge(*at("m_th", t))
                nc.vector.scalar_tensor_tensor(acc[:, :, :].rearrange("p g n -> p (g n)"),
                                               th[:, :, :].rearrange("p g n -> p (g n)"), 1.0,
                                               acc[:, :, :].rearrange("p g n -> p (g n)"), ALU.add,
                                               ALU.mult).then_inc(sem("m_xc"), 1)
                dve.wait_ge(*at("m_zt", t))
                nc.vector.scalar_tensor_tensor(zt, zt, 1.0, psS[0][:, :], ALU.add,
                                               ALU.mult).then_inc(sem("m_zs"), 1)
                hv = lambda a: a.rearrange("p (h n) -> p h n", h=HM)
                dve.wait_ge(*at("m_xr", t))
                dve.wait_ge(*at("m_dt", t))
                nc.vector.tensor_tensor(hv(xdt[:, :]), hv(xr[:, :]), wide(dts[:, 10, :], HP), ALU.mult).then_inc(sem("m_xdt"), 1)
                dve.wait_ge(*at("m_Br", t))
                nc.vector.tensor_tensor(GT[:, :], psA[:, P:2 * P], w("tri_le"), ALU.mult).then_inc(sem("m_GT"), 1)
                dve.wait_ge(*at("m_GT", t))
                dve.wait_ge(*at("m_dec", t))
                nc.vector.tensor_tensor(seg[:, :, :], seg[:, :, :], GT[:, :].unsqueeze(1).to_broadcast([P, HM, P]),
                                        ALU.mult).then_inc(sem("m_M"), 1)
                dve.wait_ge(*at("m_inter", t))
                nc.vector.tensor_tensor(hv(y[:, :]), hv(psB[:, :]), wide(dec[:, 0, :], HP), ALU.mult).then_inc(sem("m_y0"), 1)
                dve.wait_ge(*at("m_y0", t))
                dve.wait_ge(*at("m_intra", t))
                nc.vector.tensor_tensor(y[:, :], y[:, :], psO[:, :], ALU.add).then_inc(sem("m_y1"), 1)
                dve.wait_ge(*at("m_y1", t))
                dve.wait_ge(*at("m_xD", t))
                nc.vector.tensor_tensor(y[:, :], y[:, :], y2[:, :], ALU.add).then_inc(sem("m_y2"), 1)
                dve.wait_ge(*at("m_y2", t))
                nc.vector.tensor_tensor(y[:, :], y[:, :], zt, ALU.mult).then_inc(sem("m_y3"), 1)
                dve.wait_ge(*at("m_y3", t))
                nc.vector.tensor_tensor_reduce(out=y2[:, :], in0=y[:, :], in1=y[:, :], scale=1.0, scalar=0.0,
                                               op0=ALU.mult, op1=ALU.add, accum_out=st[:, 12:13]).then_inc(sem("m2_ss"), 1)
                dve.wait_ge(*at("m2_ss", t))
                nc.vector.tensor_scalar(st[:, 10:11], st[:, 12:13], 0.25 / DI, EPS, ALU.mult, ALU.add).then_inc(sem("m2_ve"), 1)
                dve.wait_ge(*at("m_xw", t))
                nc.vector.tensor_tensor(hv(xdt[:, :]), Hst[:, bass.ds(b, 1), :].rearrange("p a (h n) -> p (a h) n", h=HM),
                                        wide(dec[:, 2, :], HP), ALU.mult).then_inc(sem("m_Hd"), 1)
                dve.wait_ge(*at("m_Hd", t))
                dve.wait_ge(*at("m_state", t))
                nc.vector.tensor_tensor(Hst[:, bass.ds(b, 1), :], xdt[:, :].unsqueeze(1), psT[0][:, :].unsqueeze(1),
                                        ALU.add).then_inc(sem("m_H"), 1)
                dve.wait_ge(*at("m2_rs", t))
                nc.vector.tensor_scalar(y[:, :], y[:, :], st[:, 11:12], 0.5, ALU.mult, ALU.mult).then_inc(sem("m_un"), 1)
                add_rows("m_out", t, psB[:, 0:D], "x1")
                norm_rows("L0_n", t, xrow[:, :])
                heads(L0, t)
                add_rows("L0_op", t, psB[:, 0:D], "x2")
                heads(L1, t)
                add_rows("L1_op", t, psB[:, 0:D], "x3")
                add_rows("f_o", t, psA[:, 0:D], "x4")
                nc.vector.tensor_tensor(xrow[:, :], xrow[:, :], w("b2"), ALU.add).then_inc(sem("x5"), 1)
                dve.wait_ge(*at("x5", t))
                norm_rows("L2_n", t, xrow[:, :])
                heads(L2, t)
                dve.wait_ge(*at("L2_op", t))
                nc.vector.tensor_tensor(orows[:, :], psB[:, 0:D], w("bo2"), ALU.add).then_inc(sem("L2_pre"), 1)
                add_rows("L2_gelu", t, nrm[:, :], "x6")
                norm_rows("L3_n", t, xrow[:, :])
                heads(L3, t)
                add_rows("L3_op", t, psB[:, 0:D], "x7")
                nc.vector.tensor_tensor(xrow[:, :], xrow[:, :], w("bo3"), ALU.add).then_inc(sem("x8"), 1)
                dve.wait_ge(*at("x8", t))
                norm_rows("u", t, xrow[:, :])
                nc.vector.tensor_copy(orow[:, :], xrow[:, :]).then_inc(sem("res_ready"), 1)
                dve.wait_ge(*at("u_out", t))
                dve.wait_ge(*at("res_dma", t, 16))
                dve.wait_ge(*at("m_H", t))
                dve.wait_ge(*at("m_hist2", t))
                nc.vector.memset(st[:, 13:14], 0.0).then_inc(sem("tile_done"), 1)

            tiles(dve, tile, (1, 4, 8, 16, 20, UNITS))
            dve.wait_ge(sem("tile_done"), NT + 1)
            nc.vector.memset(st[:, 13:14], 0.0).then_inc(sem("g_done"), 1)

            def group(t, k):
                for j in range(STEPS):
                    dve.wait_ge(*at("r_th", t, j + 1))
                    nc.vector.scalar_tensor_tensor(R2[:, j + 1, :], th3[:, :], 1.0, psR[0:S3, NB * j:NB * (j + 1)],
                                                   ALU.add, ALU.mult).then_inc(sem("r_r"), 1)
                dve.wait_ge(*at("r_r", t, STEPS))
                nc.vector.scalar_tensor_tensor(SS[:, :, :], R2[:, 1:, :], 0.5, UT[:, bass.ds(k * STEPS + 1, STEPS), :],
                                               ALU.mult, ALU.add).then_inc(sem("r_ss"), 1)
                nc.vector.tensor_copy(R2[:, 0, :], R2[:, STEPS, :]).then_inc(sem("r_last"), 1)
                dve.wait_ge(*at("r_mm", t))
                dve.wait_ge(*at("r_res", t, 16))
                nc.vector.tensor_tensor(orow[:, :], psB[:, 0:D], resr[:, :], ALU.add).then_inc(sem("r_orow"), 1)
                dve.wait_ge(*at("r_out", t, 16 * NB))
                dve.wait_ge(*at("r_last", t))
                dve.wait_ge(*at("r_orow", t))
                nc.vector.memset(st[:, 13:14], 0.0).then_inc(sem("g_done"), 1)

            groups(dve, group, (1, 16, STEPS, 16 * NB))

        @block.tensor
        def _(pe):
            mm = nc.tensor.matmul
            for i in range(3):
                pe.wait_ge(sem(f"par{i}"), 16)
            pe.wait_ge(sem("probs_in"), 16)
            pe.wait_ge(sem("zeroed"), 1)
            pe.wait_ge(sem("mask_rows"), 48)
            pb = V[0][:, :, :].rearrange("p a n -> p (a n)")[:, 0:NB * NCH * S3].rearrange(
                "p (b k s) -> p b k s", b=NB, k=NCH)
            for b in range(NB):
                for k in range(NCH):
                    ins = mm(psB[0:S3, b:b + 1], pb[:, b, k, :], w("inv512"), start=k == 0, stop=k == NCH - 1)
            ins.then_inc(sem("mod_pm"), 1)
            pe.wait_ge(sem("mod_pmT"), 1)
            a = PLAN["wprog3"][0]
            mm(psS[0][0:NB, 0:D], pmT[:, :], W[0:S3, a:a + D], start=True, stop=True).then_inc(sem("mod_mm"), 1)

            def turn(dst, src, n):
                for k in range(n):
                    ins = nc.tensor.transpose(dst[:, k * P:(k + 1) * P], src[:, k * P:(k + 1) * P], ident)
                return ins

            def proj_T(dst, wname, src, n):
                for g in range(n):
                    for kk in range(KD):
                        ins = mm(dst[:, g * P:(g + 1) * P], w(wname, KD)[:, kk, g * P:(g + 1) * P], src[:, kk, :],
                                 start=kk == 0, stop=kk == KD - 1)
                return ins

            def proj(dst, wname, src, n, parts=KD, at_col=0):
                for kk in range(parts):
                    ins = mm(dst, src[:, kk, :], w(wname, parts)[:, kk, at_col:at_col + n], start=kk == 0, stop=kk == parts - 1)
                return ins

            def ctx_tile(t, b, k):
                pe.wait_ge(*at("c_used", t))
                pe.wait_ge(*at("cin", t, 16))
                turn(psA, xrow, KD).then_inc(sem("c_tp"), 1)
                pe.wait_ge(*at("c_nrm", t))
                turn(psA[:, D:2 * D], nrm, KD).then_inc(sem("c_tp"), 1)
                pe.wait_ge(*at("c_ev", t))
                proj_T(psB[:, 0:256], "wk0", cT[0], 2)
                proj_T(psB[:, 256:384], "wk1", cT[0], 1).then_inc(sem("c_k01"), 1)
                proj_T(psO[:, 0:256], "wk2", cT[1], 2)
                proj_T(psO[:, 256:512], "wk3", cT[2], 2).then_inc(sem("c_k23"), 1)
                proj(psS[0][:, 0:256], "wv0", cT[0], 256)
                proj(psS[0][:, 256:384], "wv1", cT[0], 128).then_inc(sem("c_v01"), 1)
                proj(psS[1][:, 0:256], "wv2", cT[1], 256)
                proj(psS[1][:, 256:512], "wv3", cT[2], 256).then_inc(sem("c_v23"), 1)

            pe.wait_ge(sem("mod_done"), 1)
            tiles(pe, ctx_tile, (1, 2, 16), "context")

            def attention(l, t, b):
                i, name = LAYERS.index(l), l.name
                if l is not L1:
                    pe.wait_ge(*at(f"{name}_n_nrm", t))
                turn(psA, xrow if l is L1 else nrm, KD).then_inc(sem(f"{name}_xtp"), 1)
                pe.wait_ge(*at(f"{name}_xT", t))
                proj_T(psB, f"wq{i}", xT, l.groups).then_inc(sem(f"{name}_q"), 1)
                for h in range(l.heads + 2):
                    if h < l.heads:
                        pe.wait_ge(*at(f"{name}_qm", t, h + 1))
                        if h >= 2:
                            pe.wait_ge(*at(f"{name}_exp", t, h - 1))
                        ins = mm(psS[h % 2][:, :], qm[:, h % 4, :], KT[i][:, h // l.per_group, bass.ds(b * T, T)],
                                 start=True, stop=l is not L0)
                        if l is L0:
                            ins = mm(psS[h % 2][:, :], ones_b[:, :], m_rows[:, :], start=False, stop=True)
                        ins.then_inc(sem(f"{name}_s"), 1)
                    k = h - 1
                    if 0 <= k < l.heads:
                        pe.wait_ge(*at(f"{name}_exp", t, k + 1))
                        if k >= 2:
                            pe.wait_ge(*at(f"{name}_ev", t, k - 1))
                        turn(psT[k % 2], Pr[:, k % 2, :], NCH).then_inc(sem(f"{name}_tp"), 1)
                    k = h - 2
                    if k >= 0:
                        pe.wait_ge(*at(f"{name}_ev", t, k + 1))
                        for kt in range(NCH):
                            ins = mm(psO[:, k * l.dh:(k + 1) * l.dh], PT[:, k % 2, kt, :],
                                     V[i][:, bass.ds(b * NCH + kt, 1), k * l.dh:(k + 1) * l.dh].squeeze(1),
                                     start=kt == 0, stop=kt == NCH - 1)
                        ins.then_inc(sem(f"{name}_pv"), 1)
                pe.wait_ge(*at(f"{name}_on", t))
                turn(psA, orows, l.groups).then_inc(sem(f"{name}_otp"), 1)
                pe.wait_ge(*at(f"{name}_oT", t))
                proj(psB[:, 0:D], f"wo{i}", hT, D, l.groups).then_inc(sem(f"{name}_op"), 1)

            def tile(t, c, b):
                pe.wait_ge(*at("tile_done", t))
                pe.wait_ge(*at("m1_nrm", t))
                turn(psA, nrm, KD).then_inc(sem("m1_xtp"), 1)
                pe.wait_ge(*at("m1_xT", t))
                inw = w("inw", KD)
                for g in range(XG):
                    dst = psB[:, g * P:(g + 1) * P] if g < 4 else psO[:, (g - 4) * P:(g - 3) * P]
                    for kk in range(KD):
                        ins = mm(dst, inw[:, kk, DI + g * P:DI + (g + 1) * P], xT[:, kk, :], start=kk == 0, stop=kk == KD - 1)
                    if g == 3:
                        ins.then_inc(sem("m_pa"), 1)
                proj(psO[:, 256:256 + HM], "inw", xT, HM, at_col=DI + XBC).then_inc(sem("m_pb"), 1)
                proj(psS[0][:, :], "inw", xT, DI).then_inc(sem("m_z"), 1)
                pe.wait_ge(*at("m_dA", t))
                dA = dts[:, 11, :]
                for q, name in enumerate(("tri_le", "tri_gt", "ones")):
                    mm(psA[:, 256 + q * HM:256 + (q + 1) * HM], w(name), dA, start=True, stop=True)
                pe.wait_ge(*at("m_dAm", t))
                for i in range(2):
                    ins = mm(psT[i][:, :], w("tri_gt"), dAm[:, 4 * i:4 * i + 4, :].rearrange("p h n -> p (h n)"),
                             start=True, stop=True)
                ins.then_inc(sem("m_seg"), 1)
                pe.wait_ge(*at("m_xc", t))
                pe.wait_ge(*at("m_dec", t))
                for g in range(4):
                    nc.tensor.transpose(psS[1][:, g * P:(g + 1) * P], acc[:, g, :], ident)
                nc.tensor.transpose(psA[:, 0:P], acc[:, 4, :], ident)
                mm(psA[:, P:2 * P], acc[:, 4, :], acc[:, 5, :], start=True, stop=True).then_inc(sem("m_rows"), 1)
                pe.wait_ge(*at("m_v", t))
                mm(psB[:, :], acc[:, 5, :], Hst[:, bass.ds(b, 1), :].rearrange("p a n -> p (a n)"), start=True,
                   stop=True).then_inc(sem("m_inter"), 1)
                pe.wait_ge(*at("m_M", t))
                pe.wait_ge(*at("m_xdt", t))
                for h in range(HM):
                    ins = mm(psO[:, h * HP:(h + 1) * HP], seg[:, h, :], xdt[:, h * HP:(h + 1) * HP], start=True, stop=True)
                ins.then_inc(sem("m_intra"), 1)
                pe.wait_ge(*at("m_xw", t))
                mm(psT[0][:, :], Br[:, :], xw[:, :], start=True, stop=True).then_inc(sem("m_state"), 1)
                pe.wait_ge(*at("m_un", t))
                turn(psS[1], y, 4).then_inc(sem("m_utp"), 1)
                pe.wait_ge(*at("m_uT", t))
                proj(psB[:, 0:D], "outw", uT, D, 4).then_inc(sem("m_out"), 1)
                attention(L0, t, b)
                pe.wait_ge(*at("x2", t))
                attention(L1, t, b)
                pe.wait_ge(*at("x3", t))
                turn(psA, xrow, KD).then_inc(sem("f_xtp"), 1)
                pe.wait_ge(*at("f_xT", t))
                proj_T(psB, "w1", xT, KD).then_inc(sem("f_h"), 1)
                pe.wait_ge(*at("f_hT", t))
                proj(psA[:, 0:D], "w2", hT, D).then_inc(sem("f_o"), 1)
                attention(L2, t, b)
                attention(L3, t, b)
                pe.wait_ge(*at("u_nrm", t))
                turn(psA, nrm, KD).then_inc(sem("u_xtp"), 1)
                pe.wait_ge(*at("u_xT", t))
                proj_T(psB, "win3", xT, KD).then_inc(sem("u_h"), 1)
                pe.wait_ge(*at("u_hT", t))
                for kk in range(KD):
                    ins = mm(psA[0:S3, 0:P], w("bmat3", KD)[:, kk, :], hT[:, kk, :], start=kk == 0, stop=kk == KD - 1)
                ins.then_inc(sem("u_u"), 1)

            tiles(pe, tile, (1, 4, 8, 16, 20, UNITS))

            def group(t, k):
                pe.wait_ge(*at("g_done", t))
                a3 = PLAN["at3"][0]
                mm(psR[:, 0:P], W[0:S3, a3:a3 + P],
                   UT[:, bass.ds(k * STEPS, STEPS), :].rearrange("p t b -> p (t b)"), start=True, stop=True,
                   skip_group_check=True)
                for j in range(STEPS):
                    if j:
                        pe.wait_ge(*at("r_r", t, j))
                    mm(psR[:, NB * j:NB * (j + 1)], at2[:, :], R2[:, j, :], start=False, stop=True,
                       skip_group_check=True).then_inc(sem("r_z"), 1)
                pe.wait_ge(*at("r_ss", t))
                c3 = PLAN["cmat3"][0]
                mm(psB[:, 0:D], SS[:, :, :].rearrange("p t b -> p (t b)"), W[0:S3, c3:c3 + D], start=True,
                   stop=False)
                p3 = PLAN["pick"][0]
                mm(psB[:, 0:D], W[0:NB, p3:p3 + P], mod[:, :], start=False, stop=True).then_inc(sem("r_mm"), 1)

            groups(pe, group, (1, 16, STEPS, 16 * NB))


def kernel(**inputs):
    import concourse.bacc as bacc
    from concourse.bass_utils import run_bass_kernel_spmd

    def a(name):
        return np.asarray(inputs[name])

    def parts(m):
        k = m.shape[0] // P
        return m.reshape(k, P, -1).transpose(1, 0, 2).reshape(P, -1)

    def chan(v):
        return v.reshape(-1, P).T

    def rows(v):
        return np.broadcast_to(v.reshape(1, -1), (P, v.size))

    def half(m):
        out = np.zeros((P, m.shape[1]), np.float32)
        out[:m.shape[0]] = m
        return out

    i = np.arange(P)
    wqkv, bqkv = a("L3_xattn_W_qkv"), a("L3_xattn_b_qkv")
    vals = {
        "ident": np.eye(P, dtype=np.float32),
        "wk0": parts(a("L0_xattn_Wk")), "wv0": parts(a("L0_xattn_Wv")),
        "wk1": parts(a("L1_xattn_W_k")), "wv1": parts(a("L1_xattn_W_v")),
        "wk2": parts(a("L2_xattn_Wk")), "wv2": parts(a("L2_xattn_Wv")),
        "wk3": parts(wqkv[D:2 * D].T), "wv3": parts(wqkv[2 * D:].T),
        "kvg2": chan(a("L2_xattn_kv_norm_g")), "kvb2": chan(a("L2_xattn_kv_norm_b")),
        "g31": chan(a("L3_xattn_g1")), "b31": chan(a("L3_xattn_beta1")),
        "bk3": chan(bqkv[D:2 * D]), "bv3": rows(bqkv[2 * D:]),
        "tri_le": (i[:, None] <= i[None, :]).astype(np.float32),
        "tri_gt": (i[:, None] > i[None, :]).astype(np.float32),
        "ones": np.ones((P, P), np.float32),
        "inw": parts(a("L0_xattn_in_proj_w")), "mnorm": chan(a("L0_xattn_m_norm_w")),
        "gnorm": chan(a("L0_xattn_gnorm_w")),
        "convw": parts(a("L0_xattn_conv_w")), "convb": chan(a("L0_xattn_conv_b")),
        "dtb": rows(a("L0_xattn_dt_bias")), "alog": rows(a("L0_xattn_A_log")), "dskip": rows(a("L0_xattn_D_skip")),
        "outw": parts(a("L0_xattn_out_proj_w")),
        "wq0": parts(a("L0_xattn_Wq")), "wo0": parts(a("L0_xattn_Wo")),
        "lng0": chan(a("L0_xattn_ca_ln_w")), "lnb0": chan(a("L0_xattn_ca_ln_b")),
        "wq1": parts(a("L1_xattn_W_q")), "wo1": parts(a("L1_xattn_W_o")),
        "w1": parts(a("L1_xattn_w1").T), "w2": parts(a("L1_xattn_w2").T),
        "b1": chan(a("L1_xattn_b1")), "b2": rows(a("L1_xattn_b2")),
        "wq2": parts(a("L2_xattn_Wq")), "wo2": parts(a("L2_xattn_Wo")),
        "qg2": chan(a("L2_xattn_q_norm_g")), "qb2": chan(a("L2_xattn_q_norm_b")), "bo2": rows(a("L2_xattn_bo")),
        "wq3": parts(wqkv[:D].T), "wo3": parts(a("L3_xattn_W_o").T), "bq3": chan(bqkv[:D]),
        "bo3": rows(a("L3_xattn_b_o")),
        "win3": parts(a("L3_xattn_W_in").T), "bin3": chan(a("L3_xattn_b_in")), "bmat3": parts(a("L3_xattn_Bmat")),
        "g32": chan(a("L3_xattn_g2")), "b32": chan(a("L3_xattn_beta2")),
        "at3": half(a("L3_xattn_A").T), "cmat3": half(a("L3_xattn_Cmat")), "wprog3": half(a("L3_xattn_W_prog").T),
        "bprog3": rows(a("L3_xattn_b_prog")),
        "hm32": (i[:, None] // 32 == np.arange(4)[None, :]).astype(np.float32),
        "hm16": (i[:, None] // 16 == np.arange(8)[None, :]).astype(np.float32),
        "neghalf": np.full((P, 1), -0.5, np.float32),
        "inv512": np.full((P, 1), 1.0 / T, np.float32),
        "pick": (i[:, None] == i[None, :] % NB).astype(np.float32),
    }
    pack = np.zeros((P, NPACK), np.float32)
    for name, (first, n) in PLAN.items():
        pack[:, first:first + n] = vals[name]

    mask = np.zeros((T, 4), np.uint8)
    mask[:, 0] = a("mask_1xS2_bf0").reshape(-1).view(np.uint8)

    nc = bacc.Bacc("TRN2", target_bir_lowering=False, num_devices=1)
    arrays, aps = {}, []
    for name, arr in (("x", a("x")), ("ctx", a("ctx_1024")), ("probs", a("ctxb_2048x64")),
                      ("mask", mask.view(np.int32).reshape(-1)), ("pack", pack)):
        arr = np.ascontiguousarray(arr)
        arrays[f"in_{name}"] = arr
        aps.append(nc.dram_tensor(f"in_{name}", arr.shape, mybir.dt.from_np(arr.dtype), kind="ExternalInput").ap())
    res = nc.dram_tensor("res_scratch", (T, NB, D), F32, kind="Internal").ap()
    out = nc.dram_tensor("out_0", (NB, T, D), F32, kind="ExternalOutput").ap()
    build(nc, *aps, res, out)
    r = run_bass_kernel_spmd(nc, [arrays], core_ids=[0])
    return r.results[0]["out_0"]
```

```python
from contextlib import ExitStack
from itertools import zip_longest

import numpy as np

import concourse.bass as bass
from concourse import mybir

F32 = mybir.dt.float32
BF16 = mybir.dt.bfloat16
I32 = mybir.dt.int32
ALU = mybir.AluOpType
ACT = mybir.ActivationFunctionType
AX = mybir.AxisListType.X

P = 128
NB = 4
T = 512
D = 256
KD = D // P
NCH = T // P
NT = NB * NCH
SIDES = 2
PAIRS = NB // SIDES
STEPS = P // PAIRS
EPS = 1e-5

DI = 512
NST = 128
HM = 8
HP = DI // HM
XBC = DI + 2 * NST
XG = XBC // P
CONV = 4

S3 = 64


class Layer:

    def __init__(self, name, heads, dh, kgroup, vcol):
        self.name, self.heads, self.dh = name, heads, dh
        self.width = heads * dh
        self.groups = self.width // P
        self.per_group = P // dh
        self.scale = float(dh) ** -0.5
        self.quads = heads // 4
        self.kgroup, self.vcol = kgroup, vcol


L0 = Layer("L0", 8, 32, 0, 0)
L1 = Layer("L1", 8, 16, 2, 256)
L2 = Layer("L2", 16, 16, 3, 384)
L3 = Layer("L3", 8, 32, 5, 640)
LAYERS = (L0, L1, L2, L3)
KG = sum(l.groups for l in LAYERS)
VW = sum(l.width for l in LAYERS)

STAGES = [(li, s) for li in range(len(LAYERS)) for s in range(SIDES)]
UNITS = [(i, LAYERS[li], s, h) for i, (li, s) in enumerate(STAGES) for h in range(LAYERS[li].heads)]
NU = len(UNITS)
QUADS = NU // 4
ENDS = {u + 1: unit[0] for u, unit in enumerate(UNITS) if u + 1 == NU or UNITS[u + 1][0] != unit[0]}
LAST_SLOT = NU + 4
NU_BEFORE = {st: min(u for u, unit in enumerate(UNITS) if unit[0] == i) for i, st in enumerate(STAGES)}


def value_products(u):
    work = []
    for k in range(3, NU, 4):
        if k + 1 in ENDS:
            if u == k + 3:
                work.append((k, range(NCH)))
        elif 0 <= u - (k + 3) < NCH:
            work.append((k, range(u - (k + 3), u - (k + 3) + 1)))
    return work


def step_of(u):
    if u >= NU or UNITS[u][1] is L1:
        return None
    return sum(UNITS[v][1] is not L1 for v in range(u))


def pack_plan():
    sizes = [
        ("ident", P),
        ("wk0", KD * 256), ("wv0", KD * 256), ("wk1", KD * 128), ("wv1", KD * 128),
        ("wk2", KD * 256), ("wv2", KD * 256), ("wk3", KD * 256), ("wv3", KD * 256),
        ("wprog3", 256), ("bprog3", 256),
        ("kvg2", KD), ("kvb2", KD), ("g31", KD), ("b31", KD), ("bk3", KD), ("bv3", 256),
        ("tri_le", P), ("tri_gt", P), ("ones", P),
        ("inw", KD * 1288), ("mnorm", KD), ("gnorm", 4), ("convw", XG * CONV), ("convb", XG),
        ("dtb", HM), ("alog", HM), ("dskip", HM), ("outw", 4 * 256),
        ("wq0", KD * 256), ("wo0", KD * 256), ("lng0", KD), ("lnb0", KD),
        ("wq1", KD * 128), ("wo1", 512), ("w1", KD * 256), ("w2", KD * 256), ("b1", KD), ("b2", 256),
        ("wq2", KD * 256), ("wo2", 4 * 256), ("qg2", KD), ("qb2", KD), ("bo2", 256),
        ("wq3", KD * 256), ("wo3", KD * 256), ("bq3", KD), ("bo3", 256),
        ("win3", KD * 256), ("bin3", KD), ("bmat3", KD * S3), ("g32", KD), ("b32", KD),
        ("at3", S3), ("cmat3", 256),
        ("hm32", 4), ("hm16", 8), ("neghalf", 1), ("inv512", 1), ("pickb", NB * P),
    ]
    plan, at = {}, 0
    for name, n in sizes:
        plan[name] = (at, n)
        at += n
    return plan, at


PLAN, NPACK = pack_plan()
CUTS = [0, PLAN["tri_le"][0], PLAN["wq0"][0], NPACK]


PER_SIDE = {"m_conv": CONV - 1, "p_chain": 19}
PER_TURN = {"cin": 16, "c_taken": 1, "c_used": 1, "x_in": 16, "x_taken": 1, "tile_done": 1,
            "c_st0": 32, "c_st1": 32,
            "kv_in0": 64, "kv_in1": 64, "kv_in2": 64, "kv_in3": 64, "kv_used": len(STAGES),
            "u_qm": NU, "u_s": NU, "u_mx": NU, "u_exp": NU, "u_tp": NU, "u_ev": NU, "u_pv": QUADS,
            "r_z": STEPS, "r_th": STEPS, "r_r": STEPS, "r_ss": 1, "r_last": 1,
            "e_z": STEPS, "e_th": STEPS, "e_r": STEPS, "e_ss": 1, "e_last": 1, "e_done": 1,
            "o_ss": NB, "o_mm": NB, "o_row": NB, "o_out": 16 * NB, "o_done": 1}
NORM_STEPS = ("bn", "ag", "ve", "rs", "nrm")
NORMS = ("L0", "L2", "L3", "u")
RESIDUAL = ("x2", "x3", "x4", "x5", "x6", "x7", "x8")


def counted(name, s):
    who, _, step = name.partition("_")
    if name in PER_TURN:
        return name, PER_TURN[name], 0
    if step.removeprefix("n_") in NORM_STEPS and who in NORMS:
        return f"norm_{step.removeprefix('n_')}", SIDES * len(NORMS), SIDES * NORMS.index(who) + s
    if who in ("L0", "L1", "L2", "L3") and step not in ("pre", "gelu"):
        return f"layer_{step}", len(STAGES), STAGES.index((int(who[1]), s))
    if name in RESIDUAL:
        group = next(g for g in (("x2",), ("x3", "x4", "x5"), ("x6",), ("x7", "x8")) if name in g)
        before = RESIDUAL.index(group[0])
        return "residual", SIDES * len(RESIDUAL), SIDES * before + s * len(group) + group.index(name)
    per = PER_SIDE.get(name, 1)
    return name, SIDES * per, s * per


class Turn:

    def __init__(self, eng, pers, loop):
        self.eng = eng
        self.regs = {p: eng.alloc_register(name=f"{loop}_turn_x{p}") for p in sorted(set(pers))}
        self.sum = eng.alloc_register(name=f"{loop}_sum")
        for r in self.regs.values():
            eng.reg_mov(r, 1)

    def value(self, per, n):
        if n == 1:
            return self.regs[per]
        self.eng.reg_add(self.sum, self.regs[per], n - 1)
        return self.sum

    def end(self):
        for p, r in self.regs.items():
            self.eng.reg_add(r, r, p)


def steps_after(li):
    step = {}
    if li >= 0:
        step.update(rd=2, rdT=4, rdb=5, on=7, wo=8, add=9)
    step.update({-1: dict(stats=1, nrm=3, tp=4), 0: dict(tp=10),
                 1: dict(f_tp=10, f_xT=11, f_h=12, f_relu=13, f_o=14, stats=15, nrm=17, tp=18),
                 2: dict(gelu=11, stats=13, nrm=15, tp=16), 3: dict(stats=9, nrm=11, tp=12)}[li])
    tp = step["tp"]
    step.update(xT=tp + 1, q=tp + 2, qT=tp + 3, u_hT=tp + 3, u_u=tp + 4, u_out=tp + 5)
    return step


class Chain:

    def __init__(self, body):
        self.body = body
        self.step = next(body, None)

    def go_on(self, last):
        while self.step is not None and self.step <= last:
            self.step = next(self.body, None)

    def finish(self):
        self.go_on(1000)


def build(nc, x, ctx_in, probs, maskf, pack, kd, vd, out):
    with ExitStack() as stack:
        def sb(name, shape, dt=F32):
            return stack.enter_context(nc.sbuf_tensor(name, shape, dt))

        sems = {}

        def sem(name):
            name = counted(name, 0)[0]
            if name not in sems:
                sems[name] = stack.enter_context(nc.semaphore(name))
            return sems[name]

        def at(name, turn, s=0, n=1, apart=False):
            _, per, before = counted(name, s)
            value = turn.value(per, before + n)
            if apart:
                turn.eng.wait_ge(sem("par0"), 16)
            return sem(name), value

        W = sb("W", [P, NPACK])

        def w(name, parts=None):
            a, n = PLAN[name]
            v = W[:, a:a + n]
            return v if parts is None else v.rearrange("p (k n) -> p k n", k=parts)

        def col(name, i):
            a, n = PLAN[name]
            return W[:, a + i:a + i + 1]

        def wide(ap, n):
            return ap.unsqueeze(2).to_broadcast([P, ap.shape[1], n])

        Ks = [sb(f"K{i}", [P, KD, T]) for i in range(4)]
        Vs = [sb(f"V{i}", [P, NCH, D + 16]) for i in range(4)]
        RES = sb("RES", [P, NT, D])
        early = RES[0:1, :, :].rearrange("p a n -> p (a n)")
        m_row = early[:, 0:T]
        m_tmp = early[:, T:4 * T].rearrange("p (i n) -> p i n", i=3)
        m_part = early[:, 4 * T:6 * T].bitcast(BF16)[:, 0:3 * T].rearrange("p (i n) -> p i n", i=3)
        m_rows = sb("m_rows", [3, T], BF16)
        ones_b = sb("ones_b", [3, P], BF16)
        at2 = sb("at2", [S3, P])
        mod = sb("mod", [NB, D])
        pmT = sb("pmT", [S3, NB])
        negA = sb("negA", [P, HM])
        bq3 = sb("bq3", [P, KD])
        hconv = sb("hconv", [P, XG * CONV])
        hconvb = sb("hconvb", [P, XG])
        hist = sb("hist", [P, NB, XG, CONV - 1])
        Hst = sb("Hst", [P, NB, DI])
        UT = sb("UT", [S3, P + T + 1, NB])
        R2 = sb("R2", [S3, STEPS + 1, NB])
        th3 = sb("th3", [S3, NB])
        SS = sb("SS", [S3, P + T, NB])

        xin = sb("xin", [P, SIDES, D])
        xrow = [sb(f"xrow{s}", [P, D]) for s in range(SIDES)]
        nrm = [sb(f"nrm{s}", [P, D]) for s in range(SIDES)]
        st = [sb(f"st{s}", [P, 16]) for s in range(SIDES)]
        xT = [sb(f"xT{s}", [P, KD, P]) for s in range(SIDES)]
        qT = [sb(f"qT{s}", [P, KD, P]) for s in range(SIDES)]
        hT = sb("hT", [P, KD, P])
        orows = sb("orows", [P, D])
        qm = sb("qm", [P, 4, P])
        Pr = sb("Pr", [P, 3, T])
        PT = sb("PT", [P, 8, NCH, P])
        nmax = sb("nmax", [P, NU])
        den = sb("den", [P, NU])
        rden = sb("rden", [P, NU])
        rdw = sb("rdw", [P, 4 * P])
        rdb = sb("rdb", [P, 4 * P])
        oT = sb("oT", [P, 4, P])

        room1 = sb("room1", [P, XG * (3 * P + CONV - 1) + 3 * DI])
        PTf = PT[:, :, :, :].rearrange("p a k n -> p a (k n)")
        Prf = Pr[:, 0:2, :].rearrange("p i n -> p (i n)")

        class Room:
            def __init__(self, ap, big, seg, xr):
                self.ap, self.used = ap, 0
                self.xpad = self.take(XG * (P + CONV - 1)).rearrange("p (g n) -> p g n", g=XG)
                self.acc = self.take(XG * P).rearrange("p (g n) -> p g n", g=XG)
                self.th = self.take(XG * P).rearrange("p (g n) -> p g n", g=XG)
                self.y, self.y2, self.xdt = self.take(DI), self.take(DI), self.take(DI)
                self.zt = self.th.rearrange("p g n -> p (g n)")[:, 0:DI]
                self.dAm = big.rearrange("p (h n) -> p h n", h=HM)
                self.xw = big[:, DI:]
                self.uT = big[:, 0:DI].rearrange("p (k n) -> p k n", k=4)
                self.seg = seg.rearrange("p (h n) -> p h n", h=HM)
                self.xr = xr
                self.dts = sb(f"dts{len(rooms)}", [P, 14, HM])
                self.dec = sb(f"dec{len(rooms)}", [P, 3, HM])
                self.BG = sb(f"BG{len(rooms)}", [P, 2, P])

            def take(self, n):
                self.used += n
                return self.ap[:, self.used - n:self.used]

        rooms = []
        rooms.append(Room(W[:, PLAN["wk0"][0]:PLAN["kvg2"][0]], Prf, PTf[:, 0:2, :].rearrange("p a n -> p (a n)"),
                          PTf[:, 2, :]))
        rooms.append(Room(room1, PTf[:, 3:5, :].rearrange("p a n -> p (a n)"),
                          PTf[:, 5:7, :].rearrange("p a n -> p (a n)"), PTf[:, 7, :]))

        cT = [[PTf[:, 3 * s:3 * s + 3, :].rearrange("p a n -> p (a n)")[:, i * D:(i + 1) * D]
               .rearrange("p (k n) -> p k n", k=KD) for i in range(3)] for s in range(SIDES)]
        keep = PTf[:, 7, :]
        pb = Prf.rearrange("p (b k s) -> p b k s", b=NB, k=NCH)
        KS = [room1[:, s * KG * P:(s + 1) * KG * P].rearrange("p (g n) -> p g n", g=KG) for s in range(SIDES)]
        VS = [room1[:, SIDES * KG * P + s * VW:SIDES * KG * P + (s + 1) * VW] for s in range(SIDES)]

        ps = [stack.enter_context(nc.psum_tensor(f"ps{i}", [P, 512], F32)) for i in range(8)]
        bank = [ps[0:4], ps[4:8]]
        psS, psT, psO, psR = [ps[0], ps[1], ps[6]], ps[2:4], ps[4], ps[7]
        psAB = ps[5]
        psA, psB = psAB[:, 0:D], psAB[:, D:2 * D]
        ident = w("ident")

        block = stack.enter_context(nc.Block())

        PERS = (1, SIDES, SIDES * PER_SIDE["m_conv"], len(STAGES), SIDES * len(RESIDUAL), 64, NU, QUADS, STEPS, 2 * PER_SIDE["p_chain"])

        def turns(eng, body, pers, loop, outer, inner=1):
            t = Turn(eng, pers, loop)
            with eng.Fori(0, outer) as c:
                if inner == 1:
                    body(t, c)
                    t.end()
                else:
                    with eng.Fori(0, inner) as b:
                        body(t, c, b)
                        t.end()

        def context(eng, body, pers=()):
            turns(eng, body, (1, 2) + pers, "context", NB, NCH // SIDES)

        def tiles(eng, body, pers=PERS):
            turns(eng, body, pers, "tiles", NCH, PAIRS)

        def side_by_side(first, second):
            for _ in zip_longest(first, second):
                pass

        @block.sync
        def _(sp):
            for i in range(3):
                sp.dma_start(W[:, CUTS[i]:CUTS[i + 1]], pack[:, CUTS[i]:CUTS[i + 1]]).then_inc(sem(f"par{i}"), 16)
            sp.wait_ge(sem("mask_parts"), 6)
            for i in range(3):
                sp.dma_start(m_rows[i:i + 1, :], m_part[0:1, i, :]).then_inc(sem("mask_rows"), 16)

            def ctx_pair(t, b, kp):
                for s in range(SIDES):
                    sp.wait_ge(*at("c_dve", t, s))
                    sp.dma_start(kd[b, :, :, bass.ts(kp * SIDES + s, P)], KS[s][:, :, :]).then_inc(sem(f"c_st{s}"), 16)
                    sp.dma_start(vd[b, :, bass.ds(kp * SIDES + s, 1), :].squeeze(1), VS[s]).then_inc(sem(f"c_st{s}"), 16)

            context(sp, ctx_pair)
            for s in range(SIDES):
                sp.wait_ge(sem(f"c_st{s}"), 32 * (NT // SIDES) + 1)

            def tile(t, c, bp):
                sp.wait_ge(*at("x_taken", t))
                sp.dma_start(xin[:, :, :], x[bass.ds(bp * SIDES, SIDES), bass.ts(c, P), :]
                             .rearrange("b p d -> p b d")).then_inc(sem("x_in"), 16)
                for i, (li, s) in enumerate(STAGES):
                    l = LAYERS[li]
                    sp.wait_ge(*at("kv_used", t, n=i + 1))
                    sp.dma_start(Ks[i % 4][:, 0:l.groups, :],
                                 kd[bass.ds(bp * SIDES + s, 1), :, l.kgroup:l.kgroup + l.groups, :]
                                 .squeeze(0)).then_inc(sem(f"kv_in{i % 4}"), 16)
                    sp.dma_start(Vs[i % 4][:, :, 0:l.width],
                                 vd[bass.ds(bp * SIDES + s, 1), :, :, l.vcol:l.vcol + l.width]
                                 .squeeze(0)).then_inc(sem(f"kv_in{i % 4}"), 16)

            tiles(sp, tile, (1, 8))

            def output(t, c):
                for b in range(NB):
                    sp.wait_ge(*at("o_row", t, n=b + 1))
                    sp.dma_start(out[b, bass.ts(c, P), :], RES[:, bass.ds(c * NB + b, 1), :].squeeze(1)
                                 ).then_inc(sem("o_out"), 16)

            turns(sp, output, (1, NB), "output", NCH)
            sp.wait_ge(sem("o_out"), 16 * NT)

        @block.gpsimd
        def _(pool):
            pool.dma_start(keep.bitcast(I32), maskf.partition_broadcast(P)).then_inc(sem("mask_in"), 16)
            pool.dma_start(m_row[:, :].bitcast(I32), maskf.rearrange("(a n) -> a n", a=1)).then_inc(sem("mask_in"), 16)
            pool.dma_start(pb, probs.rearrange("b (k p) s -> p b k s", p=P)).then_inc(sem("probs_in"), 16)
            pool.memset(hist[:, :, :, :], 0.0)
            pool.memset(Hst[:, :, :], 0.0)
            pool.memset(UT[:, 0:P + 1, :], 0.0)
            pool.memset(R2[:, 0, :], 0.0)
            for v in Vs:
                pool.memset(v[:, :, P:], 0.0)
            pool.memset(ones_b[:, :], 1.0).then_inc(sem("zeroed"), 1)

            def root(name, k, t, s):
                pool.wait_ge(*at(f"{name}_ve", t, s))
                nc.gpsimd.tensor_tensor(st[s][:, k + 9:k + 10], st[s][:, k + 8:k + 9], w("neghalf"),
                                        ALU.pow).then_inc(sem(f"{name}_rs"), 1)

            pool.wait_ge(sem("par2"), 16)

            def ctx_pair(t, b, kp):
                pool.wait_ge(*at("c_taken", t))
                pool.dma_start(xin[:, :, :], ctx_in[b, bass.ts(kp, SIDES * P), :].rearrange("(s p) d -> p s d", s=SIDES)
                               ).then_inc(sem("cin"), 16)
                for s in range(SIDES):
                    root("c", 0, t, s)

            context(pool, ctx_pair)

            def mamba(t, s, bp):
                r, b = rooms[s], bp * SIDES + s
                d = r.dts
                nc.gpsimd.tensor_copy(r.xpad[:, :, 0:CONV - 1], hist[:, bass.ds(b, 1), :, :].squeeze(1)
                                      ).then_inc(sem("m_hist"), 1)
                root("m1", 0, t, s)
                for _ in range(7):
                    yield
                pool.wait_ge(*at("m_r", t, s))
                nc.gpsimd.tensor_tensor(d[:, 6, :], d[:, 5, :], d[:, 5, :], ALU.mult).then_inc(sem("p_chain"), 1)
                n = 1
                pool.wait_ge(*at("p_chain", t, s, n, apart=True))
                nc.gpsimd.tensor_scalar(d[:, 7, :], d[:, 6, :], 1.0 / 19, 1.0 / 17, ALU.mult,
                                        ALU.add).then_inc(sem("p_chain"), 1)
                for q in (15, 13, 11, 9, 7, 5, 3, 1):
                    n += 1
                    pool.wait_ge(*at("p_chain", t, s, n))
                    nc.gpsimd.tensor_tensor(d[:, 8, :], d[:, 7, :], d[:, 6, :], ALU.mult).then_inc(sem("p_chain"), 1)
                    n += 1
                    pool.wait_ge(*at("p_chain", t, s, n, apart=True))
                    nc.gpsimd.tensor_scalar(d[:, 7, :], d[:, 8, :], 1.0 / q, None, ALU.add).then_inc(sem("p_chain"), 1)
                n += 1
                pool.wait_ge(*at("p_chain", t, s, n))
                nc.gpsimd.tensor_tensor(d[:, 8, :], d[:, 7, :], d[:, 5, :], ALU.mult).then_inc(sem("p_chain"), 1)
                n += 1
                assert n == PER_SIDE["p_chain"]
                pool.wait_ge(*at("p_chain", t, s, n, apart=True))
                nc.gpsimd.tensor_scalar(d[:, 9, :], d[:, 8, :], 2.0, None, ALU.mult).then_inc(sem("m_log"), 1)
                pool.wait_ge(*at("m_log", t, s))
                nc.gpsimd.tensor_tensor(d[:, 10, :], d[:, 9, :], d[:, 1, :], ALU.add).then_inc(sem("m_dt"), 1)
                pool.wait_ge(*at("m_dt", t, s))
                nc.gpsimd.tensor_tensor(d[:, 11, :], d[:, 10, :], negA[:, :], ALU.mult).then_inc(sem("m_dA"), 1)
                pool.wait_ge(*at("m_xbc", t, s, apart=True))
                nc.gpsimd.tensor_copy(hist[:, bass.ds(b, 1), :, :].squeeze(1), r.xpad[:, :, P:P + CONV - 1]
                                      ).then_inc(sem("m_hist2"), 1)
                for _ in range(4):
                    yield
                pool.wait_ge(*at("m_xr", t, s))
                nc.gpsimd.tensor_tensor(r.y2.rearrange("p (h n) -> p h n", h=HM),
                                        r.xr.rearrange("p (h n) -> p h n", h=HM),
                                        wide(w("dskip"), HP), ALU.mult).then_inc(sem("m_xD"), 1)
                pool.wait_ge(*at("m_xdt", t, s))
                pool.wait_ge(*at("m_dec", t, s))
                nc.gpsimd.tensor_tensor(r.xw.rearrange("p (h n) -> p h n", h=HM),
                                        r.xdt.rearrange("p (h n) -> p h n", h=HM),
                                        wide(r.dec[:, 1, :], HP), ALU.mult).then_inc(sem("m_xw"), 1)
                yield
                yield
                root("m2", 2, t, s)

            def between(t, li, s):
                if li != 0:
                    yield steps_after(li)["stats"]
                    root({-1: "L0_n", 1: "L2_n", 2: "L3_n", 3: "u"}[li], 0, t, s)

            def tile(t, c, bp):
                pool.wait_ge(*at("tile_done", t))
                side_by_side(mamba(t, 0, bp), mamba(t, 1, bp))
                root("L0_n", 0, t, 0)
                chain, since = Chain(between(t, -1, 1)), 0

                def mask_query(u):
                    i, l, s, h = UNITS[u]
                    if h == 0:
                        pool.wait_ge(*at(f"{l.name}_qT", t, s, apart=True))
                    if u >= 4:
                        pool.wait_ge(*at("u_s", t, n=u - 3, apart=True))
                    nc.gpsimd.tensor_scalar(qm[:, u % 4, :], qT[s][:, h // l.per_group, :],
                                            col(f"hm{l.dh}", h % l.per_group), None,
                                            ALU.mult).then_inc(sem("u_qm"), 1)

                for u in range(3):
                    mask_query(u)
                for u in range(LAST_SLOT):
                    if u in ENDS:
                        chain, since = Chain(between(t, *STAGES[ENDS[u]])), u
                    if u + 3 in ENDS:
                        chain.finish()
                    if u + 3 < NU:
                        mask_query(u + 3)
                    chain.go_on(2 * (u - since) + 1)
                chain.finish()

            tiles(pool, tile)

        @block.scalar
        def _(act):
            for i in range(3):
                act.wait_ge(sem(f"par{i}"), 16)
            nc.scalar.activation(rooms[0].dts[:, 0, :], w("alog"), ACT.Exp).then_inc(sem("expA"), 1)

            def ctx_tile(t, s):
                X = bank[s]
                yield
                yield
                act.wait_ge(*at("c_tpn", t, s))
                nc.scalar.copy(cT[s][0].rearrange("p k n -> p (k n)"), X[0][:, 0:D])
                for i, (g, bb) in ((1, ("kvg2", "kvb2")), (2, ("g31", "b31"))):
                    for kk in range(KD):
                        ins = nc.scalar.activation(cT[s][i][:, kk, :], X[0][:, D + kk * P:D + (kk + 1) * P], ACT.Identity,
                                                   bias=col(bb, kk), scale=col(g, kk))
                ins.then_inc(sem("c_ev"), 1)
                yield
                yield
                act.wait_ge(*at("c_k23", t, s))
                act.wait_ge(*at(f"c_st{s}", t, n=1))
                nc.scalar.copy(KS[s][:, 3:5, :], X[2][:, 0:D].rearrange("p (g n) -> p g n", g=2))
                for g in range(2):
                    nc.scalar.activation(KS[s][:, 5 + g, :], X[2][:, D + g * P:D + (g + 1) * P],
                                         ACT.Identity, bias=col("bk3", g))
                act.wait_ge(*at("c_v01", t, s))
                nc.scalar.copy(VS[s][:, 0:384], X[3][:, 0:384]).then_inc(sem("c_act"), 1)

            act.wait_ge(sem("mod_pm"), 1)
            nc.scalar.copy(pmT[:, :], ps[1][0:S3, 0:NB]).then_inc(sem("mod_pmT"), 1)
            act.wait_ge(sem("mod_done"), 1)
            context(act, lambda t, b, kp: side_by_side(ctx_tile(t, 0), ctx_tile(t, 1)), (32,))

            def evac_xT(name, t, s, src, g=None, b=None):
                act.wait_ge(*at(f"{name}_xtp", t, s))
                if g is None:
                    nc.scalar.copy(xT[s][:, :, :].rearrange("p k n -> p (k n)"), src[:, 0:D]).then_inc(sem(f"{name}_xT"), 1)
                else:
                    for kk in range(KD):
                        ins = nc.scalar.activation(xT[s][:, kk, :], src[:, kk * P:(kk + 1) * P], ACT.Identity,
                                                   bias=col(b, kk) if b else 0.0, scale=col(g, kk))
                    ins.then_inc(sem(f"{name}_xT"), 1)

            def mamba(t, s):
                r, X = rooms[s], bank[s]
                yield
                yield
                evac_xT("m1", t, s, X[0], "mnorm")
                yield
                yield
                act.wait_ge(*at("m_pa", t, s))
                nc.scalar.copy(r.xpad[:, 0:4, CONV - 1:], X[1][:, :].rearrange("p (g n) -> p g n", g=4))
                act.wait_ge(*at("m_pb", t, s))
                nc.scalar.copy(r.xpad[:, 4:6, CONV - 1:],
                               X[2][:, 0:256].rearrange("p (g n) -> p g n", g=2)).then_inc(sem("m_xbc"), 1)
                yield
                act.wait_ge(*at("m_v", t, s))
                nc.scalar.activation(r.dts[:, 3, :], r.dts[:, 2, :], ACT.Exp).then_inc(sem("m_e"), 1)
                yield
                yield
                yield
                act.wait_ge(*at("m_conv", t, s, CONV - 1))
                nc.scalar.activation(r.th.rearrange("p g n -> p (g n)"),
                                     r.acc.rearrange("p g n -> p (g n)"), ACT.Tanh).then_inc(sem("m_th"), 1)
                yield
                act.wait_ge(*at("m_xc", t, s))
                act.wait_ge(*at("m_z", t, s))
                nc.scalar.activation(r.zt, X[3][:, :], ACT.Tanh, scale=0.5).then_inc(sem("m_zt"), 1)
                yield
                act.wait_ge(*at("m_seg", t, s))
                for i in range(2):
                    nc.scalar.activation(r.seg[:, 4 * i:4 * i + 4, :].rearrange("p g n -> p (g n)"), X[1 + i][:, :], ACT.Exp)
                nc.scalar.activation(r.dec[:, :, :].rearrange("p g n -> p (g n)"), X[0][:, 256:256 + 3 * HM],
                                     ACT.Exp).then_inc(sem("m_dec"), 1)
                yield
                act.wait_ge(*at("m_rows", t, s))
                nc.scalar.copy(r.xr, X[3][:, :]).then_inc(sem("m_xr"), 1)
                nc.scalar.copy(r.BG[:, 0, :], X[0][:, 0:NST]).then_inc(sem("m_Br"), 1)
                yield
                yield
                yield
                act.wait_ge(*at("m_utp", t, s))
                for k in range(4):
                    ins = nc.scalar.activation(r.uT[:, k, :], X[3][:, k * P:(k + 1) * P], ACT.Copy,
                                               scale=col("gnorm", k))
                ins.then_inc(sem("m_uT"), 1)

            def between(t, li, s):
                step = steps_after(li)
                if li >= 0:
                    l = LAYERS[li]
                    yield step["rdb"]
                    act.wait_ge(*at(f"{l.name}_rdT", t, s))
                    nc.scalar.copy(rdb[:, 0:l.quads * P], psAB[:, 0:l.quads * P]).then_inc(sem(f"{l.name}_rdb"), 1)
                if li == 1:
                    yield step["f_xT"]
                    evac_xT("f", t, s, psA)
                    yield step["f_relu"]
                    act.wait_ge(*at("f_h", t, s))
                    for g in range(KD):
                        ins = nc.scalar.activation(hT[:, g, :], psB[:, g * P:(g + 1) * P], ACT.Relu, bias=col("b1", g))
                    ins.then_inc(sem("f_hT"), 1)
                if li == 2:
                    yield step["gelu"]
                    act.wait_ge(*at("L2_pre", t, s))
                    nc.scalar.activation(nrm[s][:, :], orows[:, :], ACT.Gelu).then_inc(sem("L2_gelu"), 1)
                yield step["xT"]
                if li == 3:
                    evac_xT("u", t, s, psA, "g32", "b32")
                    yield step["u_hT"]
                    act.wait_ge(*at("u_h", t, s))
                    for g in range(KD):
                        ins = nc.scalar.activation(hT[:, g, :], psB[:, g * P:(g + 1) * P], ACT.Identity, bias=col("bin3", g))
                    ins.then_inc(sem("u_hT"), 1)
                    yield step["u_out"]
                    c, b = where
                    act.wait_ge(*at("u_u", t, s))
                    nc.scalar.copy(UT[:, bass.ds(c * P + P + 1, P), bass.ds(b * SIDES + s, 1)],
                                   psA[0:S3, 0:P].unsqueeze(2)).then_inc(sem("u_out"), 1)
                    return
                l = LAYERS[li + 1]
                evac_xT(l.name, t, s, psA, *{0: ("lng0", "lnb0"), 1: (), 2: ("qg2", "qb2"), 3: ("g31", "b31")}[li + 1])
                yield step["qT"]
                act.wait_ge(*at(f"{l.name}_q", t, s))
                for gi in range(l.groups):
                    ins = nc.scalar.activation(qT[s][:, gi, :], psB[:, gi * P:(gi + 1) * P], ACT.Identity,
                                               bias=bq3[:, gi:gi + 1] if l is L3 else 0.0, scale=l.scale)
                ins.then_inc(sem(f"{l.name}_qT"), 1)

            where = None

            def tanh_step(t, j, pre):
                act.wait_ge(*at(f"{pre}_z", t, n=j + 1))
                if j:
                    act.wait_ge(*at(f"{pre}_r", t, n=j))
                nc.scalar.activation(th3[:, :], psR[0:S3, NB * j:NB * (j + 1)], ACT.Tanh,
                                     scale=0.5).then_inc(sem(f"{pre}_th"), 1)

            def tile(t, c, bp):
                nonlocal where
                where = (c, bp)
                act.wait_ge(*at("tile_done", t))
                side_by_side(mamba(t, 0), mamba(t, 1))
                Chain(between(t, -1, 0)).finish()
                chain, since = Chain(between(t, -1, 1)), 0
                tanh_step(t, 0, "r")
                for u in range(LAST_SLOT):
                    if u in ENDS:
                        chain, since = Chain(between(t, *STAGES[ENDS[u]])), u
                    chain.go_on(2 * (u - since) + 1)
                    if u < NU:
                        act.wait_ge(*at("u_mx", t, n=u + 1))
                        if u >= 3:
                            act.wait_ge(*at("u_tp", t, n=u - 2))
                        nc.scalar.activation(Pr[:, u % 3, :], psS[u % 3][:, :], ACT.Exp, bias=nmax[:, u:u + 1],
                                             accum_out=den[:, u:u + 1]).then_inc(sem("u_exp"), 1)
                    j = step_of(u + 1)
                    if j is not None and u + 1 not in ENDS:
                        tanh_step(t, j, "r")
                    k = u - 2
                    if 0 <= k < NU and k % 2 == 0:
                        act.wait_ge(*at("u_tp", t, n=k + 1))
                        if k >= 8:
                            act.wait_ge(*at("u_pv", t, n=k // 4 - 1))
                        if k:
                            act.wait_ge(*at("u_ev", t, n=k))
                        nc.scalar.copy(PT[:, k % 8, :, :].rearrange("p a n -> p (a n)"),
                                       psT[k % 2][:, :]).then_inc(sem("u_ev"), 1)
                    if u + 1 in ENDS or u + 1 == LAST_SLOT:
                        chain.finish()
                        if j is not None and u + 1 in ENDS:
                            tanh_step(t, j, "r")

            tiles(act, tile)

            def last_steps(t, k):
                for j in range(STEPS):
                    tanh_step(t, j, "e")

            turns(act, last_steps, (1, STEPS), "last", PAIRS)

            def output(t, c):
                act.wait_ge(*at("o_done", t))
                for b in range(NB):
                    nc.scalar.copy(qT[b // 2][0:S3, b % 2, :], SS[:, bass.ds(c * P + P, P), b]).then_inc(sem("o_ss"), 1)

            turns(act, output, (1, NB), "output", NCH)

        @block.vector
        def _(dve):
            for i in range(3):
                dve.wait_ge(sem(f"par{i}"), 16)
            dve.wait_ge(sem("mask_in"), 32)
            dve.wait_ge(sem("expA"), 1)
            nc.vector.tensor_scalar(keep, keep.bitcast(I32), -1.0, 1.0, ALU.mult, ALU.add)
            nc.vector.tensor_scalar(negA[:, :], rooms[0].dts[:, 0, :], -1.0, None, ALU.mult)
            nc.vector.tensor_scalar(at2[:, :], W[0:S3, PLAN["at3"][0]:PLAN["at3"][0] + P], 0.5, None, ALU.mult)
            nc.vector.tensor_scalar(bq3[:, :], w("bq3"), L3.scale, None, ALU.mult)
            nc.vector.tensor_scalar(hconv[:, :], w("convw"), 0.5, None, ALU.mult)
            nc.vector.tensor_scalar(hconvb[:, :], w("convb"), 0.5, None, ALU.mult)
            nc.vector.tensor_scalar(m_tmp[:, 0, :], m_row[:, :].bitcast(I32), -1e9, None, ALU.mult).then_inc(sem("mask_parts"), 1)
            dve.wait_ge(sem("mask_parts"), 1)
            nc.vector.tensor_copy(m_part[:, 0, :], m_tmp[:, 0, :]).then_inc(sem("mask_parts"), 1)
            dve.wait_ge(sem("mask_parts"), 2)
            nc.vector.tensor_tensor(m_tmp[:, 1, :], m_tmp[:, 0, :], m_part[:, 0, :], ALU.subtract).then_inc(sem("mask_parts"), 1)
            dve.wait_ge(sem("mask_parts"), 3)
            nc.vector.tensor_copy(m_part[:, 1, :], m_tmp[:, 1, :]).then_inc(sem("mask_parts"), 1)
            dve.wait_ge(sem("mask_parts"), 4)
            nc.vector.tensor_tensor(m_tmp[:, 2, :], m_tmp[:, 1, :], m_part[:, 1, :], ALU.subtract).then_inc(sem("mask_parts"), 1)
            dve.wait_ge(sem("mask_parts"), 5)
            nc.vector.tensor_copy(m_part[:, 2, :], m_tmp[:, 2, :]).then_inc(sem("mask_parts"), 1)
            dve.wait_ge(sem("mod_mm"), 1)
            nc.vector.tensor_tensor(mod[:, :], ps[0][0:NB, 0:D], w("bprog3")[0:NB, :], ALU.add).then_inc(sem("mod_done"), 1)
            nc.vector.memset(st[0][:, 10:11], 0.0).then_inc(sem("c_used"), 1)
            nc.vector.memset(st[0][:, 11:12], 0.0).then_inc(sem("c_taken"), 1)
            for s in range(SIDES):
                nc.vector.memset(st[s][:, 12:13], 0.0).then_inc(sem(f"c_st{s}"), 1)

            def norm_stats(name, t, s, src):
                nc.vector.bn_stats(st[s][:, 0:6], src).then_inc(sem(f"{name}_bn"), 1)
                dve.wait_ge(*at(f"{name}_bn", t, s, apart=True))
                nc.vector.bn_aggr(st[s][:, 6:8], st[s][:, 0:6]).then_inc(sem(f"{name}_ag"), 1)
                dve.wait_ge(*at(f"{name}_ag", t, s))
                nc.vector.tensor_scalar(st[s][:, 8:9], st[s][:, 7:8], EPS, None, ALU.add).then_inc(sem(f"{name}_ve"), 1)

            def norm_rows(name, t, s, src):
                dve.wait_ge(*at(f"{name}_rs", t, s))
                nc.vector.tensor_scalar(nrm[s][:, :], src, st[s][:, 6:7], st[s][:, 9:10], ALU.subtract,
                                        ALU.mult).then_inc(sem(f"{name}_nrm"), 1)

            def ctx_tile(t, s):
                X = bank[s]
                norm_stats("c", t, s, xin[:, s, :])
                yield
                norm_rows("c", t, s, xin[:, s, :])
                yield
                if s == 1:
                    dve.wait_ge(*at("c_tpx", t, 1))
                    dve.wait_ge(*at("c_nrm", t, 1))
                    nc.vector.memset(st[0][:, 11:12], 0.0).then_inc(sem("c_taken"), 1)
                yield
                yield
                dve.wait_ge(*at("c_k01", t, s))
                dve.wait_ge(*at(f"c_st{s}", t, n=1))
                nc.vector.tensor_tensor(KS[s][:, 0:2, :], X[1][:, 0:256].rearrange("p (g n) -> p g n", g=2),
                                        keep_of(t).unsqueeze(1).to_broadcast([P, 2, P]) if s == 0 else
                                        keep_of(t, 1).unsqueeze(1).to_broadcast([P, 2, P]), ALU.mult)
                nc.vector.tensor_copy(KS[s][:, 2, :], X[1][:, 256:384])
                dve.wait_ge(*at("c_v23", t, s))
                nc.vector.tensor_copy(VS[s][:, 384:640], X[0][:, 0:256])
                dve.wait_ge(*at("c_act", t, s))
                nc.vector.tensor_tensor(VS[s][:, 640:896], X[0][:, 256:512], w("bv3"), ALU.add).then_inc(sem("c_dve"), 1)

            pair_at = None

            def keep_of(t, s=0):
                return keep[:, bass.ts(pair_at * SIDES + s, P)]

            def ctx_pair(t, b, kp):
                nonlocal pair_at
                pair_at = kp
                dve.wait_ge(*at("c_used", t))
                dve.wait_ge(*at("cin", t, n=16))
                side_by_side(ctx_tile(t, 0), ctx_tile(t, 1))
                dve.wait_ge(*at("c_dve", t, 1))
                nc.vector.memset(st[0][:, 10:11], 0.0).then_inc(sem("c_used"), 1)

            context(dve, ctx_pair, (16, 32))
            for s in range(SIDES):
                dve.wait_ge(sem(f"c_st{s}"), 32 * (NT // SIDES) + 1)
            dve.wait_ge(sem("c_used"), NT // SIDES + 1)
            nc.vector.memset(st[0][:, 10:11], 0.0).then_inc(sem("x_taken"), 1)
            nc.vector.memset(st[0][:, 11:12], 0.0).then_inc(sem("kv_used"), 4)
            nc.vector.memset(st[0][:, 12:13], 0.0).then_inc(sem("tile_done"), 1)

            def mamba(t, s, bp):
                r, X, b = rooms[s], bank[s], bp * SIDES + s
                d = r.dts
                hv = lambda a: a.rearrange("p (h n) -> p h n", h=HM)
                nc.vector.tensor_tensor_reduce(out=r.y[:, 0:D], in0=xin[:, s, :], in1=xin[:, s, :], scale=1.0, scalar=0.0,
                                               op0=ALU.mult, op1=ALU.add, accum_out=st[s][:, 7:8]).then_inc(sem("m1_ss"), 1)
                dve.wait_ge(*at("m1_ss", t, s))
                nc.vector.tensor_scalar(st[s][:, 8:9], st[s][:, 7:8], 1.0 / D, EPS, ALU.mult, ALU.add).then_inc(sem("m1_ve"), 1)
                yield
                dve.wait_ge(*at("m1_rs", t, s))
                nc.vector.tensor_scalar(nrm[s][:, :], xin[:, s, :], st[s][:, 9:10], None, ALU.mult).then_inc(sem("m1_nrm"), 1)
                for _ in range(4):
                    yield
                dve.wait_ge(*at("m_xbc", t, s))
                nc.vector.tensor_tensor(d[:, 0, :], X[2][:, 256:256 + HM], w("dtb"), ALU.add).then_inc(sem("m_v0"), 1)
                dve.wait_ge(*at("m_v0", t, s))
                nc.vector.tensor_scalar(d[:, 1, :], d[:, 0, :], 0.0, None, ALU.max).then_inc(sem("m_v1"), 1)
                dve.wait_ge(*at("m_v1", t, s))
                nc.vector.scalar_tensor_tensor(d[:, 2, :], d[:, 1, :], -2.0, d[:, 0, :], ALU.mult,
                                               ALU.add).then_inc(sem("m_v"), 1)
                dve.wait_ge(*at("m_hist", t, s))
                for k in range(CONV):
                    if k == 1:
                        dve.wait_ge(*at("m_conv0", t, s))
                    elif k:
                        dve.wait_ge(*at("m_conv", t, s, k - 1))
                    for g in range(XG):
                        src = r.xpad[:, g, k:k + P]
                        wk = hconv[:, g * CONV + k:g * CONV + k + 1]
                        if k == 0:
                            ins = nc.vector.tensor_scalar(r.acc[:, g, :], src, wk, hconvb[:, g:g + 1], ALU.mult, ALU.add)
                        else:
                            ins = nc.vector.scalar_tensor_tensor(r.acc[:, g, :], src, wk, r.acc[:, g, :], ALU.mult, ALU.add)
                    ins.then_inc(sem("m_conv" if k else "m_conv0"), 1)
                    if k == 0:
                        yield
                        dve.wait_ge(*at("m_e", t, s))
                        nc.vector.tensor_scalar(d[:, 4, :], d[:, 3, :], 2.0, None, ALU.add).then_inc(sem("m_e2"), 1)
                        dve.wait_ge(*at("m_e2", t, s))
                        nc.vector.reciprocal(d[:, 12, :], d[:, 4, :]).then_inc(sem("m_rc"), 1)
                        dve.wait_ge(*at("m_rc", t, s))
                        nc.vector.tensor_tensor(d[:, 5, :], d[:, 3, :], d[:, 12, :], ALU.mult).then_inc(sem("m_r"), 1)
                        yield
                yield
                dve.wait_ge(*at("m_th", t, s))
                nc.vector.scalar_tensor_tensor(r.acc.rearrange("p g n -> p (g n)"),
                                               r.th.rearrange("p g n -> p (g n)"), 1.0,
                                               r.acc.rearrange("p g n -> p (g n)"), ALU.add,
                                               ALU.mult).then_inc(sem("m_xc"), 1)
                yield
                dve.wait_ge(*at("m_dA", t, s))
                nc.vector.tensor_tensor(r.dAm, w("tri_le").unsqueeze(1).to_broadcast([P, HM, P]),
                                        wide(d[:, 11, :], P), ALU.mult).then_inc(sem("m_dAm"), 1)
                dve.wait_ge(*at("m_zt", t, s))
                nc.vector.scalar_tensor_tensor(r.zt, r.zt, 1.0, X[3][:, :], ALU.add,
                                               ALU.mult).then_inc(sem("m_zs"), 1)
                yield
                yield
                dve.wait_ge(*at("m_Br", t, s))
                nc.vector.tensor_tensor(r.BG[:, 1, :], X[0][:, P:2 * P], w("tri_le"), ALU.mult).then_inc(sem("m_GT"), 1)
                dve.wait_ge(*at("m_xr", t, s))
                dve.wait_ge(*at("m_dt", t, s))
                nc.vector.tensor_tensor(hv(r.xdt), hv(r.xr), wide(d[:, 10, :], HP), ALU.mult).then_inc(sem("m_xdt"), 1)
                dve.wait_ge(*at("m_GT", t, s))
                dve.wait_ge(*at("m_dec", t, s))
                nc.vector.tensor_tensor(r.seg, r.seg, r.BG[:, 1, :].unsqueeze(1).to_broadcast([P, HM, P]),
                                        ALU.mult).then_inc(sem("m_M"), 1)
                yield
                yield
                dve.wait_ge(*at("m_inter", t, s))
                nc.vector.tensor_tensor(hv(r.y), hv(X[1][:, :]), wide(r.dec[:, 0, :], HP), ALU.mult).then_inc(sem("m_y0"), 1)
                dve.wait_ge(*at("m_y0", t, s))
                dve.wait_ge(*at("m_intra", t, s))
                nc.vector.tensor_tensor(r.y, r.y, X[2][:, :], ALU.add).then_inc(sem("m_y1"), 1)
                dve.wait_ge(*at("m_y1", t, s))
                dve.wait_ge(*at("m_xD", t, s))
                nc.vector.tensor_tensor(r.y, r.y, r.y2, ALU.add).then_inc(sem("m_y2"), 1)
                dve.wait_ge(*at("m_y2", t, s))
                nc.vector.tensor_tensor(r.y, r.y, r.zt, ALU.mult).then_inc(sem("m_y3"), 1)
                dve.wait_ge(*at("m_y3", t, s))
                nc.vector.tensor_tensor_reduce(out=r.y2, in0=r.y, in1=r.y, scale=1.0, scalar=0.0,
                                               op0=ALU.mult, op1=ALU.add, accum_out=st[s][:, 12:13]).then_inc(sem("m2_ss"), 1)
                dve.wait_ge(*at("m2_ss", t, s))
                nc.vector.tensor_scalar(st[s][:, 10:11], st[s][:, 12:13], 0.25 / DI, EPS, ALU.mult, ALU.add).then_inc(sem("m2_ve"), 1)
                dve.wait_ge(*at("m_xw", t, s))
                nc.vector.tensor_tensor(hv(r.xdt), Hst[:, bass.ds(b, 1), :].rearrange("p a (h n) -> p (a h) n", h=HM),
                                        wide(r.dec[:, 2, :], HP), ALU.mult).then_inc(sem("m_Hd"), 1)
                dve.wait_ge(*at("m_Hd", t, s))
                dve.wait_ge(*at("m_state", t, s))
                nc.vector.tensor_tensor(Hst[:, bass.ds(b, 1), :], r.xdt.unsqueeze(1), X[3][:, :].unsqueeze(1),
                                        ALU.add).then_inc(sem("m_H"), 1)
                yield
                dve.wait_ge(*at("m2_rs", t, s))
                nc.vector.tensor_scalar(r.y, r.y, st[s][:, 11:12], 0.5, ALU.mult, ALU.mult).then_inc(sem("m_un"), 1)
                yield
                dve.wait_ge(*at("m_out", t, s))
                nc.vector.tensor_tensor(xrow[s][:, :], xin[:, s, :], X[0][:, 0:D], ALU.add).then_inc(sem("x1"), 1)

            def add_rows(name, t, s, src, out_name):
                dve.wait_ge(*at(name, t, s))
                nc.vector.tensor_tensor(xrow[s][:, :], xrow[s][:, :], src, ALU.add).then_inc(sem(out_name), 1)
                dve.wait_ge(*at(out_name, t, s))

            def between(t, li, s):
                step = steps_after(li)
                if li >= 0:
                    l = LAYERS[li]
                    u0 = NU_BEFORE[li, s]
                    yield step["rd"]
                    dve.wait_ge(*at("u_exp", t, n=u0 + l.heads))
                    nc.vector.reciprocal(rden[:, u0:u0 + l.heads], den[:, u0:u0 + l.heads]).then_inc(sem(f"{l.name}_rd"), 1)
                    dve.wait_ge(*at(f"{l.name}_rd", t, s))
                    nc.vector.tensor_copy(rdw[:, 0:l.heads * 32].rearrange("p (h n) -> p h n", h=l.heads),
                                          wide(rden[:, u0:u0 + l.heads], 32)).then_inc(sem(f"{l.name}_rdw"), 1)
                    yield step["on"]
                    dve.wait_ge(*at("u_pv", t, n=(u0 + l.heads) // 4))
                    dve.wait_ge(*at(f"{l.name}_rdb", t, s))
                    nc.vector.tensor_tensor(oT[:, 0:l.quads, :].rearrange("p a n -> p (a n)"), psO[:, 0:l.quads * P],
                                            rdb[:, 0:l.quads * P], ALU.mult).then_inc(sem(f"{l.name}_on"), 1)
                    yield step["add"]
                if li == -1:
                    yield step["stats"]
                    dve.wait_ge(*at("x1", t, s))
                if li == 0:
                    add_rows("L0_op", t, s, psB[:, 0:D], "x2")
                if li == 1:
                    add_rows("L1_op", t, s, psB[:, 0:D], "x3")
                    yield step["stats"]
                    add_rows("f_o", t, s, psA[:, 0:D], "x4")
                    nc.vector.tensor_tensor(xrow[s][:, :], xrow[s][:, :], w("b2"), ALU.add).then_inc(sem("x5"), 1)
                    dve.wait_ge(*at("x5", t, s))
                if li == 2:
                    dve.wait_ge(*at("L2_op", t, s))
                    nc.vector.tensor_tensor(orows[:, :], psB[:, 0:D], w("bo2"), ALU.add).then_inc(sem("L2_pre"), 1)
                    yield step["stats"]
                    add_rows("L2_gelu", t, s, nrm[s][:, :], "x6")
                if li == 3:
                    add_rows("L3_op", t, s, psB[:, 0:D], "x7")
                    nc.vector.tensor_tensor(xrow[s][:, :], xrow[s][:, :], w("bo3"), ALU.add).then_inc(sem("x8"), 1)
                    dve.wait_ge(*at("x8", t, s))
                if li != 0:
                    name = {-1: "L0_n", 1: "L2_n", 2: "L3_n", 3: "u"}[li]
                    norm_stats(name, t, s, xrow[s][:, :])
                    yield step["nrm"]
                    norm_rows(name, t, s, xrow[s][:, :])
                if li == 3:
                    c, bp = where
                    nc.vector.tensor_copy(RES[:, bass.ds(c * NB + bp * SIDES + s, 1), :], xrow[s][:, :].unsqueeze(1)
                                          ).then_inc(sem("res_kept"), 1)

            where = None

            def silu_step(t, j, pre):
                dve.wait_ge(*at(f"{pre}_th", t, n=j + 1))
                nc.vector.scalar_tensor_tensor(R2[:, j + 1, :], th3[:, :], 1.0, psR[0:S3, NB * j:NB * (j + 1)],
                                               ALU.add, ALU.mult).then_inc(sem(f"{pre}_r"), 1)

            def tile(t, c, bp):
                nonlocal where
                where = (c, bp)
                dve.wait_ge(*at("tile_done", t))
                dve.wait_ge(*at("x_in", t, n=16))
                side_by_side(mamba(t, 0, bp), mamba(t, 1, bp))
                dve.wait_ge(*at("x1", t, 1))
                nc.vector.memset(st[0][:, 13:14], 0.0).then_inc(sem("x_taken"), 1)
                Chain(between(t, -1, 0)).finish()
                chain, since = Chain(between(t, -1, 1)), 0
                silu_step(t, 0, "r")
                for u in range(LAST_SLOT):
                    if u in ENDS:
                        chain, since = Chain(between(t, *STAGES[ENDS[u]])), u
                    chain.go_on(2 * (u - since) + 1)
                    if u < NU:
                        dve.wait_ge(*at("u_s", t, n=u + 1))
                        nc.vector.tensor_reduce(nmax[:, u:u + 1], psS[u % 3][:, :], AX, ALU.max,
                                                negate=True).then_inc(sem("u_mx"), 1)
                    k = u - 2
                    if 0 <= k < NU and k % 2 == 1:
                        dve.wait_ge(*at("u_tp", t, n=k + 1))
                        if k >= 8:
                            dve.wait_ge(*at("u_pv", t, n=k // 4 - 1))
                        dve.wait_ge(*at("u_ev", t, n=k))
                        nc.vector.tensor_copy(PT[:, k % 8, :, :].rearrange("p a n -> p (a n)"),
                                              psT[k % 2][:, :]).then_inc(sem("u_ev"), 1)
                    j = step_of(u + 1)
                    if j is not None and u + 1 not in ENDS:
                        silu_step(t, j, "r")
                    if u + 1 in ENDS or u + 1 == LAST_SLOT:
                        chain.finish()
                        if j is not None and u + 1 in ENDS:
                            silu_step(t, j, "r")
                dve.wait_ge(*at("r_r", t, n=STEPS))
                g = (c * PAIRS + bp) * STEPS
                nc.vector.scalar_tensor_tensor(SS[:, bass.ds(g, STEPS), :], R2[:, 1:, :], 0.5,
                                               UT[:, bass.ds(g + 1, STEPS), :], ALU.mult, ALU.add).then_inc(sem("r_ss"), 1)
                nc.vector.tensor_copy(R2[:, 0, :], R2[:, STEPS, :]).then_inc(sem("r_last"), 1)
                dve.wait_ge(*at("u_out", t, 1))
                dve.wait_ge(*at("res_kept", t, 1))
                dve.wait_ge(*at("m_H", t, 1))
                dve.wait_ge(*at("m_hist2", t, 1))
                dve.wait_ge(*at("r_ss", t))
                dve.wait_ge(*at("r_last", t))
                nc.vector.memset(st[0][:, 14:15], 0.0).then_inc(sem("tile_done"), 1)

            tiles(dve, tile, PERS + (16,))
            dve.wait_ge(sem("tile_done"), NT // SIDES + 1)
            nc.vector.memset(st[0][:, 13:14], 0.0).then_inc(sem("e_done"), 1)

            def last_steps(t, k):
                for j in range(STEPS):
                    silu_step(t, j, "e")
                dve.wait_ge(*at("e_r", t, n=STEPS))
                g = k * STEPS + T
                nc.vector.scalar_tensor_tensor(SS[:, bass.ds(g, STEPS), :], R2[:, 1:, :], 0.5,
                                               UT[:, bass.ds(g + 1, STEPS), :], ALU.mult, ALU.add).then_inc(sem("e_ss"), 1)
                nc.vector.tensor_copy(R2[:, 0, :], R2[:, STEPS, :]).then_inc(sem("e_last"), 1)
                dve.wait_ge(*at("e_ss", t))
                dve.wait_ge(*at("e_last", t))
                nc.vector.memset(st[0][:, 13:14], 0.0).then_inc(sem("e_done"), 1)

            turns(dve, last_steps, (1, STEPS), "last", PAIRS)
            dve.wait_ge(sem("e_done"), PAIRS + 1)
            nc.vector.memset(st[0][:, 12:13], 0.0).then_inc(sem("o_done"), 1)

            def output(t, c):
                for b in range(NB):
                    dve.wait_ge(*at("o_mm", t, n=b + 1))
                    row = RES[:, bass.ds(c * NB + b, 1), :]
                    nc.vector.tensor_tensor(row, row, ps[b][:, 0:D].unsqueeze(1), ALU.add).then_inc(sem("o_row"), 1)
                dve.wait_ge(*at("o_row", t, n=NB))
                nc.vector.memset(st[0][:, 12:13], 0.0).then_inc(sem("o_done"), 1)

            turns(dve, output, (1, NB), "output", NCH)

        @block.tensor
        def _(pe):
            mm = nc.tensor.matmul
            for i in range(3):
                pe.wait_ge(sem(f"par{i}"), 16)
            pe.wait_ge(sem("probs_in"), 16)
            pe.wait_ge(sem("zeroed"), 1)
            pe.wait_ge(sem("mask_rows"), 48)
            for b in range(NB):
                for k in range(NCH):
                    ins = mm(ps[1][0:S3, b:b + 1], pb[:, b, k, :], w("inv512"), start=k == 0, stop=k == NCH - 1)
            ins.then_inc(sem("mod_pm"), 1)
            pe.wait_ge(sem("mod_pmT"), 1)
            a = PLAN["wprog3"][0]
            mm(ps[0][0:NB, 0:D], pmT[:, :], W[0:S3, a:a + D], start=True, stop=True).then_inc(sem("mod_mm"), 1)

            def turn(dst, src, n):
                for k in range(n):
                    ins = nc.tensor.transpose(dst[:, k * P:(k + 1) * P], src[:, k * P:(k + 1) * P], ident)
                return ins

            def proj_T(dst, wname, src, n):
                for g in range(n):
                    for kk in range(KD):
                        ins = mm(dst[:, g * P:(g + 1) * P], w(wname, KD)[:, kk, g * P:(g + 1) * P], src[:, kk, :],
                                 start=kk == 0, stop=kk == KD - 1)
                return ins

            def proj(dst, wname, src, n, parts=KD, at_col=0):
                for kk in range(parts):
                    ins = mm(dst, src[:, kk, :], w(wname, parts)[:, kk, at_col:at_col + n], start=kk == 0, stop=kk == parts - 1)
                return ins

            def ctx_tile(t, s):
                X = bank[s]
                turn(X[0], xin[:, s, :], KD).then_inc(sem("c_tpx"), 1)
                yield
                pe.wait_ge(*at("c_nrm", t, s))
                turn(X[0][:, D:2 * D], nrm[s], KD).then_inc(sem("c_tpn"), 1)
                yield
                yield
                pe.wait_ge(*at("c_ev", t, s))
                proj_T(X[1][:, 0:256], "wk0", cT[s][0], 2)
                proj_T(X[1][:, 256:384], "wk1", cT[s][0], 1).then_inc(sem("c_k01"), 1)
                proj_T(X[2][:, 0:256], "wk2", cT[s][1], 2)
                proj_T(X[2][:, 256:512], "wk3", cT[s][2], 2).then_inc(sem("c_k23"), 1)
                proj(X[3][:, 0:256], "wv0", cT[s][0], 256)
                proj(X[3][:, 256:384], "wv1", cT[s][0], 128).then_inc(sem("c_v01"), 1)
                proj(X[0][:, 0:256], "wv2", cT[s][1], 256)
                proj(X[0][:, 256:512], "wv3", cT[s][2], 256).then_inc(sem("c_v23"), 1)

            def ctx_pair(t, b, kp):
                pe.wait_ge(*at("c_used", t))
                pe.wait_ge(*at("cin", t, n=16))
                side_by_side(ctx_tile(t, 0), ctx_tile(t, 1))

            pe.wait_ge(sem("mod_done"), 1)
            context(pe, ctx_pair, (16,))

            def mamba(t, s, bp):
                r, X, b = rooms[s], bank[s], bp * SIDES + s
                yield
                pe.wait_ge(*at("m1_nrm", t, s))
                turn(X[0], nrm[s], KD).then_inc(sem("m1_xtp"), 1)
                yield
                yield
                pe.wait_ge(*at("m1_xT", t, s))
                inw = w("inw", KD)
                for g in range(XG):
                    dst = X[1][:, g * P:(g + 1) * P] if g < 4 else X[2][:, (g - 4) * P:(g - 3) * P]
                    for kk in range(KD):
                        ins = mm(dst, inw[:, kk, DI + g * P:DI + (g + 1) * P], xT[s][:, kk, :], start=kk == 0,
                                 stop=kk == KD - 1)
                    if g == 3:
                        ins.then_inc(sem("m_pa"), 1)
                proj(X[2][:, 256:256 + HM], "inw", xT[s], HM, at_col=DI + XBC).then_inc(sem("m_pb"), 1)
                proj(X[3][:, :], "inw", xT[s], DI).then_inc(sem("m_z"), 1)
                for _ in range(6):
                    yield
                pe.wait_ge(*at("m_dA", t, s))
                dA = r.dts[:, 11, :]
                for q, name in enumerate(("tri_le", "tri_gt", "ones")):
                    mm(X[0][:, 256 + q * HM:256 + (q + 1) * HM], w(name), dA, start=True, stop=True)
                pe.wait_ge(*at("m_dAm", t, s))
                pe.wait_ge(*at("m_v", t, s))
                for i in range(2):
                    ins = mm(X[1 + i][:, :], w("tri_gt"), r.dAm[:, 4 * i:4 * i + 4, :].rearrange("p h n -> p (h n)"),
                             start=True, stop=True)
                ins.then_inc(sem("m_seg"), 1)
                yield
                pe.wait_ge(*at("m_xc", t, s))
                pe.wait_ge(*at("m_zs", t, s))
                pe.wait_ge(*at("m_dec", t, s))
                for g in range(4):
                    nc.tensor.transpose(X[3][:, g * P:(g + 1) * P], r.acc[:, g, :], ident)
                nc.tensor.transpose(X[0][:, 0:P], r.acc[:, 4, :], ident)
                mm(X[0][:, P:2 * P], r.acc[:, 4, :], r.acc[:, 5, :], start=True, stop=True).then_inc(sem("m_rows"), 1)
                mm(X[1][:, :], r.acc[:, 5, :], Hst[:, bass.ds(b, 1), :].rearrange("p a n -> p (a n)"), start=True,
                   stop=True).then_inc(sem("m_inter"), 1)
                yield
                yield
                pe.wait_ge(*at("m_M", t, s))
                pe.wait_ge(*at("m_xdt", t, s))
                for h in range(HM):
                    ins = mm(X[2][:, h * HP:(h + 1) * HP], r.seg[:, h, :], r.xdt[:, h * HP:(h + 1) * HP], start=True,
                             stop=True)
                ins.then_inc(sem("m_intra"), 1)
                pe.wait_ge(*at("m_xw", t, s))
                mm(X[3][:, :], r.BG[:, 0, :], r.xw, start=True, stop=True).then_inc(sem("m_state"), 1)
                yield
                yield
                pe.wait_ge(*at("m_un", t, s))
                pe.wait_ge(*at("m_H", t, s))
                turn(X[3], r.y, 4).then_inc(sem("m_utp"), 1)
                yield
                pe.wait_ge(*at("m_uT", t, s))
                proj(X[0][:, 0:D], "outw", r.uT, D, 4).then_inc(sem("m_out"), 1)

            def between(t, li, s):
                step = steps_after(li)
                if li >= 0:
                    l = LAYERS[li]
                    yield step["rdT"]
                    pe.wait_ge(*at(f"{l.name}_rdw", t, s))
                    if (li, s) == (3, 1):
                        pe.wait_ge(*at("u_out", t, 0))
                    elif s:
                        pe.wait_ge(*at(f"{LAYERS[li + 1].name}_qT", t, 0))
                    else:
                        pe.wait_ge(*at(f"{l.name}_qT", t, 1))
                    turn(psAB, rdw, l.quads).then_inc(sem(f"{l.name}_rdT"), 1)
                    yield step["wo"]
                    pe.wait_ge(*at(f"{l.name}_on", t, s))
                    parts = 2 if l.dh == 32 else l.quads
                    proj(psB[:, 0:D], f"wo{li}", oT, D, parts).then_inc(sem(f"{l.name}_op"), 1)
                if li == 1:
                    yield step["f_tp"]
                    pe.wait_ge(*at("x3", t, s))
                    turn(psA, xrow[s], KD).then_inc(sem("f_xtp"), 1)
                    yield step["f_h"]
                    pe.wait_ge(*at("f_xT", t, s))
                    proj_T(psB, "w1", xT[s], KD).then_inc(sem("f_h"), 1)
                    yield step["f_o"]
                    pe.wait_ge(*at("f_hT", t, s))
                    proj(psA[:, 0:D], "w2", hT, D).then_inc(sem("f_o"), 1)
                yield step["tp"]
                if li == 0:
                    pe.wait_ge(*at("x2", t, s))
                    turn(psA, xrow[s], KD).then_inc(sem("L1_xtp"), 1)
                else:
                    name, nxt = {-1: ("L0_n", "L0"), 1: ("L2_n", "L2"), 2: ("L3_n", "L3"), 3: ("u", "u")}[li]
                    pe.wait_ge(*at(f"{name}_nrm", t, s))
                    turn(psA, nrm[s], KD).then_inc(sem(f"{nxt}_xtp"), 1)
                yield step["q"]
                if li == 3:
                    pe.wait_ge(*at("u_xT", t, s))
                    proj_T(psB, "win3", xT[s], KD).then_inc(sem("u_h"), 1)
                    yield step["u_u"]
                    pe.wait_ge(*at("u_hT", t, s))
                    for kk in range(KD):
                        ins = mm(psA[0:S3, 0:P], w("bmat3", KD)[:, kk, :], hT[:, kk, :], start=kk == 0, stop=kk == KD - 1)
                    ins.then_inc(sem("u_u"), 1)
                    return
                l = LAYERS[li + 1]
                pe.wait_ge(*at(f"{l.name}_xT", t, s))
                proj_T(psB, f"wq{li + 1}", xT[s], l.groups).then_inc(sem(f"{l.name}_q"), 1)

            def preload(g):
                a3 = PLAN["at3"][0]
                mm(psR[:, 0:STEPS * NB], W[0:S3, a3:a3 + P], UT[:, bass.ds(g, STEPS), :].rearrange("p t b -> p (t b)"),
                   start=True, stop=True, skip_group_check=True)

            def state_step(t, j, pre):
                if j:
                    pe.wait_ge(*at(f"{pre}_r", t, n=j))
                mm(psR[:, NB * j:NB * (j + 1)], at2[:, :], R2[:, j, :], start=False, stop=True,
                   skip_group_check=True).then_inc(sem(f"{pre}_z"), 1)

            def tile(t, c, bp):
                pe.wait_ge(*at("tile_done", t))
                side_by_side(mamba(t, 0, bp), mamba(t, 1, bp))
                pe.wait_ge(*at("x1", t, 1))
                preload((c * PAIRS + bp) * STEPS)
                Chain(between(t, -1, 0)).finish()
                chain, since = Chain(between(t, -1, 1)), 0
                for u in range(LAST_SLOT):
                    if u in ENDS:
                        chain, since = Chain(between(t, *STAGES[ENDS[u]])), u
                    j = step_of(u)
                    if j is not None:
                        state_step(t, j, "r")
                    chain.go_on(2 * (u - since) + 1)
                    if u < NU:
                        i, l, s, h = UNITS[u]
                        if h == 0:
                            pe.wait_ge(*at(f"kv_in{i % 4}", t, n=32 * (i // 4 + 1)))
                        pe.wait_ge(*at("u_qm", t, n=u + 1))
                        if u >= 3:
                            pe.wait_ge(*at("u_exp", t, n=u - 2))
                        ins = mm(psS[u % 3][:, :], qm[:, u % 4, :], Ks[i % 4][:, h // l.per_group, :],
                                 start=True, stop=l is not L0)
                        if l is L0:
                            ins = mm(psS[u % 3][:, :], ones_b[:, :], m_rows[:, :], start=False, stop=True)
                        ins.then_inc(sem("u_s"), 1)
                    k = u - 2
                    if 0 <= k < NU:
                        pe.wait_ge(*at("u_exp", t, n=k + 1))
                        if k >= 2:
                            pe.wait_ge(*at("u_ev", t, n=k - 1))
                        turn(psT[k % 2], Pr[:, k % 3, :], NCH).then_inc(sem("u_tp"), 1)
                    for k, kts in value_products(u):
                        i, l, s, h = UNITS[k]
                        q = h // 4
                        if q == 0 and i and kts[0] == 0:
                            prev, prev_s = STAGES[i - 1]
                            pe.wait_ge(*at(f"{LAYERS[prev].name}_on", t, prev_s))
                        if kts[0] == 0:
                            pe.wait_ge(*at("u_ev", t, n=k + 1))
                        for kt in kts:
                            for g in range(4):
                                first = (4 * q + g) * l.dh
                                ins = mm(psO[32 * g:32 * g + 32, q * P:(q + 1) * P],
                                         Vs[i % 4][:, kt, first:first + 32], PT[:, (k - 3 + g) % 8, kt, :],
                                         start=kt == 0, stop=kt == NCH - 1)
                        if kts[-1] == NCH - 1:
                            ins.then_inc(sem("u_pv"), 1)
                            if h + 1 == l.heads:
                                pe.wait_ge(*at("u_pv", t, n=k // 4 + 1))
                                pe.sem_inc(sem("kv_used"), 1)
                    if u + 1 in ENDS or u + 1 == LAST_SLOT:
                        chain.finish()

            tiles(pe, tile, PERS)

            def last_steps(t, k):
                pe.wait_ge(*at("e_done", t))
                preload(k * STEPS + T)
                for j in range(STEPS):
                    state_step(t, j, "e")

            turns(pe, last_steps, (1, STEPS), "last", PAIRS)

            def output(t, c):
                pe.wait_ge(*at("o_done", t))
                for b in range(NB):
                    pe.wait_ge(*at("o_ss", t, n=b + 1))
                    c3 = PLAN["cmat3"][0]
                    mm(ps[b][:, 0:D], qT[b // 2][0:S3, b % 2, :], W[0:S3, c3:c3 + D], start=True, stop=False)
                    p3 = PLAN["pickb"][0] + b * P
                    mm(ps[b][:, 0:D], W[0:NB, p3:p3 + P], mod[:, :], start=False, stop=True).then_inc(sem("o_mm"), 1)

            turns(pe, output, (1, NB), "output", NCH)


def kernel(**inputs):
    import concourse.bacc as bacc
    from concourse.bass_utils import run_bass_kernel_spmd

    def a(name):
        return np.asarray(inputs[name])

    def parts(m):
        k = m.shape[0] // P
        return m.reshape(k, P, -1).transpose(1, 0, 2).reshape(P, -1)

    def chan(v):
        return v.reshape(-1, P).T

    def rows(v):
        return np.broadcast_to(v.reshape(1, -1), (P, v.size))

    def half(m):
        out = np.zeros((P, m.shape[1]), np.float32)
        out[:m.shape[0]] = m
        return out

    def spaced(m):
        out = np.zeros((m.shape[0] // 16, 32, m.shape[1]), np.float32)
        out[:, :16] = m.reshape(-1, 16, m.shape[1])
        return out.reshape(-1, m.shape[1])

    i = np.arange(P)
    wqkv, bqkv = a("L3_xattn_W_qkv"), a("L3_xattn_b_qkv")
    vals = {
        "ident": np.eye(P, dtype=np.float32),
        "wk0": parts(a("L0_xattn_Wk")), "wv0": parts(a("L0_xattn_Wv")),
        "wk1": parts(a("L1_xattn_W_k")), "wv1": parts(a("L1_xattn_W_v")),
        "wk2": parts(a("L2_xattn_Wk")), "wv2": parts(a("L2_xattn_Wv")),
        "wk3": parts(wqkv[D:2 * D].T), "wv3": parts(wqkv[2 * D:].T),
        "kvg2": chan(a("L2_xattn_kv_norm_g")), "kvb2": chan(a("L2_xattn_kv_norm_b")),
        "g31": chan(a("L3_xattn_g1")), "b31": chan(a("L3_xattn_beta1")),
        "bk3": chan(bqkv[D:2 * D]), "bv3": rows(bqkv[2 * D:]),
        "tri_le": (i[:, None] <= i[None, :]).astype(np.float32),
        "tri_gt": (i[:, None] > i[None, :]).astype(np.float32),
        "ones": np.ones((P, P), np.float32),
        "inw": parts(a("L0_xattn_in_proj_w")), "mnorm": chan(a("L0_xattn_m_norm_w")),
        "gnorm": chan(a("L0_xattn_gnorm_w")),
        "convw": parts(a("L0_xattn_conv_w")), "convb": chan(a("L0_xattn_conv_b")),
        "dtb": rows(a("L0_xattn_dt_bias")), "alog": rows(a("L0_xattn_A_log")), "dskip": rows(a("L0_xattn_D_skip")),
        "outw": parts(a("L0_xattn_out_proj_w")),
        "wq0": parts(a("L0_xattn_Wq")), "wo0": parts(a("L0_xattn_Wo")),
        "lng0": chan(a("L0_xattn_ca_ln_w")), "lnb0": chan(a("L0_xattn_ca_ln_b")),
        "wq1": parts(a("L1_xattn_W_q")), "wo1": parts(spaced(a("L1_xattn_W_o"))),
        "w1": parts(a("L1_xattn_w1").T), "w2": parts(a("L1_xattn_w2").T),
        "b1": chan(a("L1_xattn_b1")), "b2": rows(a("L1_xattn_b2")),
        "wq2": parts(a("L2_xattn_Wq")), "wo2": parts(spaced(a("L2_xattn_Wo"))),
        "qg2": chan(a("L2_xattn_q_norm_g")), "qb2": chan(a("L2_xattn_q_norm_b")), "bo2": rows(a("L2_xattn_bo")),
        "wq3": parts(wqkv[:D].T), "wo3": parts(a("L3_xattn_W_o").T), "bq3": chan(bqkv[:D]),
        "bo3": rows(a("L3_xattn_b_o")),
        "win3": parts(a("L3_xattn_W_in").T), "bin3": chan(a("L3_xattn_b_in")), "bmat3": parts(a("L3_xattn_Bmat")),
        "g32": chan(a("L3_xattn_g2")), "b32": chan(a("L3_xattn_beta2")),
        "at3": half(a("L3_xattn_A").T), "cmat3": half(a("L3_xattn_Cmat")), "wprog3": half(a("L3_xattn_W_prog").T),
        "bprog3": rows(a("L3_xattn_b_prog")),
        "hm32": (i[:, None] // 32 == np.arange(4)[None, :]).astype(np.float32),
        "hm16": (i[:, None] // 16 == np.arange(8)[None, :]).astype(np.float32),
        "neghalf": np.full((P, 1), -0.5, np.float32),
        "inv512": np.full((P, 1), 1.0 / T, np.float32),
        "pickb": (i[:, None] == np.arange(NB * P)[None, :] // P).astype(np.float32),
    }
    pack = np.zeros((P, NPACK), np.float32)
    for name, (first, n) in PLAN.items():
        pack[:, first:first + n] = vals[name]

    mask = np.zeros((T, 4), np.uint8)
    mask[:, 0] = a("mask_1xS2_bf0").reshape(-1).view(np.uint8)

    nc = bacc.Bacc("TRN2", target_bir_lowering=False, num_devices=1)
    arrays, aps = {}, []
    for name, arr in (("x", a("x")), ("ctx", a("ctx_1024")), ("probs", a("ctxb_2048x64")),
                      ("mask", mask.view(np.int32).reshape(-1)), ("pack", pack)):
        arr = np.ascontiguousarray(arr)
        arrays[f"in_{name}"] = arr
        aps.append(nc.dram_tensor(f"in_{name}", arr.shape, mybir.dt.from_np(arr.dtype), kind="ExternalInput").ap())
    kd = nc.dram_tensor("keys", (NB, P, KG, T), F32, kind="Internal").ap()
    vd = nc.dram_tensor("values", (NB, P, NCH, VW), F32, kind="Internal").ap()
    out = nc.dram_tensor("out_0", (NB, T, D), F32, kind="ExternalOutput").ap()
    build(nc, *aps, kd, vd, out)
    r = run_bass_kernel_spmd(nc, [arrays], core_ids=[0])
    return r.results[0]["out_0"]
```

```python
from contextlib import ExitStack

import numpy as np

import concourse.bass as bass
from concourse import mybir

F32 = mybir.dt.float32
BF16 = mybir.dt.bfloat16
I32 = mybir.dt.int32
ALU = mybir.AluOpType
ACT = mybir.ActivationFunctionType
AX = mybir.AxisListType.X

P = 128
NB = 4
T = 512
D = 256
KD = D // P
NCH = T // P
NT = NB * NCH
SIDES = 2
PAIRS = NB // SIDES
STEPS = P // PAIRS
EPS = 1e-5

DI = 512
NST = 128
HM = 8
HP = DI // HM
XBC = DI + 2 * NST
XG = XBC // P
CONV = 4
PE_CONV = 3
PE_CONV = 3
PE_CONV = 3
PE_CONV = 3

S3 = 64


class Layer:

    def __init__(self, name, heads, dh, kgroup, vcol):
        self.name, self.heads, self.dh = name, heads, dh
        self.width = heads * dh
        self.groups = self.width // P
        self.per_group = P // dh
        self.scale = float(dh) ** -0.5
        self.quads = heads // 4
        self.kgroup, self.vcol = kgroup, vcol


L0 = Layer("L0", 8, 32, 0, 0)
L1 = Layer("L1", 8, 16, 2, 256)
L2 = Layer("L2", 16, 16, 3, 384)
L3 = Layer("L3", 8, 32, 5, 640)
LAYERS = (L0, L1, L2, L3)
KG = sum(l.groups for l in LAYERS)
VW = sum(l.width for l in LAYERS)

STAGES = [(li, s) for li in range(len(LAYERS)) for s in range(SIDES)]
UNITS = [(i, LAYERS[li], s, h) for i, (li, s) in enumerate(STAGES) for h in range(LAYERS[li].heads)]
NU = len(UNITS)
QUADS = NU // 4
ENDS = {u + 1: unit[0] for u, unit in enumerate(UNITS) if u + 1 == NU or UNITS[u + 1][0] != unit[0]}
LAST_SLOT = NU + 3
NU_BEFORE = {st: min(u for u, unit in enumerate(UNITS) if unit[0] == i) for i, st in enumerate(STAGES)}


def turned_in(u):
    return [k for k in range(NU) if u == k + (1 if k + 1 in ENDS else 2)]


def value_products(u):
    work = []
    for k in range(3, NU, 4):
        if k + 1 in ENDS:
            if u == k + 2:
                work.append((k, range(NCH)))
        elif 0 <= u - (k + 3) < NCH:
            work.append((k, range(u - (k + 3), u - (k + 3) + 1)))
    return work


def step_of(u):
    if u >= NU or UNITS[u][1] is L1:
        return None
    return sum(UNITS[v][1] is not L1 for v in range(u))


def pack_plan():
    sizes = [
        ("ident", P), ("neghalf", 1), ("inv512", 1),
        ("wk0", KD * 256), ("wv0", KD * 256), ("wk1", KD * 128), ("wv1", KD * 128),
        ("wk2", KD * 256), ("wv2", KD * 256), ("wk3", KD * 256), ("wv3", KD * 256),
        ("wprog3", 256), ("bprog3", 256),
        ("kvg2", KD), ("kvb2", KD), ("g31", KD), ("b31", KD), ("bk3", KD), ("bv3", 256),
        ("tri_le", P), ("tri_gt", P), ("ones", P),
        ("inw", KD * 1288), ("mnorm", KD), ("gnorm", 4), ("convw", XG * CONV), ("convb", XG),
        ("dtb", HM), ("alog", HM), ("dskip", HM), ("outw", 4 * 256),
        ("wq0", KD * 256), ("wo0", KD * 256), ("lng0", KD), ("lnb0", KD),
        ("wq1", KD * 128), ("wo1", 512), ("w1", KD * 256), ("w2", KD * 256), ("b1", KD), ("b2", 256),
        ("wq2", KD * 256), ("wo2", 4 * 256), ("qg2", KD), ("qb2", KD), ("bo2", 256),
        ("wq3", KD * 256), ("wo3", KD * 256), ("bq3", KD), ("bo3", 256),
        ("win3", KD * 256), ("bin3", KD), ("bmat3", KD * S3), ("g32", KD), ("b32", KD),
        ("at3", S3), ("cmat3", 256),
        ("hm32", 4), ("hm16", 8), ("eyeb", NB),
    ]
    plan, at = {}, 0
    for name, n in sizes:
        plan[name] = (at, n)
        at += n
    return plan, at


PLAN, NPACK = pack_plan()
CUTS = [0, PLAN["tri_le"][0], PLAN["wq0"][0], NPACK]


EARLY = (NCH - 1) * SIDES
EARLY_GAP = STEPS // EARLY

PER_SIDE = {"m_conv": CONV - 1}
PER_TURN = {"cin": 16, "c_taken": 1, "c_used": 1, "x_in": 16, "x_taken": 1, "tile_done": 1,
            "c_st0": 32, "c_st1": 32,
            "kv_in0": 64, "kv_in1": 64, "kv_in2": 64, "kv_in3": 64, "kv_used": len(STAGES),
            "m_v1": 1, "m_v": 1, "m_e": 1, "m_e2": 1, "m_rc": 1, "m_r": 1, "m_log": 11, "m_dt": 1, "m_dA": 1,
            "u_qm": NU, "u_s": NU, "u_mx": NU, "u_exp": NU, "u_tp": NU, "u_ev": NU, "u_pv": QUADS,
            "r_z": STEPS, "r_th": STEPS, "r_r": STEPS, "r_ss": 1, "r_last": 1,
            "e_half": 1, "e_z": STEPS, "e_r": STEPS, "e_ss": 1, "e_last": 1, "e_done": 1,
            "o_ss": EARLY, "o_mm": EARLY, "o_row": EARLY}
NORM_STEPS = ("bn", "ag", "ve", "rs", "nrm")
NORMS = ("L0", "L2", "L3", "u")
RESIDUAL = ("x2", "x3", "x4", "x5", "x6", "x7", "x8")


def counted(name, s):
    who, _, step = name.partition("_")
    if name in PER_TURN:
        return name, PER_TURN[name], 0
    if step.removeprefix("n_") in NORM_STEPS and who in NORMS:
        return f"norm_{step.removeprefix('n_')}", SIDES * len(NORMS), SIDES * NORMS.index(who) + s
    if who in ("L0", "L1", "L2", "L3") and step not in ("pre", "gelu"):
        return f"layer_{step}", len(STAGES), STAGES.index((int(who[1]), s))
    if name in RESIDUAL:
        group = next(g for g in (("x2",), ("x3", "x4", "x5"), ("x6",), ("x7", "x8")) if name in g)
        before = RESIDUAL.index(group[0])
        return "residual", SIDES * len(RESIDUAL), SIDES * before + s * len(group) + group.index(name)
    per = PER_SIDE.get(name, 1)
    return name, SIDES * per, s * per


class Turn:

    def __init__(self, eng, pers, loop):
        self.eng = eng
        self.regs = {p: eng.alloc_register(name=f"{loop}_turn_x{p}") for p in sorted(set(pers))}
        self.sum = eng.alloc_register(name=f"{loop}_sum")
        for r in self.regs.values():
            eng.reg_mov(r, 1)

    def value(self, per, n):
        if n == 1:
            return self.regs[per]
        self.eng.reg_add(self.sum, self.regs[per], n - 1)
        return self.sum

    def end(self):
        for p, r in self.regs.items():
            self.eng.reg_add(r, r, p)


class First:

    def __init__(self, eng):
        self.eng = eng

    def value(self, per, n):
        return n


class After:

    def __init__(self, eng, count):
        self.eng, self.count = eng, count

    def value(self, per, n):
        return self.count * per + n


class Ahead:

    def __init__(self, turn):
        self.eng, self.turn = turn.eng, turn

    def value(self, per, n):
        return self.turn.value(per, per + n)


def steps_after(li):
    step = {}
    if li >= 0:
        step.update(rd=1, rdT=2, rdb=3, on=5, wo=6, add=7)
    step.update({-1: dict(stats=1, nrm=3, tp=4), 0: dict(tp=8),
                 1: dict(f_tp=8, f_xT=9, f_h=10, f_relu=11, f_o=12, stats=13, nrm=15, tp=16),
                 2: dict(gelu=9, stats=11, nrm=13, tp=14), 3: dict(stats=7, nrm=9, tp=10)}[li])
    tp = step["tp"]
    step.update(xT=tp + 1, q=tp + 2, qT=tp + 3, u_hT=tp + 3, u_u=tp + 4, u_out=tp + 5)
    return step


class Chain:

    def __init__(self, body):
        self.body = body
        self.step = next(body, None)

    def go_on(self, last):
        while self.step is not None and self.step <= last:
            self.step = next(self.body, None)

    def finish(self):
        self.go_on(1000)


def build(nc, x, ctx_in, probs, maskf, pack, kd, vd, out):
    with ExitStack() as stack:
        def sb(name, shape, dt=F32):
            return stack.enter_context(nc.sbuf_tensor(name, shape, dt))

        sems = {}

        def sem(name):
            name = counted(name, 0)[0]
            if name not in sems:
                sems[name] = stack.enter_context(nc.semaphore(name))
            return sems[name]

        def at(name, turn, s=0, n=1, apart=False):
            _, per, before = counted(name, s)
            value = turn.value(per, before + n)
            if apart:
                turn.eng.wait_ge(sem("par0"), 16)
            return sem(name), value

        W = sb("W", [P, NPACK])

        def w(name, parts=None):
            a, n = PLAN[name]
            v = W[:, a:a + n]
            return v if parts is None else v.rearrange("p (k n) -> p k n", k=parts)

        def col(name, i):
            a, n = PLAN[name]
            return W[:, a + i:a + i + 1]

        def wide(ap, n):
            return ap.unsqueeze(2).to_broadcast([P, ap.shape[1], n])

        Ks = [sb(f"K{i}", [P, KD, T]) for i in range(4)]
        Vs = [sb(f"V{i}", [P, NCH, D + 16]) for i in range(4)]
        RES = sb("RES", [P, NT, D])
        early = RES[0:1, :, :].rearrange("p a n -> p (a n)")
        m_row = early[:, 0:T]
        m_tmp = early[:, T:4 * T].rearrange("p (i n) -> p i n", i=3)
        m_part = early[:, 4 * T:6 * T].bitcast(BF16)[:, 0:3 * T].rearrange("p (i n) -> p i n", i=3)
        m_rows = sb("m_rows", [3, T], BF16)
        ones_b = sb("ones_b", [3, P], BF16)
        at2 = sb("at2", [S3, P])
        cm = sb("cm", [S3 + NB, D])
        pmT = sb("pmT", [S3, NB])
        negA = sb("negA", [P, HM])
        bq3 = sb("bq3", [P, KD])
        hconv = sb("hconv", [P, XG * CONV])
        hconvb = sb("hconvb", [P, XG])
        hist = sb("hist", [P, NB, XG, CONV - 1])
        Hst = sb("Hst", [P, NB, DI])
        UT = sb("UT", [S3, P + T + 1, NB])
        R2 = sb("R2", [S3, STEPS + 1, NB])
        th3 = sb("th3", [S3, NB])
        SS = sb("SS", [S3 + NB, P + T, NB])

        xin = sb("xin", [P, SIDES, D])
        xrow = [sb(f"xrow{s}", [P, D]) for s in range(SIDES)]
        nrm = [sb(f"nrm{s}", [P, D]) for s in range(SIDES)]
        st = [sb(f"st{s}", [P, 16]) for s in range(SIDES)]
        xT = [sb(f"xT{s}", [P, KD, P]) for s in range(SIDES)]
        qT = [sb(f"qT{s}", [P, KD, P]) for s in range(SIDES)]
        hT = sb("hT", [P, KD, P])
        orows = sb("orows", [P, D])
        qm = sb("qm", [P, 4, P])
        Pr = sb("Pr", [P, 3, T])
        PT = sb("PT", [P, 8, NCH, P])
        nmax = sb("nmax", [P, NU])
        den = sb("den", [P, NU])
        rden = sb("rden", [P, NU])
        rdb = sb("rdb", [P, 4 * P])
        oT = sb("oT", [P, 4, P])
        rdw = oT[:, :, :].rearrange("p a n -> p (a n)")

        room1 = sb("room1", [P, XG * (3 * P + CONV - 1) + 3 * DI])
        PTf = PT[:, :, :, :].rearrange("p a k n -> p a (k n)")
        Prf = Pr[:, 0:2, :].rearrange("p i n -> p (i n)")

        class Room:
            def __init__(self, ap, big, seg, xr):
                self.ap, self.used = ap, 0
                self.xpad = self.take(XG * (P + CONV - 1)).rearrange("p (g n) -> p g n", g=XG)
                self.acc = self.take(XG * P).rearrange("p (g n) -> p g n", g=XG)
                self.th = self.take(XG * P).rearrange("p (g n) -> p g n", g=XG)
                self.y, self.y2, self.xdt = self.take(DI), self.take(DI), self.take(DI)
                self.nrm = self.y2[:, 0:D]
                self.xT = self.y[:, D:2 * D].rearrange("p (k n) -> p k n", k=KD)
                self.st = sb(f"stm{len(rooms)}", [P, 8])
                self.zt = self.th.rearrange("p g n -> p (g n)")[:, 0:DI]
                self.dAm = big.rearrange("p (h n) -> p h n", h=HM)
                self.xw = big[:, DI:]
                self.uT = big[:, 0:DI].rearrange("p (k n) -> p k n", k=4)
                self.seg = seg.rearrange("p (h n) -> p h n", h=HM)
                self.xr = xr
                self.dec = sb(f"dec{len(rooms)}", [P, 3, HM])
                self.BG = qm[:, 2 * len(rooms):2 * len(rooms) + 2, :]

            def take(self, n):
                self.used += n
                return self.ap[:, self.used - n:self.used]

        SSb = [qT[i // 2][0:S3 + NB, i % 2, :] for i in range(4)]
        rooms = []
        dts = sb("dts", [P, 12, SIDES, HM])
        diag = sb("diag", [P, PE_CONV, CONV, P])
        rooms.append(Room(W[:, PLAN["wk0"][0]:PLAN["kvg2"][0]], Prf, PTf[:, 0:2, :].rearrange("p a n -> p (a n)"),
                          PTf[:, 2, :]))
        rooms.append(Room(room1, PTf[:, 3:5, :].rearrange("p a n -> p (a n)"),
                          PTf[:, 5:7, :].rearrange("p a n -> p (a n)"), PTf[:, 7, :]))

        cT = [[PTf[:, 3 * s:3 * s + 3, :].rearrange("p a n -> p (a n)")[:, i * D:(i + 1) * D]
               .rearrange("p (k n) -> p k n", k=KD) for i in range(3)] for s in range(SIDES)]
        keep = PTf[:, 7, :]
        pb = Prf.rearrange("p (b k s) -> p b k s", b=NB, k=NCH)
        KS = [room1[:, s * KG * P:(s + 1) * KG * P].rearrange("p (g n) -> p g n", g=KG) for s in range(SIDES)]
        VS = [room1[:, SIDES * KG * P + s * VW:SIDES * KG * P + (s + 1) * VW] for s in range(SIDES)]

        ps = [stack.enter_context(nc.psum_tensor(f"ps{i}", [P, 512], F32)) for i in range(8)]
        bank = [ps[0:4], ps[4:8]]
        psS, psT, psO, psR = [ps[0], ps[5], ps[6]], ps[1:3], ps[4], ps[7]
        psAB = ps[3]
        psA, psB = psAB[:, 0:D], psAB[:, D:2 * D]
        ident = w("ident")

        TAIL = 6
        AFTER = 22
        LATE = 4

        block = stack.enter_context(nc.Block())

        PERS = (1, SIDES, SIDES * PER_SIDE["m_conv"], len(STAGES), SIDES * len(RESIDUAL), 64, NU, QUADS, STEPS, PER_TURN["m_log"])

        def turns(eng, body, pers, loop, outer, inner=1):
            t = Turn(eng, pers, loop)
            with eng.Fori(0, outer) as c:
                if inner == 1:
                    body(t, c)
                    t.end()
                else:
                    with eng.Fori(0, inner) as b:
                        body(t, c, b)
                        t.end()

        def context(eng, body, pers=()):
            turns(eng, body, (1, 2) + pers, "context", NB, NCH // SIDES)

        def tiles(eng, body, pers=PERS):
            turns(eng, body, pers, "tiles", NCH, PAIRS)

        def side_by_side(first, second, then=None, before=None):
            chains = [(Chain(first), 0), (Chain(second), 0)]
            if then is not None:
                chains.append((Chain(then), AFTER))
            if before is not None:
                chains.insert(0, (before, -TAIL))
            for step in range(50):
                for chain, since in chains:
                    chain.go_on(step - since)

        @block.sync
        def _(sp):
            sp.dma_start(W[:, CUTS[0]:CUTS[1]], pack[:, CUTS[0]:CUTS[1]]).then_inc(sem("par0"), 16)
            sp.wait_ge(sem("mask_in"), 32)
            sp.wait_ge(sem("probs_in"), 16)
            sp.wait_ge(sem("cin"), 16)
            for i in range(1, 3):
                sp.dma_start(W[:, CUTS[i]:CUTS[i + 1]], pack[:, CUTS[i]:CUTS[i + 1]]).then_inc(sem(f"par{i}"), 16)
            sp.wait_ge(sem("mask_parts"), 6)
            for i in range(3):
                sp.dma_start(m_rows[i:i + 1, :], m_part[0:1, i, :]).then_inc(sem("mask_rows"), 16)

            def ctx_pair(t, b, kp):
                for s in range(SIDES):
                    sp.wait_ge(*at("c_dve", t, s))
                    sp.dma_start(kd[b, :, :, bass.ts(kp * SIDES + s, P)], KS[s][:, :, :]).then_inc(sem(f"c_st{s}"), 16)
                    sp.dma_start(vd[b, :, bass.ds(kp * SIDES + s, 1), :].squeeze(1), VS[s]).then_inc(sem(f"c_st{s}"), 16)

            context(sp, ctx_pair)
            for s in range(SIDES):
                sp.wait_ge(sem(f"c_st{s}"), 32 * (NT // SIDES) + 1)

            def tile(t, c, bp):
                sp.wait_ge(*at("x_taken", t))
                sp.dma_start(xin[:, :, :], x[bass.ds(bp * SIDES, SIDES), bass.ts(c, P), :]
                             .rearrange("b p d -> p b d")).then_inc(sem("x_in"), 16)
                for i, (li, s) in enumerate(STAGES):
                    l = LAYERS[li]
                    sp.wait_ge(*at("kv_used", t, n=i + 1))
                    sp.dma_start(Ks[i % 4][:, 0:l.groups, :],
                                 kd[bass.ds(bp * SIDES + s, 1), :, l.kgroup:l.kgroup + l.groups, :]
                                 .squeeze(0)).then_inc(sem(f"kv_in{i % 4}"), 16)
                    sp.dma_start(Vs[i % 4][:, :, 0:l.width],
                                 vd[bass.ds(bp * SIDES + s, 1), :, :, l.vcol:l.vcol + l.width]
                                 .squeeze(0)).then_inc(sem(f"kv_in{i % 4}"), 16)

            tiles(sp, tile, (1, 8))
            sp.wait_ge(sem("x_taken"), NT // SIDES + 1)
            sp.dma_start(xin[:, :, :], x[0:SIDES, 0:P, :].rearrange("b p d -> p b d")).then_inc(sem("x_in"), 16)

            def last_steps(t, k):
                for i in range(EARLY):
                    sp.wait_ge(*at("o_row", t, n=i + 1))
                    store(i // SIDES, k * SIDES + i % SIDES)

            def store(c, b):
                sp.dma_start(out[bass.ds(b, 1), c * P:(c + 1) * P, :].squeeze(0),
                             RES[:, bass.ds(c * NB + b, 1), :].squeeze(1)).then_inc(sem("o_out"), 16)

            turns(sp, last_steps, (1, EARLY), "last", PAIRS)
            for b in range(NB):
                sp.wait_ge(sem("f_row"), b + 1)
                sp.dma_start(out[b, T - P:, :], RES[:, (NCH - 1) * NB + b, :]).then_inc(sem("o_out"), 16)
            sp.wait_ge(sem("o_out"), 16 * NT)

        @block.gpsimd
        def _(pool):
            pool.dma_start(keep.bitcast(I32), maskf.partition_broadcast(P)).then_inc(sem("mask_in"), 16)
            pool.dma_start(m_row[:, :].bitcast(I32), maskf.rearrange("(a n) -> a n", a=1)).then_inc(sem("mask_in"), 16)
            pool.dma_start(pb, probs.rearrange("b (k p) s -> p b k s", p=P)).then_inc(sem("probs_in"), 16)
            pool.memset(hist[:, :, :, :], 0.0)
            pool.memset(Hst[:, :, :], 0.0)
            pool.memset(UT[:, 0:P + 1, :], 0.0)
            pool.memset(R2[:, 0, :], 0.0)
            for v in Vs:
                pool.memset(v[:, :, P:], 0.0)
            pool.memset(ones_b[:, :], 1.0).then_inc(sem("zeroed"), 1)

            def root(name, k, t, s, st=st):
                pool.wait_ge(*at(f"{name}_ve", t, s))
                nc.gpsimd.tensor_tensor(st[s][:, k + 9:k + 10], st[s][:, k + 8:k + 9], w("neghalf"),
                                        ALU.pow).then_inc(sem(f"{name}_rs"), 1)

            pool.wait_ge(sem("par0"), 16)

            def ctx_pair(t, b, kp):
                pool.wait_ge(*at("c_taken", t))
                pool.dma_start(xin[:, :, :], ctx_in[b, bass.ts(kp, SIDES * P), :].rearrange("(s p) d -> p s d", s=SIDES)
                               ).then_inc(sem("cin"), 16)
                for s in range(SIDES):
                    root("c", 0, t, s)

            context(pool, ctx_pair)
            pool.wait_ge(sem("c_taken"), NT // SIDES + 1)
            pool.dma_start(xin[:, :, :], ctx_in[0, 0:SIDES * P, :].rearrange("(s p) d -> p s d", s=SIDES)
                           ).then_inc(sem("cin"), 16)
            for s in range(SIDES):
                root("c", 0, After(pool, NT // SIDES), s)
            for i in range(1, 3):
                pool.wait_ge(sem(f"par{i}"), 16)

            def mamba(t, s, b):
                r, late = rooms[s], LATE * s
                yield 0
                nc.gpsimd.tensor_copy(r.xpad[:, :, 0:CONV - 1], hist[:, bass.ds(b, 1), :, :].squeeze(1)
                                      ).then_inc(sem("m_hist"), 1)
                root("m1", -8, t, s, [r.st for r in rooms])
                yield 7
                pool.wait_ge(*at("m_xbc", t, s, apart=True))
                nc.gpsimd.tensor_copy(hist[:, bass.ds(b, 1), :, :].squeeze(1), r.xpad[:, :, P:P + CONV - 1]
                                      ).then_inc(sem("m_hist2"), 1)
                if s == 1:
                    yield 8
                    pool.wait_ge(*at("m_dA", t))
                    pool.wait_ge(*at("m_dAm", t, 0))
                    nc.gpsimd.tensor_tensor(r.dAm, w("tri_le").unsqueeze(1).to_broadcast([P, HM, P]),
                                            wide(dts[:, 11, s, :], P), ALU.mult).then_inc(sem("m_dAm"), 1)
                yield 14 + late
                pool.wait_ge(*at("m_xr", t, s))
                nc.gpsimd.tensor_tensor(r.y2.rearrange("p (h n) -> p h n", h=HM),
                                        r.xr.rearrange("p (h n) -> p h n", h=HM),
                                        wide(w("dskip"), HP), ALU.mult).then_inc(sem("m_xD"), 1)
                pool.wait_ge(*at("m_xdt", t, s))
                pool.wait_ge(*at("m_dec", t, s))
                nc.gpsimd.tensor_tensor(r.xw.rearrange("p (h n) -> p h n", h=HM),
                                        r.xdt.rearrange("p (h n) -> p h n", h=HM),
                                        wide(r.dec[:, 1, :], HP), ALU.mult).then_inc(sem("m_xw"), 1)
                yield 17 + late
                root("m2", -5, t, s, [r.st for r in rooms])

            def between(t, li, s):
                if li != 0:
                    yield steps_after(li)["stats"]
                    root({-1: "L0_n", 1: "L2_n", 2: "L3_n", 3: "u"}[li], 0, t, s)

            def mamba_block(t, b, before=None):
                side_by_side(mamba(t, 0, b), mamba(t, 1, b + 1), between(t, -1, 0), before)

            def tile(t, c, bp):
                pool.wait_ge(*at("tile_done", t, apart=True))
                chain, since = Chain(between(t, -1, 1)), 0

                def mask_query(u):
                    i, l, s, h = UNITS[u]
                    if h == 0:
                        pool.wait_ge(*at(f"{l.name}_qT", t, s, apart=True))
                    if u >= 4:
                        pool.wait_ge(*at("u_s", t, n=u - 3, apart=True))
                    nc.gpsimd.tensor_scalar(qm[:, u % 4, :], qT[s][:, h // l.per_group, :],
                                            col(f"hm{l.dh}", h % l.per_group), None,
                                            ALU.mult).then_inc(sem("u_qm"), 1)

                for u in range(3):
                    mask_query(u)
                for u in range(LAST_SLOT):
                    if u in ENDS:
                        chain, since = Chain(between(t, *STAGES[ENDS[u]])), u
                    if u + 3 in ENDS:
                        chain.finish()
                    if u + 3 < NU:
                        mask_query(u + 3)
                    chain.go_on(2 * (u - since) + 1)
                mamba_block(Ahead(t), SIDES - bp * SIDES, chain)

            pool.wait_ge(sem("ready"), 1)
            mamba_block(First(pool), 0)
            tiles(pool, tile)

        @block.scalar
        def _(act):
            act.wait_ge(sem("par0"), 16)

            def ctx_tile(t, s):
                X = bank[s]
                yield 2
                act.wait_ge(*at("c_tpn", t, s))
                nc.scalar.copy(cT[s][0].rearrange("p k n -> p (k n)"), X[0][:, 0:D])
                for i, (g, bb) in ((1, ("kvg2", "kvb2")), (2, ("g31", "b31"))):
                    for kk in range(KD):
                        ins = nc.scalar.activation(cT[s][i][:, kk, :], X[0][:, D + kk * P:D + (kk + 1) * P], ACT.Identity,
                                                   bias=col(bb, kk), scale=col(g, kk))
                ins.then_inc(sem("c_ev"), 1)
                yield 4
                act.wait_ge(*at("c_k23", t, s))
                act.wait_ge(*at(f"c_st{s}", t, n=1))
                nc.scalar.copy(KS[s][:, 3:5, :], X[2][:, 0:D].rearrange("p (g n) -> p g n", g=2))
                for g in range(2):
                    nc.scalar.activation(KS[s][:, 5 + g, :], X[2][:, D + g * P:D + (g + 1) * P],
                                         ACT.Identity, bias=col("bk3", g))
                act.wait_ge(*at("c_v01", t, s))
                nc.scalar.copy(VS[s][:, 0:384], X[3][:, 0:384]).then_inc(sem("c_act"), 1)

            act.wait_ge(sem("mod_pm"), 1)
            nc.scalar.copy(pmT[:, :], ps[1][0:S3, 0:NB]).then_inc(sem("mod_pmT"), 1)
            act.wait_ge(sem("mod_done"), 1)
            context(act, lambda t, b, kp: side_by_side(ctx_tile(t, 0), ctx_tile(t, 1)), (32,))
            for i in range(1, 3):
                act.wait_ge(sem(f"par{i}"), 16)
            nc.scalar.activation(dts[:, 0, 0, :], w("alog"), ACT.Exp).then_inc(sem("expA"), 1)

            def evac_xT(name, t, s, src, g=None, b=None, dst=None):
                dst = xT[s] if dst is None else dst
                act.wait_ge(*at(f"{name}_xtp", t, s))
                if g is None:
                    nc.scalar.copy(dst[:, :, :].rearrange("p k n -> p (k n)"), src[:, 0:D]).then_inc(sem(f"{name}_xT"), 1)
                else:
                    for kk in range(KD):
                        ins = nc.scalar.activation(dst[:, kk, :], src[:, kk * P:(kk + 1) * P], ACT.Identity,
                                                   bias=col(b, kk) if b else 0.0, scale=col(g, kk))
                    ins.then_inc(sem(f"{name}_xT"), 1)

            def mamba(t, s):
                r, X, late = rooms[s], bank[s], LATE * s
                yield 3
                evac_xT("m1", t, s, X[0], "mnorm", dst=r.xT)
                yield 5
                act.wait_ge(*at("m_pa", t, s))
                nc.scalar.copy(r.xpad[:, 0:4, CONV - 1:], X[1][:, :].rearrange("p (g n) -> p g n", g=4))
                act.wait_ge(*at("m_pb", t, s))
                nc.scalar.copy(r.xpad[:, 4:6, CONV - 1:],
                               X[2][:, 0:256].rearrange("p (g n) -> p g n", g=2)).then_inc(sem("m_xbc"), 1)
                act.wait_ge(*at("m_xbc", t, s))
                act.wait_ge(*at("m_hist", t, s))
                for g in range(XG - PE_CONV):
                    ins = nc.scalar.activation(r.acc[:, g, :], r.xpad[:, g, 0:P], ACT.Identity,
                                               bias=hconvb[:, g:g + 1], scale=hconv[:, g * CONV:g * CONV + 1])
                ins.then_inc(sem("m_conv0"), 1)
                if s == 1:
                    yield 6
                    act.wait_ge(*at("m_v", t))
                    nc.scalar.activation(dts[:, 3, :, :], dts[:, 2, :, :], ACT.Exp).then_inc(sem("m_e"), 1)
                yield 7
                act.wait_ge(*at("m_cv", t, s))
                for g in range(PE_CONV):
                    c = XG - PE_CONV + g
                    ins = nc.scalar.activation(r.acc[:, c, :], X[1][:, g * P:(g + 1) * P], ACT.Identity,
                                               bias=hconvb[:, c:c + 1])
                ins.then_inc(sem("m_cev"), 1)
                yield 9 + late
                act.wait_ge(*at("m_conv", t, s, CONV - 1))
                act.wait_ge(*at("m_cev", t, s))
                nc.scalar.activation(r.th.rearrange("p g n -> p (g n)"),
                                     r.acc.rearrange("p g n -> p (g n)"), ACT.Tanh).then_inc(sem("m_th"), 1)
                yield 10 + late
                act.wait_ge(*at("m_seg", t, s))
                for i in range(2):
                    nc.scalar.activation(r.seg[:, 4 * i:4 * i + 4, :].rearrange("p g n -> p (g n)"), X[1 + i][:, :], ACT.Exp)
                nc.scalar.activation(r.dec[:, :, :].rearrange("p g n -> p (g n)"), X[0][:, 256:256 + 3 * HM],
                                     ACT.Exp).then_inc(sem("m_dec"), 1)
                yield 12 + late
                act.wait_ge(*at("m_rows", t, s))
                nc.scalar.copy(r.xr, X[3][:, :]).then_inc(sem("m_xr"), 1)
                nc.scalar.copy(r.BG[:, 0, :], X[0][:, 0:NST]).then_inc(sem("m_Br"), 1)
                yield 14 + late
                act.wait_ge(*at("m_xc", t, s))
                act.wait_ge(*at("m_z", t, s))
                nc.scalar.activation(r.zt, X[3][:, :], ACT.Tanh, scale=0.5).then_inc(sem("m_zt"), 1)
                yield 16 + late
                act.wait_ge(*at("m_y3", t, s))
                nc.scalar.activation(r.y2, r.y, ACT.Square, accum_out=r.st[:, 6:7]).then_inc(sem("m2_ss"), 1)
                yield 20 + late
                act.wait_ge(*at("m_utp", t, s))
                for k in range(4):
                    ins = nc.scalar.activation(r.uT[:, k, :], X[1][:, k * P:(k + 1) * P], ACT.Copy,
                                               scale=col("gnorm", k))
                ins.then_inc(sem("m_uT"), 1)

            def between(t, li, s):
                step = steps_after(li)
                if li >= 0:
                    l = LAYERS[li]
                    yield step["rdb"]
                    act.wait_ge(*at(f"{l.name}_rdT", t, s))
                    nc.scalar.copy(rdb[:, 0:l.quads * P], psAB[:, 0:l.quads * P]).then_inc(sem(f"{l.name}_rdb"), 1)
                if li == 1:
                    yield step["f_xT"]
                    evac_xT("f", t, s, psA)
                    yield step["f_relu"]
                    act.wait_ge(*at("f_h", t, s))
                    for g in range(KD):
                        ins = nc.scalar.activation(hT[:, g, :], psB[:, g * P:(g + 1) * P], ACT.Relu, bias=col("b1", g))
                    ins.then_inc(sem("f_hT"), 1)
                if li == 2:
                    yield step["gelu"]
                    act.wait_ge(*at("L2_pre", t, s))
                    nc.scalar.activation(nrm[s][:, :], orows[:, :], ACT.Gelu).then_inc(sem("L2_gelu"), 1)
                yield step["xT"]
                if li == 3:
                    evac_xT("u", t, s, psA, "g32", "b32")
                    yield step["u_hT"]
                    act.wait_ge(*at("u_h", t, s))
                    for g in range(KD):
                        ins = nc.scalar.activation(hT[:, g, :], psB[:, g * P:(g + 1) * P], ACT.Identity, bias=col("bin3", g))
                    ins.then_inc(sem("u_hT"), 1)
                    yield step["u_out"]
                    c, b = where
                    act.wait_ge(*at("u_u", t, s))
                    nc.scalar.copy(UT[:, bass.ds(c * P + P + 1, P), bass.ds(b * SIDES + s, 1)],
                                   psA[0:S3, 0:P].unsqueeze(2)).then_inc(sem("u_out"), 1)
                    return
                l = LAYERS[li + 1]
                evac_xT(l.name, t, s, psA, *{0: ("lng0", "lnb0"), 1: (), 2: ("qg2", "qb2"), 3: ("g31", "b31")}[li + 1])
                yield step["qT"]
                act.wait_ge(*at(f"{l.name}_q", t, s))
                for gi in range(l.groups):
                    ins = nc.scalar.activation(qT[s][:, gi, :], psB[:, gi * P:(gi + 1) * P], ACT.Identity,
                                               bias=bq3[:, gi:gi + 1] if l is L3 else 0.0, scale=l.scale)
                ins.then_inc(sem(f"{l.name}_qT"), 1)

            where = None

            def tanh_step(t, j):
                act.wait_ge(*at("r_z", t, n=j + 1))
                if j:
                    act.wait_ge(*at("r_r", t, n=j))
                nc.scalar.activation(th3[:, :], psR[0:S3, NB * j:NB * (j + 1)], ACT.Tanh,
                                     scale=0.5).then_inc(sem("r_th"), 1)

            def mamba_block(t, before=None):
                side_by_side(mamba(t, 0), mamba(t, 1), between(t, -1, 0), before)

            def tile(t, c, bp):
                nonlocal where
                where = (c, bp)
                act.wait_ge(*at("tile_done", t))
                chain, since = Chain(between(t, -1, 1)), 0
                tanh_step(t, 0)
                for u in range(LAST_SLOT):
                    if u in ENDS:
                        chain, since = Chain(between(t, *STAGES[ENDS[u]])), u
                    chain.go_on(2 * (u - since) + 1)
                    if u < NU:
                        act.wait_ge(*at("u_mx", t, n=u + 1))
                        if u >= 3:
                            act.wait_ge(*at("u_tp", t, n=u - 2))
                        nc.scalar.activation(Pr[:, u % 3, :], psS[u % 3][:, :], ACT.Exp, bias=nmax[:, u:u + 1],
                                             accum_out=den[:, u:u + 1]).then_inc(sem("u_exp"), 1)
                    j = step_of(u + 1)
                    if j is not None and u + 1 not in ENDS:
                        tanh_step(t, j)
                    for k in (k for k in turned_in(u) if k % 2 == 0):
                        act.wait_ge(*at("u_tp", t, n=k + 1))
                        if k >= 8:
                            act.wait_ge(*at("u_pv", t, n=k // 4 - 1))
                        if k:
                            act.wait_ge(*at("u_ev", t, n=k))
                        nc.scalar.copy(PT[:, k % 8, :, :].rearrange("p a n -> p (a n)"),
                                       psT[k % 2][:, :]).then_inc(sem("u_ev"), 1)
                    if u + 1 in ENDS:
                        chain.finish()
                        if j is not None and u + 1 in ENDS:
                            tanh_step(t, j)
                mamba_block(Ahead(t), chain)

            act.wait_ge(sem("ready"), 1)
            mamba_block(First(act))
            nc.scalar.copy(SS[S3:, :, :], w("eyeb")[S3:S3 + NB, :].unsqueeze(1).to_broadcast([NB, P + T, NB])
                           ).then_inc(sem("picks"), 1)
            tiles(act, tile)

            def last_steps(t, k):
                for j in range(STEPS):
                    act.wait_ge(*at("e_z", t, n=j + 1))
                    nc.scalar.activation(R2[:, j + 1, :], psR[0:S3, NB * j:NB * (j + 1)], ACT.Silu).then_inc(sem("e_r"), 1)
                    i = j // EARLY_GAP
                    if j % EARLY_GAP == 0 and i < EARLY:
                        if i >= 4:
                            act.wait_ge(*at("o_mm", t, n=i - 3))
                        nc.scalar.copy(SSb[i % 4], SS[:, (i // SIDES + 1) * P:(i // SIDES + 2) * P,
                                                      bass.ds(k * SIDES + i % SIDES, 1)].squeeze(2)).then_inc(sem("o_ss"), 1)

            act.wait_ge(sem("picks"), 1)
            act.wait_ge(sem("L0_qT"), len(STAGES) * NT // SIDES + 1)
            act.wait_ge(sem("e_done"), 1)
            turns(act, last_steps, (1, EARLY, STEPS), "last", PAIRS)

            act.wait_ge(sem("e_done"), PAIRS + 1)
            for b in range(NB):
                nc.scalar.copy(SSb[b], SS[:, T:, b]).then_inc(sem("f_ss"), 1)

        @block.vector
        def _(dve):
            nc.vector.memset(st[0][:, 11:12], 0.0).then_inc(sem("c_taken"), 1)
            for s in range(SIDES):
                nc.vector.memset(st[s][:, 12:13], 0.0).then_inc(sem(f"c_st{s}"), 1)
            dve.wait_ge(sem("par0"), 16)
            dve.wait_ge(sem("mask_in"), 32)
            nc.vector.tensor_scalar(keep, keep.bitcast(I32), -1.0, 1.0, ALU.mult, ALU.add)
            nc.vector.tensor_scalar(m_tmp[:, 0, :], m_row[:, :].bitcast(I32), -1e9, None, ALU.mult).then_inc(sem("mask_parts"), 1)
            dve.wait_ge(sem("mask_parts"), 1)
            nc.vector.tensor_copy(m_part[:, 0, :], m_tmp[:, 0, :]).then_inc(sem("mask_parts"), 1)
            dve.wait_ge(sem("mask_parts"), 2)
            nc.vector.tensor_tensor(m_tmp[:, 1, :], m_tmp[:, 0, :], m_part[:, 0, :], ALU.subtract).then_inc(sem("mask_parts"), 1)
            dve.wait_ge(sem("mask_parts"), 3)
            nc.vector.tensor_copy(m_part[:, 1, :], m_tmp[:, 1, :]).then_inc(sem("mask_parts"), 1)
            dve.wait_ge(sem("mask_parts"), 4)
            nc.vector.tensor_tensor(m_tmp[:, 2, :], m_tmp[:, 1, :], m_part[:, 1, :], ALU.subtract).then_inc(sem("mask_parts"), 1)
            dve.wait_ge(sem("mask_parts"), 5)
            nc.vector.tensor_copy(m_part[:, 2, :], m_tmp[:, 2, :]).then_inc(sem("mask_parts"), 1)
            dve.wait_ge(sem("mod_mm"), 1)
            nc.vector.tensor_tensor(cm[S3:, :], ps[0][S3:S3 + NB, 0:D], w("bprog3")[S3:S3 + NB, :], ALU.add).then_inc(sem("mod_done"), 1)
            nc.vector.memset(st[0][:, 10:11], 0.0).then_inc(sem("c_used"), 1)

            def norm_stats(name, t, s, src):
                nc.vector.bn_stats(st[s][:, 0:6], src).then_inc(sem(f"{name}_bn"), 1)
                dve.wait_ge(*at(f"{name}_bn", t, s, apart=True))
                nc.vector.bn_aggr(st[s][:, 6:8], st[s][:, 0:6]).then_inc(sem(f"{name}_ag"), 1)
                dve.wait_ge(*at(f"{name}_ag", t, s))
                nc.vector.tensor_scalar(st[s][:, 8:9], st[s][:, 7:8], EPS, None, ALU.add).then_inc(sem(f"{name}_ve"), 1)

            def norm_rows(name, t, s, src):
                dve.wait_ge(*at(f"{name}_rs", t, s))
                nc.vector.tensor_scalar(nrm[s][:, :], src, st[s][:, 6:7], st[s][:, 9:10], ALU.subtract,
                                        ALU.mult).then_inc(sem(f"{name}_nrm"), 1)

            def ctx_norms(t):
                dve.wait_ge(*at("cin", t, n=16))
                for s in range(SIDES):
                    norm_stats("c", t, s, xin[:, s, :])
                for s in range(SIDES):
                    norm_rows("c", t, s, xin[:, s, :])

            def ctx_keys(t, s, kp):
                X = bank[s]
                dve.wait_ge(*at("c_k01", t, s))
                dve.wait_ge(*at(f"c_st{s}", t, n=1))
                nc.vector.tensor_tensor(KS[s][:, 0:2, :], X[1][:, 0:256].rearrange("p (g n) -> p g n", g=2),
                                        keep[:, bass.ts(kp * SIDES + s, P)].unsqueeze(1).to_broadcast([P, 2, P]), ALU.mult)
                nc.vector.tensor_copy(KS[s][:, 2, :], X[1][:, 256:384])

            def ctx_values(t, s):
                X = bank[s]
                dve.wait_ge(*at("c_v23", t, s))
                nc.vector.tensor_copy(VS[s][:, 384:640], X[0][:, 0:256])
                dve.wait_ge(*at("c_act", t, s))
                nc.vector.tensor_tensor(VS[s][:, 640:896], X[0][:, 256:512], w("bv3"), ALU.add).then_inc(sem("c_dve"), 1)

            def ctx_pair(t, b, kp):
                dve.wait_ge(*at("c_used", t))
                dve.wait_ge(*at("c_tpn", t, 1))
                nc.vector.memset(st[0][:, 11:12], 0.0).then_inc(sem("c_taken"), 1)
                ctx_keys(t, 0, kp)
                ctx_norms(Ahead(t))
                ctx_values(t, 0)
                ctx_keys(t, 1, kp)
                ctx_values(t, 1)
                dve.wait_ge(*at("c_dve", t, 1))
                nc.vector.memset(st[0][:, 10:11], 0.0).then_inc(sem("c_used"), 1)

            ctx_norms(First(dve))
            context(dve, ctx_pair, (16, 32))
            dve.wait_ge(sem("c_used"), NT // SIDES + 1)
            nc.vector.memset(st[0][:, 10:11], 0.0).then_inc(sem("x_taken"), 1)
            nc.vector.memset(st[0][:, 11:12], 0.0).then_inc(sem("kv_used"), 4)
            for i in range(1, 3):
                dve.wait_ge(sem(f"par{i}"), 16)
            dve.wait_ge(sem("expA"), 1)
            nc.vector.tensor_scalar(negA[:, :], dts[:, 0, 0, :], -1.0, None, ALU.mult)
            nc.vector.tensor_scalar(at2[:, :], W[0:S3, PLAN["at3"][0]:PLAN["at3"][0] + P], 0.5, None, ALU.mult)
            nc.vector.tensor_scalar(bq3[:, :], w("bq3"), L3.scale, None, ALU.mult)
            nc.vector.tensor_copy(cm[0:S3, :], W[0:S3, PLAN["cmat3"][0]:PLAN["cmat3"][0] + D])
            nc.vector.tensor_scalar(hconv[:, :], w("convw"), 0.5, None, ALU.mult)
            nc.vector.tensor_scalar(hconvb[:, :], w("convb"), 0.5, None, ALU.mult).then_inc(sem("halved"), 1)
            dve.wait_ge(sem("halved"), 1)
            for g in range(PE_CONV):
                for k in range(CONV):
                    c = (XG - PE_CONV + g) * CONV + k
                    nc.vector.tensor_scalar(diag[:, g, k, :], ident, hconv[:, c:c + 1], None, ALU.mult)
            for s in range(SIDES):
                dve.wait_ge(sem(f"c_st{s}"), 32 * (NT // SIDES) + 1)
            nc.vector.memset(st[0][:, 12:13], 0.0).then_inc(sem("ready"), 1)

            def log_steps(t):
                d = lambda k: dts[:, k, :, :]
                dve.wait_ge(*at("m_e", t))
                nc.vector.tensor_scalar(d(4), d(3), 2.0, None, ALU.add).then_inc(sem("m_e2"), 1)
                yield
                dve.wait_ge(*at("m_e2", t))
                nc.vector.reciprocal(d(9), d(4)).then_inc(sem("m_rc"), 1)
                yield
                dve.wait_ge(*at("m_rc", t))
                nc.vector.tensor_tensor(d(5), d(3), d(9), ALU.mult).then_inc(sem("m_r"), 1)
                yield
                dve.wait_ge(*at("m_r", t))
                nc.vector.tensor_tensor(d(6), d(5), d(5), ALU.mult).then_inc(sem("m_log"), 1)
                yield
                dve.wait_ge(*at("m_log", t, n=1))
                nc.vector.tensor_scalar(d(7), d(6), 1.0 / 19, None, ALU.mult).then_inc(sem("m_log"), 1)
                yield
                for n, q in enumerate((17, 15, 13, 11, 9, 7, 5, 3)):
                    dve.wait_ge(*at("m_log", t, n=n + 2))
                    nc.vector.scalar_tensor_tensor(d(7), d(7), 1.0 / q, d(6), ALU.add, ALU.mult
                                                   ).then_inc(sem("m_log"), 1)
                    yield
                dve.wait_ge(*at("m_log", t, n=10))
                nc.vector.scalar_tensor_tensor(d(8), d(7), 1.0, d(5), ALU.add, ALU.mult).then_inc(sem("m_log"), 1)
                yield
                dve.wait_ge(*at("m_log", t, n=11))
                nc.vector.scalar_tensor_tensor(d(10), d(8), 2.0, d(1), ALU.mult, ALU.add).then_inc(sem("m_dt"), 1)
                yield
                dve.wait_ge(*at("m_dt", t))
                nc.vector.tensor_tensor(d(11), d(10), negA[:, :].unsqueeze(1).to_broadcast([P, SIDES, HM]),
                                        ALU.mult).then_inc(sem("m_dA"), 1)

            def mamba(t, s, b):
                r, X, late = rooms[s], bank[s], LATE * s
                hv = lambda a: a.rearrange("p (h n) -> p h n", h=HM)
                yield 0
                if s == 0:
                    dve.wait_ge(*at("x_in", t, n=16))
                nc.vector.tensor_tensor_reduce(out=r.y[:, 0:D], in0=xin[:, s, :], in1=xin[:, s, :], scale=1.0, scalar=0.0,
                                               op0=ALU.mult, op1=ALU.add, accum_out=r.st[:, 5:6]).then_inc(sem("m1_ss"), 1)
                dve.wait_ge(*at("m1_ss", t, s))
                nc.vector.tensor_scalar(r.st[:, 0:1], r.st[:, 5:6], 1.0 / D, EPS, ALU.mult, ALU.add).then_inc(sem("m1_ve"), 1)
                yield 1
                dve.wait_ge(*at("m1_rs", t, s))
                nc.vector.tensor_scalar(r.nrm, xin[:, s, :], r.st[:, 1:2], None, ALU.mult).then_inc(sem("m1_nrm"), 1)
                yield 5
                dve.wait_ge(*at("m_xbc", t, s))
                nc.vector.tensor_tensor(dts[:, 0, s, :], X[2][:, 256:256 + HM], w("dtb"), ALU.add).then_inc(sem("m_v0"), 1)
                if s == 1:
                    dve.wait_ge(*at("m_v0", t, s))
                    nc.vector.tensor_scalar(dts[:, 1, :, :], dts[:, 0, :, :], 0.0, None, ALU.max).then_inc(sem("m_v1"), 1)
                    dve.wait_ge(*at("m_v1", t))
                    nc.vector.scalar_tensor_tensor(dts[:, 2, :, :], dts[:, 1, :, :], -2.0, dts[:, 0, :, :], ALU.mult,
                                                   ALU.add).then_inc(sem("m_v"), 1)
                yield (7, 8 + late)[s]
                dve.wait_ge(*at("m_hist", t, s))
                log = iter(()) if s else log_steps(t)
                for k in range(1, CONV):
                    if k == 1:
                        dve.wait_ge(*at("m_conv0", t, s))
                    else:
                        dve.wait_ge(*at("m_conv", t, s, k - 1))
                    for g in range(XG - PE_CONV):
                        src = r.xpad[:, g, k:k + P]
                        wk = hconv[:, g * CONV + k:g * CONV + k + 1]
                        ins = nc.vector.scalar_tensor_tensor(r.acc[:, g, :], src, wk, r.acc[:, g, :], ALU.mult, ALU.add)
                        next(log, None)
                    ins.then_inc(sem("m_conv"), 1)
                for _ in log:
                    pass
                if s == 0:
                    yield 8
                    dve.wait_ge(*at("m_dA", t))
                    nc.vector.tensor_tensor(r.dAm, w("tri_le").unsqueeze(1).to_broadcast([P, HM, P]),
                                            wide(dts[:, 11, s, :], P), ALU.mult).then_inc(sem("m_dAm"), 1)
                yield 10 + late
                dve.wait_ge(*at("m_th", t, s))
                nc.vector.scalar_tensor_tensor(r.acc.rearrange("p g n -> p (g n)"),
                                               r.th.rearrange("p g n -> p (g n)"), 1.0,
                                               r.acc.rearrange("p g n -> p (g n)"), ALU.add,
                                               ALU.mult).then_inc(sem("m_xc"), 1)
                yield 12 + late
                dve.wait_ge(*at("m_Br", t, s))
                nc.vector.tensor_tensor(r.BG[:, 1, :], X[0][:, P:2 * P], w("tri_le"), ALU.mult).then_inc(sem("m_GT"), 1)
                dve.wait_ge(*at("m_xr", t, s))
                dve.wait_ge(*at("m_dt", t))
                nc.vector.tensor_tensor(hv(r.xdt), hv(r.xr), wide(dts[:, 10, s, :], HP), ALU.mult).then_inc(sem("m_xdt"), 1)
                yield 13 + late
                dve.wait_ge(*at("m_GT", t, s))
                dve.wait_ge(*at("m_dec", t, s))
                nc.vector.tensor_tensor(r.seg, r.seg, r.BG[:, 1, :].unsqueeze(1).to_broadcast([P, HM, P]),
                                        ALU.mult).then_inc(sem("m_M"), 1)
                yield 15 + late
                dve.wait_ge(*at("m_inter", t, s))
                dve.wait_ge(*at("m_z", t, s))
                nc.vector.tensor_tensor(hv(r.y), hv(X[1][:, :]), wide(r.dec[:, 0, :], HP), ALU.mult).then_inc(sem("m_y0"), 1)
                dve.wait_ge(*at("m_zt", t, s))
                nc.vector.scalar_tensor_tensor(r.zt, r.zt, 1.0, X[3][:, :], ALU.add,
                                               ALU.mult).then_inc(sem("m_zs"), 1)
                dve.wait_ge(*at("m_y0", t, s))
                dve.wait_ge(*at("m_xD", t, s))
                nc.vector.tensor_tensor(r.y, r.y, r.y2, ALU.add).then_inc(sem("m_y1"), 1)
                dve.wait_ge(*at("m_y1", t, s))
                dve.wait_ge(*at("m_intra", t, s))
                nc.vector.tensor_tensor(r.y, r.y, X[2][:, :], ALU.add).then_inc(sem("m_y2"), 1)
                dve.wait_ge(*at("m_y2", t, s))
                dve.wait_ge(*at("m_zs", t, s))
                nc.vector.tensor_tensor(r.y, r.y, r.zt, ALU.mult).then_inc(sem("m_y3"), 1)
                yield 17 + late
                dve.wait_ge(*at("m2_ss", t, s))
                nc.vector.tensor_scalar(r.st[:, 3:4], r.st[:, 6:7], 0.25 / DI, EPS, ALU.mult, ALU.add).then_inc(sem("m2_ve"), 1)
                yield 18 + late
                dve.wait_ge(*at("m2_rs", t, s))
                nc.vector.tensor_scalar(r.y, r.y, r.st[:, 4:5], 0.5, ALU.mult, ALU.mult).then_inc(sem("m_un"), 1)
                dve.wait_ge(*at("m_xw", t, s, apart=True))
                nc.vector.tensor_tensor(hv(r.xdt), Hst[:, bass.ds(b, 1), :].rearrange("p a (h n) -> p (a h) n", h=HM),
                                        wide(r.dec[:, 2, :], HP), ALU.mult).then_inc(sem("m_Hd"), 1)
                dve.wait_ge(*at("m_Hd", t, s, apart=True))
                dve.wait_ge(*at("m_state", t, s))
                nc.vector.tensor_tensor(Hst[:, bass.ds(b, 1), :], r.xdt.unsqueeze(1), X[3][:, :].unsqueeze(1),
                                        ALU.add).then_inc(sem("m_H"), 1)
                yield 22 + late
                dve.wait_ge(*at("m_out", t, s))
                nc.vector.tensor_tensor(xrow[s][:, :], xin[:, s, :], X[0][:, 0:D], ALU.add).then_inc(sem("x1"), 1)

            def add_rows(name, t, s, src, out_name):
                dve.wait_ge(*at(name, t, s))
                nc.vector.tensor_tensor(xrow[s][:, :], xrow[s][:, :], src, ALU.add).then_inc(sem(out_name), 1)
                dve.wait_ge(*at(out_name, t, s))

            def between(t, li, s):
                step = steps_after(li)
                if li >= 0:
                    l = LAYERS[li]
                    u0 = NU_BEFORE[li, s]
                    yield step["rd"]
                    dve.wait_ge(*at("u_exp", t, n=u0 + l.heads))
                    nc.vector.reciprocal(rden[:, u0:u0 + l.heads], den[:, u0:u0 + l.heads]).then_inc(sem(f"{l.name}_rd"), 1)
                    dve.wait_ge(*at(f"{l.name}_rd", t, s))
                    nc.vector.tensor_copy(rdw[:, 0:l.heads * 32].rearrange("p (h n) -> p h n", h=l.heads),
                                          wide(rden[:, u0:u0 + l.heads], 32)).then_inc(sem(f"{l.name}_rdw"), 1)
                    yield step["on"]
                    dve.wait_ge(*at("u_pv", t, n=(u0 + l.heads) // 4))
                    dve.wait_ge(*at(f"{l.name}_rdb", t, s))
                    nc.vector.tensor_tensor(oT[:, 0:l.quads, :].rearrange("p a n -> p (a n)"), psO[:, 0:l.quads * P],
                                            rdb[:, 0:l.quads * P], ALU.mult).then_inc(sem(f"{l.name}_on"), 1)
                    yield step["add"]
                if li == -1:
                    yield step["stats"]
                    dve.wait_ge(*at("x1", t, s))
                if li == 0:
                    add_rows("L0_op", t, s, psB[:, 0:D], "x2")
                if li == 1:
                    add_rows("L1_op", t, s, psB[:, 0:D], "x3")
                    yield step["stats"]
                    add_rows("f_o", t, s, psA[:, 0:D], "x4")
                    nc.vector.tensor_tensor(xrow[s][:, :], xrow[s][:, :], w("b2"), ALU.add).then_inc(sem("x5"), 1)
                    dve.wait_ge(*at("x5", t, s))
                if li == 2:
                    dve.wait_ge(*at("L2_op", t, s))
                    nc.vector.tensor_tensor(orows[:, :], psB[:, 0:D], w("bo2"), ALU.add).then_inc(sem("L2_pre"), 1)
                    yield step["stats"]
                    add_rows("L2_gelu", t, s, nrm[s][:, :], "x6")
                if li == 3:
                    add_rows("L3_op", t, s, psB[:, 0:D], "x7")
                    nc.vector.tensor_tensor(xrow[s][:, :], xrow[s][:, :], w("bo3"), ALU.add).then_inc(sem("x8"), 1)
                    dve.wait_ge(*at("x8", t, s))
                if li != 0:
                    name = {-1: "L0_n", 1: "L2_n", 2: "L3_n", 3: "u"}[li]
                    norm_stats(name, t, s, xrow[s][:, :])
                    yield step["nrm"]
                    norm_rows(name, t, s, xrow[s][:, :])
                if li == 3:
                    c, bp = where
                    nc.vector.tensor_copy(RES[:, bass.ds(c * NB + bp * SIDES + s, 1), :], xrow[s][:, :].unsqueeze(1)
                                          ).then_inc(sem("res_kept"), 1)

            where = None

            def silu_step(t, j):
                dve.wait_ge(*at("r_th", t, n=j + 1))
                nc.vector.scalar_tensor_tensor(R2[:, j + 1, :], th3[:, :], 1.0, psR[0:S3, NB * j:NB * (j + 1)],
                                               ALU.add, ALU.mult).then_inc(sem("r_r"), 1)

            def mamba_block(t, b, before=None):
                side_by_side(mamba(t, 0, b), mamba(t, 1, b + 1), between(t, -1, 0), before)
                dve.wait_ge(*at("x1", t, 1))
                nc.vector.memset(st[0][:, 13:14], 0.0).then_inc(sem("x_taken"), 1)
                dve.wait_ge(*at("m_H", t, 1))
                dve.wait_ge(*at("m_hist2", t, 1))

            def tile(t, c, bp):
                nonlocal where
                where = (c, bp)
                dve.wait_ge(*at("tile_done", t))
                chain, since = Chain(between(t, -1, 1)), 0
                silu_step(t, 0)
                for u in range(LAST_SLOT):
                    if u in ENDS:
                        chain, since = Chain(between(t, *STAGES[ENDS[u]])), u
                    chain.go_on(2 * (u - since) + 1)
                    if u < NU:
                        dve.wait_ge(*at("u_s", t, n=u + 1))
                        nc.vector.tensor_reduce(nmax[:, u:u + 1], psS[u % 3][:, :], AX, ALU.max,
                                                negate=True).then_inc(sem("u_mx"), 1)
                    for k in (k for k in turned_in(u) if k % 2 == 1):
                        dve.wait_ge(*at("u_tp", t, n=k + 1))
                        if k >= 8:
                            dve.wait_ge(*at("u_pv", t, n=k // 4 - 1))
                        dve.wait_ge(*at("u_ev", t, n=k))
                        nc.vector.tensor_copy(PT[:, k % 8, :, :].rearrange("p a n -> p (a n)"),
                                              psT[k % 2][:, :]).then_inc(sem("u_ev"), 1)
                    j = step_of(u + 1)
                    if j is not None and u + 1 not in ENDS:
                        silu_step(t, j)
                    if u + 1 in ENDS:
                        chain.finish()
                        if j is not None and u + 1 in ENDS:
                            silu_step(t, j)
                dve.wait_ge(*at("r_r", t, n=STEPS))
                g = (c * PAIRS + bp) * STEPS
                nc.vector.scalar_tensor_tensor(SS[0:S3, bass.ds(g, STEPS), :], R2[:, 1:, :], 0.5,
                                               UT[:, bass.ds(g + 1, STEPS), :], ALU.mult, ALU.add).then_inc(sem("r_ss"), 1)
                nc.vector.tensor_copy(R2[:, 0, :], R2[:, STEPS, :]).then_inc(sem("r_last"), 1)
                mamba_block(Ahead(t), SIDES - bp * SIDES, chain)
                dve.wait_ge(*at("u_out", t, 1))
                dve.wait_ge(*at("res_kept", t, 1))
                dve.wait_ge(*at("r_ss", t))
                dve.wait_ge(*at("r_last", t))
                nc.vector.memset(st[0][:, 14:15], 0.0).then_inc(sem("tile_done"), 1)

            mamba_block(First(dve), 0)
            nc.vector.memset(st[0][:, 12:13], 0.0).then_inc(sem("tile_done"), 1)
            tiles(dve, tile, PERS + (16,))
            dve.wait_ge(sem("tile_done"), NT // SIDES + 1)
            nc.vector.tensor_scalar(R2[:, 0, :], R2[:, 0, :], 0.5, None, ALU.mult).then_inc(sem("e_half"), 1)
            dve.wait_ge(sem("e_half"), 1)
            nc.vector.memset(st[0][:, 13:14], 0.0).then_inc(sem("e_done"), 1)

            def last_steps(t, k):
                for i in range(EARLY):
                    dve.wait_ge(*at("o_mm", t, n=i + 1))
                    row = RES[:, bass.ds(i // SIDES * NB + k * SIDES + i % SIDES, 1), :]
                    nc.vector.tensor_tensor(row, row, ps[i % 4][:, 0:D].unsqueeze(1), ALU.add).then_inc(sem("o_row"), 1)
                dve.wait_ge(*at("o_row", t, n=EARLY))
                dve.wait_ge(*at("e_r", t, n=STEPS))
                g = k * STEPS + T
                nc.vector.tensor_tensor(SS[0:S3, bass.ds(g, STEPS), :], R2[:, 1:, :], UT[:, bass.ds(g + 1, STEPS), :],
                                        ALU.add).then_inc(sem("e_ss"), 1)
                nc.vector.tensor_copy(R2[:, 0, :], R2[:, STEPS, :]).then_inc(sem("e_last"), 1)
                dve.wait_ge(*at("e_ss", t))
                dve.wait_ge(*at("e_last", t))
                nc.vector.memset(st[0][:, 13:14], 0.0).then_inc(sem("e_done"), 1)

            turns(dve, last_steps, (1, EARLY, STEPS), "last", PAIRS)
            for b in range(NB):
                dve.wait_ge(sem("f_mm"), b + 1)
                row = RES[:, (NCH - 1) * NB + b, :]
                nc.vector.tensor_tensor(row, row, ps[b][:, 0:D], ALU.add).then_inc(sem("f_row"), 1)

        @block.tensor
        def _(pe):
            mm = nc.tensor.matmul
            pe.wait_ge(sem("par0"), 16)
            pe.wait_ge(sem("probs_in"), 16)
            for b in range(NB):
                for k in range(NCH):
                    ins = mm(ps[1][0:S3, b:b + 1], pb[:, b, k, :], w("inv512"), start=k == 0, stop=k == NCH - 1)
            ins.then_inc(sem("mod_pm"), 1)
            pe.wait_ge(sem("mod_pmT"), 1)
            a = PLAN["wprog3"][0]
            mm(ps[0][S3:S3 + NB, 0:D], pmT[:, :], W[0:S3, a:a + D], start=True, stop=True).then_inc(sem("mod_mm"), 1)

            def turn(dst, src, n):
                for k in range(n):
                    ins = nc.tensor.transpose(dst[:, k * P:(k + 1) * P], src[:, k * P:(k + 1) * P], ident)
                return ins

            def proj_T(dst, wname, src, n):
                for g in range(n):
                    for kk in range(KD):
                        ins = mm(dst[:, g * P:(g + 1) * P], w(wname, KD)[:, kk, g * P:(g + 1) * P], src[:, kk, :],
                                 start=kk == 0, stop=kk == KD - 1)
                return ins

            def proj(dst, wname, src, n, parts=KD, at_col=0):
                for kk in range(parts):
                    ins = mm(dst, src[:, kk, :], w(wname, parts)[:, kk, at_col:at_col + n], start=kk == 0, stop=kk == parts - 1)
                return ins

            def ctx_tile(t, s):
                X = bank[s]
                yield 0
                turn(X[0], xin[:, s, :], KD).then_inc(sem("c_tpx"), 1)
                yield 1
                pe.wait_ge(*at("c_nrm", t, s))
                turn(X[0][:, D:2 * D], nrm[s], KD).then_inc(sem("c_tpn"), 1)
                yield 3
                pe.wait_ge(*at("c_ev", t, s))
                proj_T(X[1][:, 0:256], "wk0", cT[s][0], 2)
                proj_T(X[1][:, 256:384], "wk1", cT[s][0], 1).then_inc(sem("c_k01"), 1)
                proj_T(X[2][:, 0:256], "wk2", cT[s][1], 2)
                proj_T(X[2][:, 256:512], "wk3", cT[s][2], 2).then_inc(sem("c_k23"), 1)
                proj(X[3][:, 0:256], "wv0", cT[s][0], 256)
                proj(X[3][:, 256:384], "wv1", cT[s][0], 128).then_inc(sem("c_v01"), 1)
                proj(X[0][:, 0:256], "wv2", cT[s][1], 256)
                proj(X[0][:, 256:512], "wv3", cT[s][2], 256).then_inc(sem("c_v23"), 1)

            def ctx_pair(t, b, kp):
                pe.wait_ge(*at("c_used", t))
                pe.wait_ge(*at("cin", t, n=16))
                side_by_side(ctx_tile(t, 0), ctx_tile(t, 1))

            pe.wait_ge(sem("mod_done"), 1)
            context(pe, ctx_pair, (16,))
            for i in range(1, 3):
                pe.wait_ge(sem(f"par{i}"), 16)
            pe.wait_ge(sem("zeroed"), 1)
            pe.wait_ge(sem("mask_rows"), 48)

            def mamba(t, s, b):
                r, X, late = rooms[s], bank[s], LATE * s
                yield 2
                pe.wait_ge(*at("m1_nrm", t, s))
                turn(X[0], r.nrm, KD).then_inc(sem("m1_xtp"), 1)
                yield 4
                pe.wait_ge(*at("m1_xT", t, s))
                inw = w("inw", KD)
                for g in range(XG):
                    dst = X[1][:, g * P:(g + 1) * P] if g < 4 else X[2][:, (g - 4) * P:(g - 3) * P]
                    for kk in range(KD):
                        ins = mm(dst, inw[:, kk, DI + g * P:DI + (g + 1) * P], r.xT[:, kk, :], start=kk == 0,
                                 stop=kk == KD - 1)
                    if g == 3:
                        ins.then_inc(sem("m_pa"), 1)
                proj(X[2][:, 256:256 + HM], "inw", r.xT, HM, at_col=DI + XBC).then_inc(sem("m_pb"), 1)
                yield 6
                pe.wait_ge(*at("m_hist", t, s))
                pe.wait_ge(*at("m_xbc", t, s))
                for g in range(PE_CONV):
                    for k in range(CONV):
                        ins = mm(X[1][:, g * P:(g + 1) * P], diag[:, g, k, :], r.xpad[:, XG - PE_CONV + g, k:k + P],
                                 start=k == 0, stop=k == CONV - 1)
                ins.then_inc(sem("m_cv"), 1)
                yield 9 + late
                pe.wait_ge(*at("m_dAm", t, s))
                pe.wait_ge(*at("m_cev", t, s))
                pe.wait_ge(*at("m_v0", t, s))
                for i in range(2):
                    mm(X[1 + i][:, :], w("tri_gt"), r.dAm[:, 4 * i:4 * i + 4, :].rearrange("p h n -> p (h n)"),
                       start=True, stop=True)
                for q, name in enumerate(("tri_le", "tri_gt", "ones")):
                    ins = mm(X[0][:, 256 + q * HM:256 + (q + 1) * HM], w(name), dts[:, 11, s, :], start=True, stop=True)
                ins.then_inc(sem("m_seg"), 1)
                yield 11 + late
                pe.wait_ge(*at("m_xc", t, s))
                pe.wait_ge(*at("m_dec", t, s))
                for g in range(4):
                    nc.tensor.transpose(X[3][:, g * P:(g + 1) * P], r.acc[:, g, :], ident)
                nc.tensor.transpose(X[0][:, 0:P], r.acc[:, 4, :], ident)
                mm(X[0][:, P:2 * P], r.acc[:, 4, :], r.acc[:, 5, :], start=True, stop=True).then_inc(sem("m_rows"), 1)
                yield 13 + late
                pe.wait_ge(*at("m_dec", t, s))
                mm(X[1][:, :], r.acc[:, 5, :], Hst[:, bass.ds(b, 1), :].rearrange("p a n -> p (a n)"), start=True,
                   stop=True).then_inc(sem("m_inter"), 1)
                pe.wait_ge(*at("m_xr", t, s))
                proj(X[3][:, :], "inw", r.xT, DI).then_inc(sem("m_z"), 1)
                yield 14 + late
                pe.wait_ge(*at("m_M", t, s))
                pe.wait_ge(*at("m_xdt", t, s))
                for h in range(HM):
                    ins = mm(X[2][:, h * HP:(h + 1) * HP], r.seg[:, h, :], r.xdt[:, h * HP:(h + 1) * HP], start=True,
                             stop=True)
                ins.then_inc(sem("m_intra"), 1)
                yield 16 + late
                pe.wait_ge(*at("m_Br", t, s))
                pe.wait_ge(*at("m_xw", t, s))
                pe.wait_ge(*at("m_zs", t, s))
                mm(X[3][:, :], r.BG[:, 0, :], r.xw, start=True, stop=True).then_inc(sem("m_state"), 1)
                yield 19 + late
                pe.wait_ge(*at("m_un", t, s))
                turn(X[1], r.y, 4).then_inc(sem("m_utp"), 1)
                yield 21 + late
                pe.wait_ge(*at("m_uT", t, s))
                proj(X[0][:, 0:D], "outw", r.uT, D, 4).then_inc(sem("m_out"), 1)

            def between(t, li, s):
                step = steps_after(li)
                if li >= 0:
                    l = LAYERS[li]
                    yield step["rdT"]
                    pe.wait_ge(*at(f"{l.name}_rdw", t, s))
                    if (li, s) == (3, 1):
                        pe.wait_ge(*at("u_out", t, 0))
                    elif s:
                        pe.wait_ge(*at(f"{LAYERS[li + 1].name}_qT", t, 0))
                    else:
                        pe.wait_ge(*at(f"{l.name}_qT", t, 1))
                    turn(psAB, rdw, l.quads).then_inc(sem(f"{l.name}_rdT"), 1)
                    yield step["wo"]
                    pe.wait_ge(*at(f"{l.name}_on", t, s))
                    parts = 2 if l.dh == 32 else l.quads
                    proj(psB[:, 0:D], f"wo{li}", oT, D, parts).then_inc(sem(f"{l.name}_op"), 1)
                if li == 1:
                    yield step["f_tp"]
                    pe.wait_ge(*at("x3", t, s))
                    turn(psA, xrow[s], KD).then_inc(sem("f_xtp"), 1)
                    yield step["f_h"]
                    pe.wait_ge(*at("f_xT", t, s))
                    proj_T(psB, "w1", xT[s], KD).then_inc(sem("f_h"), 1)
                    yield step["f_o"]
                    pe.wait_ge(*at("f_hT", t, s))
                    proj(psA[:, 0:D], "w2", hT, D).then_inc(sem("f_o"), 1)
                yield step["tp"]
                if li == 0:
                    pe.wait_ge(*at("x2", t, s))
                    turn(psA, xrow[s], KD).then_inc(sem("L1_xtp"), 1)
                else:
                    name, nxt = {-1: ("L0_n", "L0"), 1: ("L2_n", "L2"), 2: ("L3_n", "L3"), 3: ("u", "u")}[li]
                    pe.wait_ge(*at(f"{name}_nrm", t, s))
                    turn(psA, nrm[s], KD).then_inc(sem(f"{nxt}_xtp"), 1)
                yield step["q"]
                if li == 3:
                    pe.wait_ge(*at("u_xT", t, s))
                    proj_T(psB, "win3", xT[s], KD).then_inc(sem("u_h"), 1)
                    yield step["u_u"]
                    pe.wait_ge(*at("u_hT", t, s))
                    for kk in range(KD):
                        ins = mm(psA[0:S3, 0:P], w("bmat3", KD)[:, kk, :], hT[:, kk, :], start=kk == 0, stop=kk == KD - 1)
                    ins.then_inc(sem("u_u"), 1)
                    return
                l = LAYERS[li + 1]
                pe.wait_ge(*at(f"{l.name}_xT", t, s))
                proj_T(psB, f"wq{li + 1}", xT[s], l.groups).then_inc(sem(f"{l.name}_q"), 1)

            def preload(g):
                a3 = PLAN["at3"][0]
                mm(psR[:, 0:STEPS * NB], W[0:S3, a3:a3 + P], UT[:, bass.ds(g, STEPS), :].rearrange("p t b -> p (t b)"),
                   start=True, stop=True, skip_group_check=True)

            def state_step(t, j, pre, weights):
                if j:
                    pe.wait_ge(*at(f"{pre}_r", t, n=j))
                mm(psR[:, NB * j:NB * (j + 1)], weights, R2[:, j, :], start=False, stop=True,
                   skip_group_check=True).then_inc(sem(f"{pre}_z"), 1)

            def mamba_block(t, b, before=None):
                side_by_side(mamba(t, 0, b), mamba(t, 1, b + 1), between(t, -1, 0), before)

            def tile(t, c, bp):
                pe.wait_ge(*at("tile_done", t))
                pe.wait_ge(*at("x1", t, 1))
                preload((c * PAIRS + bp) * STEPS)
                chain, since = Chain(between(t, -1, 1)), 0
                for u in range(LAST_SLOT):
                    if u in ENDS:
                        chain, since = Chain(between(t, *STAGES[ENDS[u]])), u
                    j = step_of(u)
                    if j is not None:
                        state_step(t, j, "r", at2[:, :])
                    chain.go_on(2 * (u - since) + 1)
                    if u < NU:
                        i, l, s, h = UNITS[u]
                        if h == 0:
                            pe.wait_ge(*at(f"kv_in{i % 4}", t, n=32 * (i // 4 + 1)))
                        pe.wait_ge(*at("u_qm", t, n=u + 1))
                        if u >= 3:
                            pe.wait_ge(*at("u_exp", t, n=u - 2))
                        ins = mm(psS[u % 3][:, :], qm[:, u % 4, :], Ks[i % 4][:, h // l.per_group, :],
                                 start=True, stop=l is not L0)
                        if l is L0:
                            ins = mm(psS[u % 3][:, :], ones_b[:, :], m_rows[:, :], start=False, stop=True)
                        ins.then_inc(sem("u_s"), 1)
                    for k in turned_in(u):
                        pe.wait_ge(*at("u_exp", t, n=k + 1))
                        if k >= 2:
                            pe.wait_ge(*at("u_ev", t, n=k - 1))
                        turn(psT[k % 2], Pr[:, k % 3, :], NCH).then_inc(sem("u_tp"), 1)
                    for k, kts in value_products(u):
                        i, l, s, h = UNITS[k]
                        q = h // 4
                        if q == 0 and i and kts[0] == 0:
                            prev, prev_s = STAGES[i - 1]
                            pe.wait_ge(*at(f"{LAYERS[prev].name}_on", t, prev_s))
                        if kts[0] == 0:
                            pe.wait_ge(*at("u_ev", t, n=k + 1))
                        for kt in kts:
                            for g in range(4):
                                first = (4 * q + g) * l.dh
                                ins = mm(psO[32 * g:32 * g + 32, q * P:(q + 1) * P],
                                         Vs[i % 4][:, kt, first:first + 32], PT[:, (k - 3 + g) % 8, kt, :],
                                         start=kt == 0, stop=kt == NCH - 1)
                        if kts[-1] == NCH - 1:
                            ins.then_inc(sem("u_pv"), 1)
                            if h + 1 == l.heads:
                                pe.wait_ge(*at("u_pv", t, n=k // 4 + 1))
                                pe.sem_inc(sem("kv_used"), 1)
                    if u + 1 in ENDS:
                        chain.finish()
                pe.wait_ge(*at("r_r", t, n=STEPS))
                mamba_block(Ahead(t), SIDES - bp * SIDES, chain)

            pe.wait_ge(sem("ready"), 1)
            mamba_block(First(pe), 0)
            tiles(pe, tile, PERS)

            def last_steps(t, k):
                pe.wait_ge(*at("e_done", t))
                preload(k * STEPS + T)
                for j in range(STEPS):
                    state_step(t, j, "e", W[0:S3, PLAN["at3"][0]:PLAN["at3"][0] + P])
                    i = j // EARLY_GAP
                    if j % EARLY_GAP == 2 and i < EARLY:
                        pe.wait_ge(*at("o_ss", t, n=i + 1))
                        if i >= 4:
                            pe.wait_ge(*at("o_row", t, n=i - 3))
                        mm(ps[i % 4][:, 0:D], SSb[i % 4], cm[:, :], start=True, stop=True).then_inc(sem("o_mm"), 1)

            turns(pe, last_steps, (1, EARLY, STEPS), "last", PAIRS)

            for b in range(NB):
                pe.wait_ge(sem("f_ss"), b + 1)
                mm(ps[b][:, 0:D], SSb[b], cm[:, :], start=True, stop=True).then_inc(sem("f_mm"), 1)


def kernel(**inputs):
    import concourse.bacc as bacc
    from concourse.bass_utils import run_bass_kernel_spmd

    def a(name):
        return np.asarray(inputs[name])

    def parts(m):
        k = m.shape[0] // P
        return m.reshape(k, P, -1).transpose(1, 0, 2).reshape(P, -1)

    def chan(v):
        return v.reshape(-1, P).T

    def rows(v):
        return np.broadcast_to(v.reshape(1, -1), (P, v.size))

    def half(m):
        out = np.zeros((P, m.shape[1]), np.float32)
        out[:m.shape[0]] = m
        return out

    def spaced(m):
        out = np.zeros((m.shape[0] // 16, 32, m.shape[1]), np.float32)
        out[:, :16] = m.reshape(-1, 16, m.shape[1])
        return out.reshape(-1, m.shape[1])

    i = np.arange(P)
    wqkv, bqkv = a("L3_xattn_W_qkv"), a("L3_xattn_b_qkv")
    vals = {
        "ident": np.eye(P, dtype=np.float32),
        "wk0": parts(a("L0_xattn_Wk")), "wv0": parts(a("L0_xattn_Wv")),
        "wk1": parts(a("L1_xattn_W_k")), "wv1": parts(a("L1_xattn_W_v")),
        "wk2": parts(a("L2_xattn_Wk")), "wv2": parts(a("L2_xattn_Wv")),
        "wk3": parts(wqkv[D:2 * D].T), "wv3": parts(wqkv[2 * D:].T),
        "kvg2": chan(a("L2_xattn_kv_norm_g")), "kvb2": chan(a("L2_xattn_kv_norm_b")),
        "g31": chan(a("L3_xattn_g1")), "b31": chan(a("L3_xattn_beta1")),
        "bk3": chan(bqkv[D:2 * D]), "bv3": rows(bqkv[2 * D:]),
        "tri_le": (i[:, None] <= i[None, :]).astype(np.float32),
        "tri_gt": (i[:, None] > i[None, :]).astype(np.float32),
        "ones": np.ones((P, P), np.float32),
        "inw": parts(a("L0_xattn_in_proj_w")), "mnorm": chan(a("L0_xattn_m_norm_w")),
        "gnorm": chan(a("L0_xattn_gnorm_w")),
        "convw": parts(a("L0_xattn_conv_w")), "convb": chan(a("L0_xattn_conv_b")),
        "dtb": rows(a("L0_xattn_dt_bias")), "alog": rows(a("L0_xattn_A_log")), "dskip": rows(a("L0_xattn_D_skip")),
        "outw": parts(a("L0_xattn_out_proj_w")),
        "wq0": parts(a("L0_xattn_Wq")), "wo0": parts(a("L0_xattn_Wo")),
        "lng0": chan(a("L0_xattn_ca_ln_w")), "lnb0": chan(a("L0_xattn_ca_ln_b")),
        "wq1": parts(a("L1_xattn_W_q")), "wo1": parts(spaced(a("L1_xattn_W_o"))),
        "w1": parts(a("L1_xattn_w1").T), "w2": parts(a("L1_xattn_w2").T),
        "b1": chan(a("L1_xattn_b1")), "b2": rows(a("L1_xattn_b2")),
        "wq2": parts(a("L2_xattn_Wq")), "wo2": parts(spaced(a("L2_xattn_Wo"))),
        "qg2": chan(a("L2_xattn_q_norm_g")), "qb2": chan(a("L2_xattn_q_norm_b")), "bo2": rows(a("L2_xattn_bo")),
        "wq3": parts(wqkv[:D].T), "wo3": parts(a("L3_xattn_W_o").T), "bq3": chan(bqkv[:D]),
        "bo3": rows(a("L3_xattn_b_o")),
        "win3": parts(a("L3_xattn_W_in").T), "bin3": chan(a("L3_xattn_b_in")), "bmat3": parts(a("L3_xattn_Bmat")),
        "g32": chan(a("L3_xattn_g2")), "b32": chan(a("L3_xattn_beta2")),
        "at3": half(a("L3_xattn_A").T), "cmat3": half(a("L3_xattn_Cmat")), "wprog3": half(a("L3_xattn_W_prog").T),
        "bprog3": rows(a("L3_xattn_b_prog")),
        "hm32": (i[:, None] // 32 == np.arange(4)[None, :]).astype(np.float32),
        "hm16": (i[:, None] // 16 == np.arange(8)[None, :]).astype(np.float32),
        "neghalf": np.full((P, 1), -0.5, np.float32),
        "inv512": np.full((P, 1), 1.0 / T, np.float32),
        "eyeb": (i[:, None] == S3 + np.arange(NB)[None, :]).astype(np.float32),
    }
    pack = np.zeros((P, NPACK), np.float32)
    for name, (first, n) in PLAN.items():
        pack[:, first:first + n] = vals[name]

    mask = np.zeros((T, 4), np.uint8)
    mask[:, 0] = a("mask_1xS2_bf0").reshape(-1).view(np.uint8)

    nc = bacc.Bacc("TRN2", target_bir_lowering=False, num_devices=1)
    arrays, aps = {}, []
    for name, arr in (("x", a("x")), ("ctx", a("ctx_1024")), ("probs", a("ctxb_2048x64")),
                      ("mask", mask.view(np.int32).reshape(-1)), ("pack", pack)):
        arr = np.ascontiguousarray(arr)
        arrays[f"in_{name}"] = arr
        aps.append(nc.dram_tensor(f"in_{name}", arr.shape, mybir.dt.from_np(arr.dtype), kind="ExternalInput").ap())
    kd = nc.dram_tensor("keys", (NB, P, KG, T), F32, kind="Internal").ap()
    vd = nc.dram_tensor("values", (NB, P, NCH, VW), F32, kind="Internal").ap()
    out = nc.dram_tensor("out_0", (NB, T, D), F32, kind="ExternalOutput").ap()
    build(nc, *aps, kd, vd, out)
    r = run_bass_kernel_spmd(nc, [arrays], core_ids=[0])
    return r.results[0]["out_0"]
```
